# Optimizing a Trainium2 kernel written in Bass

```python
import numpy as np
import jax
import jax.numpy as jnp

def _softmax(x, axis=-1):
    return jax.nn.softmax(x, axis=axis)

def _gelu(x):
    return jax.nn.gelu(x, approximate=True)

def _silu(x):
    return jax.nn.silu(x)

def _sigmoid(x):
    return jax.nn.sigmoid(x)

def _layernorm(x, axis=-1, eps=1e-05):
    m = jnp.mean(x, axis=axis, keepdims=True)
    v = jnp.var(x, axis=axis, keepdims=True)
    return (x - m) / jnp.sqrt(v + eps)

def _scatter_add(tgt, idx, src, axis=0):
    return tgt.at[idx].add(src)

def _segment_sum(src, seg, n):
    return jax.ops.segment_sum(src, seg, n)
kernel_name = 'mk_gnn_ffn_d2_gnn_r64_e08322'

def setup_inputs(seed: int=0):
    np.random.seed(seed)
    _w = jnp.asarray

    def _rec_inputs():
        import jax
        import jax.numpy as jnp
        _gk = jax.random.key(seed)
        x = -0.0005963 + 1.001 * jax.random.normal(jax.random.fold_in(_gk, 1), (64, 768), jnp.float32)
        src = jax.random.randint(jax.random.fold_in(_gk, 2), (2048,), 0, 64, jnp.int32)
        dst = jax.random.randint(jax.random.fold_in(_gk, 3), (2048,), 0, 64, jnp.int32)
        _o = jnp.argsort(dst, stable=True)
        src = src[_o]
        dst = dst[_o]
        edge_attr_256 = 0.000121155 + 1.00018 * jax.random.normal(jax.random.fold_in(_gk, 11), (2048, 256), jnp.float32)
        edge_attr_32 = 0.000376506 + 0.999991 * jax.random.normal(jax.random.fold_in(_gk, 12), (2048, 32), jnp.float32)
        node_type_6 = jax.random.randint(jax.random.fold_in(_gk, 14), (64,), 0, 6, jnp.int32)
        return (x, src, dst, edge_attr_256, edge_attr_32, node_type_6)
    x, src, dst, edge_attr_256, edge_attr_32, node_type_6 = _rec_inputs()

    def _L0_gnn_setup():
        import jax, jax.numpy as jnp
        import numpy as np
        N_NODES = 64
        N_EDGES = 2048
        D = 768
        DE = 256
        L = 3
        H = 8
        DH = D // H
        EPS = 1e-05

        def _layernorm(x, g, b):
            mu = jnp.mean(x, axis=-1, keepdims=True)
            var = jnp.var(x, axis=-1, keepdims=True)
            return (x - mu) * jax.lax.rsqrt(var + EPS) * g + b
        key = jax.random.key(seed)
        ks = jax.random.split(key, 20)
        s = 0.02
        inp = {'node_features': jax.random.normal(ks[0], (N_NODES, D), jnp.float32), 'edge_index': jax.random.randint(ks[1], (2, N_EDGES), 0, N_NODES, jnp.int64 if jax.config.x64_enabled else jnp.int32), 'edge_features': jax.random.normal(ks[2], (N_EDGES, DE), jnp.float32), 'Wn': jax.random.normal(ks[3], (D, D), jnp.float32) * s, 'bn': jnp.zeros((D,), jnp.float32), 'We': jax.random.normal(ks[4], (D, DE), jnp.float32) * s, 'be': jnp.zeros((D,), jnp.float32), 'W1': jax.random.normal(ks[5], (L, D, 2 * D), jnp.float32) * s, 'b1': jnp.zeros((L, D), jnp.float32), 'ln_g': jnp.ones((L, D), jnp.float32), 'ln_b': jnp.zeros((L, D), jnp.float32), 'W2': jax.random.normal(ks[6], (L, D, D), jnp.float32) * s, 'b2': jnp.zeros((L, D), jnp.float32), 'Wqkv': jax.random.normal(ks[7], (3 * D, D), jnp.float32) * s, 'bqkv': jnp.zeros((3 * D,), jnp.float32), 'Wo': jax.random.normal(ks[8], (D, D), jnp.float32) * s, 'bo': jnp.zeros((D,), jnp.float32)}
        return inp
    _L0_gnn_all = _L0_gnn_setup()
    _L0_gnn_in = {k: v for k, v in _L0_gnn_all.items() if k in ('Wn', 'bn', 'We', 'be', 'W1', 'b1', 'ln_g', 'ln_b', 'W2', 'b2', 'Wqkv', 'bqkv', 'Wo', 'bo')}
    del _L0_gnn_all

    def _L0_ffn_setup():
        import jax, jax.numpy as jnp
        import numpy as np
        EPS_NORM = 1e-05
        RMS_EPS = 1e-05

        def _l2_normalize(v):
            n = jnp.sqrt(jnp.sum(v * v, axis=-1, keepdims=True))
            return v / jnp.maximum(n, EPS_NORM)

        def _rms_norm(x, weight, eps):
            ms = jnp.mean(x * x, axis=-1, keepdims=True)
            return x * jax.lax.rsqrt(ms + eps) * weight
        key = jax.random.key(seed)
        ks = jax.random.split(key, 6)
        B, T, D = (8, 64, 768)
        S, F = (64, 48)
        x = jax.random.normal(ks[0], (B, T, D), dtype=jnp.float32)
        slots = 0.02 * jax.random.normal(ks[1], (S, D), dtype=jnp.float32)
        scale = jnp.ones((S,), dtype=jnp.float32)
        fc1_weight = 0.02 * jax.random.normal(ks[2], (S, D, F), dtype=jnp.float32)
        fc1_bias = jnp.zeros((S, F), dtype=jnp.float32)
        fc2_weight = 0.02 * jax.random.normal(ks[3], (S, F, D), dtype=jnp.float32)
        fc2_bias = jnp.zeros((S, D), dtype=jnp.float32)
        norm_weight = jnp.ones((D,), dtype=jnp.float32)
        return {'x': x, 'slots': slots, 'scale': scale, 'fc1_weight': fc1_weight, 'fc1_bias': fc1_bias, 'fc2_weight': fc2_weight, 'fc2_bias': fc2_bias, 'norm_weight': norm_weight}
    _L0_ffn_all = _L0_ffn_setup()
    _L0_ffn_in = {k: v for k, v in _L0_ffn_all.items() if k in ('slots', 'scale', 'fc1_weight', 'fc1_bias', 'fc2_weight', 'fc2_bias', 'norm_weight')}
    del _L0_ffn_all

    def _L1_gnn_setup():
        import jax, jax.numpy as jnp
        import numpy as np
        N, E, D, T, EA = (50000, 2048, 768, 6, 32)
        H4 = D // 4
        EPS = 1e-05
        key = jax.random.key(seed)
        ks = jax.random.split(key, 24)

        def init(k, shape, fan_in):
            return (jax.random.normal(k, shape, jnp.float32) / np.sqrt(fan_in)).astype(jnp.float32)
        inp = {'x': jax.random.normal(ks[0], (N, D), jnp.float32), 'edge_index': jax.random.randint(ks[1], (2, E), 0, N, jnp.int64), 'edge_attr': jax.random.normal(ks[2], (E, EA), jnp.float32), 'node_types': jax.random.randint(ks[3], (N,), 0, T, jnp.int64), 'W_type': init(ks[4], (T, D, D), D), 'b_type': jnp.zeros((T, D), jnp.float32), 'msg_W1': init(ks[5], (2 * D, D), 2 * D), 'msg_b1': jnp.zeros((D,), jnp.float32), 'msg_W2': init(ks[6], (D, D), D), 'msg_b2': jnp.zeros((D,), jnp.float32), 'edge_W1': init(ks[7], (EA, H4), EA), 'edge_b1': jnp.zeros((H4,), jnp.float32), 'edge_W2': init(ks[8], (H4, 1), H4), 'edge_b2': jnp.zeros((1,), jnp.float32), 'agg_W1': init(ks[9], (D, D), D), 'agg_b1': jnp.zeros((D,), jnp.float32), 'agg_W2': init(ks[10], (D, D), D), 'agg_b2': jnp.zeros((D,), jnp.float32), 'out_W': init(ks[11], (D, D), D), 'out_b': jnp.zeros((D,), jnp.float32), 'ln_g': jnp.ones((D,), jnp.float32), 'ln_b': jnp.zeros((D,), jnp.float32)}
        return inp
    _L1_gnn_all = _L1_gnn_setup()
    _L1_gnn_in = {k: v for k, v in _L1_gnn_all.items() if k in ('W_type', 'b_type', 'msg_W1', 'msg_b1', 'msg_W2', 'msg_b2', 'edge_W1', 'edge_b1', 'edge_W2', 'edge_b2', 'agg_W1', 'agg_b1', 'agg_W2', 'agg_b2', 'out_W', 'out_b', 'ln_g', 'ln_b')}
    del _L1_gnn_all

    def _L1_ffn_setup():
        import jax, jax.numpy as jnp
        import numpy as np
        H = 768
        R = 64
        E = 8
        B, S = (8, 32)
        key = jax.random.key(seed)
        ks = jax.random.split(key, 10)
        s_in = 1.0 / np.sqrt(H)
        s_r = 1.0 / np.sqrt(R)
        return {'x': jax.random.normal(ks[0], (B, S, H), dtype=jnp.float32), 'enc_w': jax.random.uniform(ks[1], (H, R), jnp.float32, -s_in, s_in), 'enc_b': jax.random.uniform(ks[2], (R,), jnp.float32, -s_in, s_in), 'sw_w': jax.random.uniform(ks[3], (R, E), jnp.float32, -s_r, s_r), 'sw_b': jax.random.uniform(ks[4], (E,), jnp.float32, -s_r, s_r), 'w1': jax.random.uniform(ks[5], (E, H, R), jnp.float32, -s_in, s_in), 'b1': jax.random.uniform(ks[6], (E, R), jnp.float32, -s_in, s_in), 'w2': jax.random.uniform(ks[7], (E, R, H), jnp.float32, -s_r, s_r), 'b2': jax.random.uniform(ks[8], (E, H), jnp.float32, -s_r, s_r)}
    _L1_ffn_all = _L1_ffn_setup()
    _L1_ffn_in = {k: v for k, v in _L1_ffn_all.items() if k in ('enc_w', 'enc_b', 'sw_w', 'sw_b', 'w1', 'b1', 'w2', 'b2')}
    del _L1_ffn_all
    return {'x': x, 'src': src, 'dst': dst, 'edge_attr_256': edge_attr_256, 'edge_attr_32': edge_attr_32, 'node_type_6': node_type_6, 'L0_gnn_Wn': _L0_gnn_in['Wn'], 'L0_gnn_bn': _L0_gnn_in['bn'], 'L0_gnn_We': _L0_gnn_in['We'], 'L0_gnn_be': _L0_gnn_in['be'], 'L0_gnn_W1': _L0_gnn_in['W1'], 'L0_gnn_b1': _L0_gnn_in['b1'], 'L0_gnn_ln_g': _L0_gnn_in['ln_g'], 'L0_gnn_ln_b': _L0_gnn_in['ln_b'], 'L0_gnn_W2': _L0_gnn_in['W2'], 'L0_gnn_b2': _L0_gnn_in['b2'], 'L0_gnn_Wqkv': _L0_gnn_in['Wqkv'], 'L0_gnn_bqkv': _L0_gnn_in['bqkv'], 'L0_gnn_Wo': _L0_gnn_in['Wo'], 'L0_gnn_bo': _L0_gnn_in['bo'], 'L0_ffn_slots': _L0_ffn_in['slots'], 'L0_ffn_scale': _L0_ffn_in['scale'], 'L0_ffn_fc1_weight': _L0_ffn_in['fc1_weight'], 'L0_ffn_fc1_bias': _L0_ffn_in['fc1_bias'], 'L0_ffn_fc2_weight': _L0_ffn_in['fc2_weight'], 'L0_ffn_fc2_bias': _L0_ffn_in['fc2_bias'], 'L0_ffn_norm_weight': _L0_ffn_in['norm_weight'], 'L1_gnn_W_type': _L1_gnn_in['W_type'], 'L1_gnn_b_type': _L1_gnn_in['b_type'], 'L1_gnn_msg_W1': _L1_gnn_in['msg_W1'], 'L1_gnn_msg_b1': _L1_gnn_in['msg_b1'], 'L1_gnn_msg_W2': _L1_gnn_in['msg_W2'], 'L1_gnn_msg_b2': _L1_gnn_in['msg_b2'], 'L1_gnn_edge_W1': _L1_gnn_in['edge_W1'], 'L1_gnn_edge_b1': _L1_gnn_in['edge_b1'], 'L1_gnn_edge_W2': _L1_gnn_in['edge_W2'], 'L1_gnn_edge_b2': _L1_gnn_in['edge_b2'], 'L1_gnn_agg_W1': _L1_gnn_in['agg_W1'], 'L1_gnn_agg_b1': _L1_gnn_in['agg_b1'], 'L1_gnn_agg_W2': _L1_gnn_in['agg_W2'], 'L1_gnn_agg_b2': _L1_gnn_in['agg_b2'], 'L1_gnn_out_W': _L1_gnn_in['out_W'], 'L1_gnn_out_b': _L1_gnn_in['out_b'], 'L1_gnn_ln_g': _L1_gnn_in['ln_g'], 'L1_gnn_ln_b': _L1_gnn_in['ln_b'], 'L1_ffn_enc_w': _L1_ffn_in['enc_w'], 'L1_ffn_enc_b': _L1_ffn_in['enc_b'], 'L1_ffn_sw_w': _L1_ffn_in['sw_w'], 'L1_ffn_sw_b': _L1_ffn_in['sw_b'], 'L1_ffn_w1': _L1_ffn_in['w1'], 'L1_ffn_b1': _L1_ffn_in['b1'], 'L1_ffn_w2': _L1_ffn_in['w2'], 'L1_ffn_b2': _L1_ffn_in['b2']}

def reference(x, src, dst, edge_attr_256, edge_attr_32, node_type_6, L0_gnn_Wn, L0_gnn_bn, L0_gnn_We, L0_gnn_be, L0_gnn_W1, L0_gnn_b1, L0_gnn_ln_g, L0_gnn_ln_b, L0_gnn_W2, L0_gnn_b2, L0_gnn_Wqkv, L0_gnn_bqkv, L0_gnn_Wo, L0_gnn_bo, L0_ffn_slots, L0_ffn_scale, L0_ffn_fc1_weight, L0_ffn_fc1_bias, L0_ffn_fc2_weight, L0_ffn_fc2_bias, L0_ffn_norm_weight, L1_gnn_W_type, L1_gnn_b_type, L1_gnn_msg_W1, L1_gnn_msg_b1, L1_gnn_msg_W2, L1_gnn_msg_b2, L1_gnn_edge_W1, L1_gnn_edge_b1, L1_gnn_edge_W2, L1_gnn_edge_b2, L1_gnn_agg_W1, L1_gnn_agg_b1, L1_gnn_agg_W2, L1_gnn_agg_b2, L1_gnn_out_W, L1_gnn_out_b, L1_gnn_ln_g, L1_gnn_ln_b, L1_ffn_enc_w, L1_ffn_enc_b, L1_ffn_sw_w, L1_ffn_sw_b, L1_ffn_w1, L1_ffn_b1, L1_ffn_w2, L1_ffn_b2):
    import jax
    import jax.numpy as jnp

    def _L0_gnn_ref(node_features, edge_index, edge_features, Wn, bn, We, be, W1, b1, ln_g, ln_b, W2, b2, Wqkv, bqkv, Wo, bo):
        import jax, jax.numpy as jnp
        import numpy as np
        N_NODES = 64
        N_EDGES = 2048
        D = 768
        DE = 256
        L = 3
        H = 8
        DH = D // H
        EPS = 1e-05

        def _layernorm(x, g, b):
            mu = jnp.mean(x, axis=-1, keepdims=True)
            var = jnp.var(x, axis=-1, keepdims=True)
            return (x - mu) * jax.lax.rsqrt(var + EPS) * g + b
        n = node_features.shape[0]
        nodes = node_features @ Wn.T + bn
        edge_proj = edge_features @ We.T + be
        src, dst = (edge_index[0], edge_index[1])
        for l in range(L):
            msgs = nodes[src] + nodes[dst] + edge_proj
            agg = jax.ops.segment_sum(msgs, dst, num_segments=n)
            combined = jnp.concatenate([nodes, agg], axis=-1)
            h = combined @ W1[l].T + b1[l]
            h = _layernorm(h, ln_g[l], ln_b[l])
            h = jax.nn.relu(h)
            h = h @ W2[l].T + b2[l]
            nodes = h + nodes
        qkv = nodes @ Wqkv.T + bqkv
        q, k, v = jnp.split(qkv, 3, axis=-1)
        q = q.reshape(n, H, DH) * DH ** (-0.5)
        k = k.reshape(n, H, DH)
        v = v.reshape(n, H, DH)
        scores = jnp.einsum('nhd,mhd->hnm', q, k)
        probs = jax.nn.softmax(scores, axis=-1)
        attn = jnp.einsum('hnm,mhd->nhd', probs, v).reshape(n, D)
        attended = attn @ Wo.T + bo
        return nodes + attended

    def _L0_ffn_ref(x, slots, scale, fc1_weight, fc1_bias, fc2_weight, fc2_bias, norm_weight):
        import jax, jax.numpy as jnp
        import numpy as np
        EPS_NORM = 1e-05
        RMS_EPS = 1e-05

        def _l2_normalize(v):
            n = jnp.sqrt(jnp.sum(v * v, axis=-1, keepdims=True))
            return v / jnp.maximum(n, EPS_NORM)

        def _rms_norm(x, weight, eps):
            ms = jnp.mean(x * x, axis=-1, keepdims=True)
            return x * jax.lax.rsqrt(ms + eps) * weight
        xn = _rms_norm(x, norm_weight, RMS_EPS)
        tok = _l2_normalize(xn)
        sl = _l2_normalize(slots) * scale[:, None]
        logits = jnp.einsum('sd,btd->bst', sl, tok)
        dispatch_w = jax.nn.softmax(logits, axis=-1)
        combine_w = jax.nn.softmax(logits, axis=-2)
        y = jnp.einsum('btd,bst->bsd', xn, dispatch_w)
        y = jnp.einsum('sio,bsi->bso', fc1_weight, y) + fc1_bias
        y = jax.nn.gelu(y, approximate=False)
        y = jnp.einsum('sio,bsi->bso', fc2_weight, y) + fc2_bias
        out = jnp.einsum('bsd,bst->btd', y, combine_w)
        return out

    def _L1_gnn_ref(x, edge_index, edge_attr, node_types, W_type, b_type, msg_W1, msg_b1, msg_W2, msg_b2, edge_W1, edge_b1, edge_W2, edge_b2, agg_W1, agg_b1, agg_W2, agg_b2, out_W, out_b, ln_g, ln_b):
        import jax, jax.numpy as jnp
        import numpy as np
        N, E, D, T, EA = (50000, 2048, 768, 6, 32)
        H4 = D // 4
        EPS = 1e-05
        n = x.shape[0]
        all_h = jnp.einsum('ni,tio->tno', x, W_type)
        h = jnp.take_along_axis(all_h, node_types[None, :, None], axis=0)[0]
        h = h + b_type[node_types]
        row, col = (edge_index[0], edge_index[1])
        m_in = jnp.concatenate([h[row], h[col]], axis=1)
        m = jax.nn.relu(m_in @ msg_W1 + msg_b1) @ msg_W2 + msg_b2
        ew = jax.nn.sigmoid(jax.nn.relu(edge_attr @ edge_W1 + edge_b1) @ edge_W2 + edge_b2)
        m = m * ew
        agg = jax.ops.segment_sum(m, col, num_segments=n)
        agg = jax.nn.relu(agg @ agg_W1 + agg_b1) @ agg_W2 + agg_b2
        h = h + agg
        h = h @ out_W + out_b
        h = h + x
        mu = jnp.mean(h, axis=-1, keepdims=True)
        var = jnp.mean(jnp.square(h - mu), axis=-1, keepdims=True)
        h = (h - mu) * jax.lax.rsqrt(var + EPS) * ln_g + ln_b
        return h

    def _L1_ffn_ref(x, enc_w, enc_b, sw_w, sw_b, w1, b1, w2, b2):
        import jax, jax.numpy as jnp
        import numpy as np
        H = 768
        R = 64
        E = 8
        B, S = (8, 32)
        b, s, d = x.shape
        xt = x.reshape(-1, d)
        x_enc = xt @ enc_w + enc_b
        route_prob = jax.nn.softmax(x_enc @ sw_w + sw_b, axis=-1)
        route_prob_max = jnp.max(route_prob, axis=-1)
        routes = jnp.argmax(route_prob, axis=-1)
        onehot = jax.nn.one_hot(routes, E, dtype=xt.dtype)
        h = jnp.einsum('td,edr->ter', xt, w1) + b1[None]
        h = jax.nn.gelu(h, approximate=False)
        h = h * onehot[..., None]
        out = jnp.einsum('ter,erd->td', h, w2) + onehot @ b2
        out = out * route_prob_max[:, None]
        return out.reshape(b, s, d)
    edge_index = jnp.stack([src, dst])
    x = x + _L0_gnn_ref(_layernorm(x, axis=-1), edge_index, edge_attr_256, L0_gnn_Wn, L0_gnn_bn, L0_gnn_We, L0_gnn_be, L0_gnn_W1, L0_gnn_b1, L0_gnn_ln_g, L0_gnn_ln_b, L0_gnn_W2, L0_gnn_b2, L0_gnn_Wqkv, L0_gnn_bqkv, L0_gnn_Wo, L0_gnn_bo)
    x = x + _L0_ffn_ref(_layernorm(x, axis=-1)[None], L0_ffn_slots, L0_ffn_scale, L0_ffn_fc1_weight, L0_ffn_fc1_bias, L0_ffn_fc2_weight, L0_ffn_fc2_bias, L0_ffn_norm_weight)[0]
    x = x + _L1_gnn_ref(_layernorm(x, axis=-1), edge_index, edge_attr_32, node_type_6, L1_gnn_W_type, L1_gnn_b_type, L1_gnn_msg_W1, L1_gnn_msg_b1, L1_gnn_msg_W2, L1_gnn_msg_b2, L1_gnn_edge_W1, L1_gnn_edge_b1, L1_gnn_edge_W2, L1_gnn_edge_b2, L1_gnn_agg_W1, L1_gnn_agg_b1, L1_gnn_agg_W2, L1_gnn_agg_b2, L1_gnn_out_W, L1_gnn_out_b, L1_gnn_ln_g, L1_gnn_ln_b)
    x = x + _L1_ffn_ref(_layernorm(x, axis=-1)[None], L1_ffn_enc_w, L1_ffn_enc_b, L1_ffn_sw_w, L1_ffn_sw_b, L1_ffn_w1, L1_ffn_b1, L1_ffn_w2, L1_ffn_b2)[0]
    return x

_drawn_inputs = setup_inputs


def setup_inputs(seed=0):
    import zlib

    import numpy as np

    out = dict(_drawn_inputs(seed))
    spreads = {'L0_gnn_bn': (0.0, 0.1),
     'L0_gnn_be': (0.0, 0.1),
     'L0_gnn_b1': (0.0, 0.8),
     'L0_gnn_ln_g': (1.0, 0.2),
     'L0_gnn_ln_b': (0.0, 0.1),
     'L0_gnn_b2': (0.0, 0.1),
     'L0_gnn_bqkv': (0.0, 0.1),
     'L0_gnn_bo': (0.0, 0.1),
     'L0_ffn_scale': (1.0, 0.6),
     'L0_ffn_fc1_bias': (0.0, 0.8),
     'L0_ffn_fc2_bias': (0.0, 0.8),
     'L0_ffn_norm_weight': (1.0, 0.6),
     'L1_gnn_b_type': (0.0, 0.1),
     'L1_gnn_msg_b1': (0.0, 0.1),
     'L1_gnn_msg_b2': (0.0, 0.1),
     'L1_gnn_edge_b1': (0.0, 0.8),
     'L1_gnn_agg_b1': (0.0, 0.8),
     'L1_gnn_agg_b2': (0.0, 0.8),
     'L1_gnn_out_b': (0.0, 0.8),
     'L1_gnn_ln_g': (1.0, 0.2),
     'L1_gnn_ln_b': (0.0, 0.1)}
    factors = {'edge_attr_32': 2.842,
     'L0_ffn_slots': 8.0,
     'L0_ffn_fc1_weight': 8.0,
     'L0_ffn_fc2_weight': 8.0,
     'L1_gnn_edge_W1': 2.973,
     'L1_ffn_enc_w': 3.09,
     'L1_ffn_enc_b': 8.0,
     'L1_ffn_sw_w': 3.116,
     'L1_ffn_sw_b': 4.837,
     'L1_ffn_w1': 3.158,
     'L1_ffn_b1': 8.0,
     'L1_ffn_w2': 3.073,
     'L1_ffn_b2': 7.89}
    for name, (base, spread) in spreads.items():
        noise = np.random.default_rng([zlib.crc32(name.encode()), seed]).standard_normal(out[name].shape)
        drawn = base * np.exp(spread * noise) if base else spread * noise
        out[name] = jnp.asarray(drawn.astype(out[name].dtype))
    for name, factor in factors.items():
        out[name] = (out[name] * factor).astype(out[name].dtype)
    return out
```

```python
import concourse.bass as bass
from concourse import mybir
from contextlib import ExitStack

N = 64
E = 2048
D = 768
HALF = D // 2
P = 128
NI = D // P
NJ = NI // 2
L = 3
DE = 256
DA = 32
H4 = D // 4
HEADS = 8
DH = D // HEADS
HJ = HEADS // 2
F = 48
TYPES = 6
R = 64
X = 8
TE = E // P
NB = N * F // D
SLOT = 3 * D
RING = 12
EPS = 1e-5

ROW_BE, ROW_BN, ROW_B1, ROW_B2, ROW_BQKV, ROW_BO, ROW_FC1 = 0, 1, 2, 5, 8, 11, 12
ROW_TYPE, ROW_MSG1, ROW_AGG1, ROW_AGG2, ROW_OUT, ROW_FFN1, ROW_EDGE1 = 16, 22, 23, 24, 25, 26, 27
ROW_MSG2, ROW_FFN2, ROW_FC2 = 32, 33, 64
SELS = ROW_EDGE1 + 1

C_NW, C_LNG, C_LNB, C_EW2, C_SWB, C_EB2 = 0, HALF, 2 * HALF, 3 * HALF, 4 * HALF, 4 * HALF + X
ROW_PACK = 4 * HALF + X + 1
C_G, C_B, C_ENCB, C_SCALE = 0, L * NI, 2 * L * NI, 2 * L * NI + 1
COL_PACK = 2 * L * NI + 2


def chunk(i):
    return 3 * (i % 2) + i // 2


def load_order():
    order = [("ef", 0), ("ef", 1), ("We", 0), ("Wn", 0), ("Wn", 1)]
    for l in range(L):
        order += [(f"W1a{l}", 0), (f"W1a{l}", 1), (f"W1b{l}", 0), (f"W1b{l}", 1), (f"W2{l}", 0), (f"W2{l}", 1)]
    order += [(f"W{c}", k) for c in "qkvo" for k in range(2)]
    order += [(f"fc1{b}", k) for b in range(NB) for k in range(2)]
    order += [(f"fc2{b}", k) for b in range(NB) for k in range(2)]
    order += [(f"Wt{t}", k) for t in range(TYPES) for k in range(2)]
    order += [("Wma", 0), ("Wmb", 0), ("Wma", 1), ("Wmb", 1)]
    order += [(w, k) for w in ("Wm2", "Wg1", "Wg2", "Wout", "w1", "w2") for k in range(2)]
    return order


def part_width(name):
    return {"ef": TE // 2 * DE, "We": 2 * D, "w1": 3 * X * R, "w2": 2 * D}.get(name, SLOT)


LOADS = load_order()
LOAD = {part: k for k, part in enumerate(LOADS)}

COMBINES = ["x0", "slots", "l0", "l1", "l2", "f0", "tok", "g1", "go", "f1"]
POWERS = ["x0", "slots", "l0", "l1", "l2", "f0", "rms", "tok", "g1", "go", "f1"]
TURNS = ["x0", "edges", "slots", "l0", "l1", "l2", "nodes", "attn", "tok", "xn1", "h", "msg", "agg1", "agg2", "h2", "x3"]
GATES = [(2, 1), (2, 1), (2, 0)]
CONSTS = ["ident", "mix", "iota", "pair", "small", "blocks", "sel", "fills", "slotmask"]


def build(nc, ins, out):
    fp32, bf16, i32 = mybir.dt.float32, mybir.dt.bfloat16, mybir.dt.int32
    ALU, ACT, AX = mybir.AluOpType, mybir.ActivationFunctionType, mybir.AxisListType
    ctx = ExitStack()
    with ctx:
        def sb(name, shape, dt=fp32):
            return ctx.enter_context(nc.sbuf_tensor(name, shape, dt))

        def bank(name):
            return ctx.enter_context(nc.psum_tensor(name, [P, 512], fp32))

        def sem(name):
            return ctx.enter_context(nc.semaphore(name))

        ring = sb("ring", [P, RING, SLOT])
        bias = sb("bias", [P, D])
        rowp = sb("rowp", [P, ROW_PACK])
        colp = sb("colp", [P, COL_PACK])
        x0 = sb("x0", [P, HALF])
        x1 = sb("x1", [P, HALF])
        x2 = sb("x2", [P, HALF])
        x3 = sb("x3", [P, HALF])
        nodes = sb("nodes", [P, HALF])
        row = sb("row", [P, HALF])
        keep = sb("keep", [P, HALF])
        hrow = sb("hrow", [P, HALF])
        tmp = sb("tmp", [P, HALF])
        cols = sb("cols", [P, NI, N])
        slots = sb("slots", [P, HALF])
        slots_t = sb("slots_t", [P, NI, N])
        edges2 = sb("edges2", [P, NJ, 4, N])
        comb = sb("comb", [P, NJ, 4, N])
        spread = sb("spread", [P, 4, N])
        idx = sb("idx", [P, 2 * TE], i32)
        idxf = sb("idxf", [P, 2 * TE])
        types = sb("types", [P, N], i32)
        typesf = sb("typesf", [P, N])
        typemask = sb("typemask", [P, TYPES, N])
        typesel = sb("typesel", [P, N])
        irow_i = sb("irow_i", [P, N], i32)
        irow = sb("irow", [P, N])
        icol_i = sb("icol_i", [P, 3], i32)
        icol = sb("icol", [P, 3])
        ramp_i = sb("ramp_i", [P, X], i32)
        ramp = sb("ramp", [P, X])
        pair = sb("pair", [P, E])
        to_dst = sb("to_dst", [P, TE, N])
        ones_b = sb("ones_b", [P, 1], bf16)
        degsel = sb("degsel", [P, N])
        gatesel = sb("gatesel", [P, N])
        routesel = sb("routesel", [P, N])
        ident = sb("ident", [P, P])
        mean2 = sb("mean2", [P, P])
        diff2 = sb("diff2", [P, P])
        pairup = sb("pairup", [P, N])
        sel = sb("sel", [P, SELS + 1, N])
        eps3 = sb("eps3", [P, 3])
        nhalf = sb("nhalf", [P, 1])
        slotmask = sb("slotmask", [P, NB * NI, N], bf16)
        stat6 = sb("stat6", [P, 6])
        mv = sb("mv", [P, len(COMBINES), 2])
        sc = sb("sc", [P, len(COMBINES), 4])
        pin = sb("pin", [P, len(POWERS)])
        pout = sb("pout", [P, len(POWERS)])
        small = sb("small", [P, 8])
        ea = sb("ea", [P, 4, P])
        ew1 = sb("ew1", [P, 4 * H4])
        ehid = sb("ehid", [P, 2, 2 * H4])
        eprod = sb("eprod", [P, 2, 2 * H4])
        gate_in = sb("gate_in", [P, TE])
        gate_z = sb("gate_z", [P, TE])
        gate_e = sb("gate_e", [P, TE])
        gate_d = sb("gate_d", [P, TE])
        gate = sb("gate", [P, TE])
        encw = sb("encw", [P, NI, R])
        sww = sb("sww", [R, X])
        big = sb("big", [P, 2 * NB * HALF + P + 2 * P + 2 * P])
        to_dst_b = big[:, 0:512].bitcast(bf16).rearrange("p (t n) -> p t n", t=TE)
        from_src_b = big[:, 512:1024].bitcast(bf16).rearrange("p (t n) -> p t n", t=TE)
        both_b = big[:, 1024:2048].bitcast(bf16).rearrange("p (t a n) -> p t a n", t=TE, a=2)
        qt = big[0:DH, 0:HJ * P].rearrange("p (j n) -> p j n", j=HJ)
        kt = big[0:DH, HJ * P:2 * HJ * P].rearrange("p (j n) -> p j n", j=HJ)
        qrow = big[:, 1024:1024 + HALF]
        krow = big[:, 1408:1408 + HALF]
        vrow = big[:, 1792:1792 + HALF]
        shifted = big[:, 2176:2432].rearrange("p (j m) -> p j m", j=HJ)
        probs = big[:, 2432:2944].rearrange("p (j m) -> p j m", j=HJ)
        probs_t = big[:, 2944:3456].rearrange("p (j m) -> p j m", j=HJ)
        hid = big[:, 0:NB * HALF].rearrange("p (b c) -> p b c", b=NB)
        hid_t = big[:, NB * HALF:2 * NB * HALF].rearrange("p (c n) -> p c n", n=N)
        typed = big[:, 0:TYPES * HALF].rearrange("p (t i n) -> p t i n", t=TYPES, i=NI)
        pq = big[:, 0:D]
        msg = big[:, D:4 * D].rearrange("p (k c) -> p k c", k=3)
        spare = big[:, 2 * NB * HALF + 3 * P:2 * NB * HALF + 5 * P]
        combine_w = spare[:, 0:P]
        dispatch_w = spare[:, P:2 * P]
        soft = sb("soft", [P, N])
        soft2 = sb("soft2", [P, 2, N])
        mx = sb("mx", [P, HJ])
        ssum = sb("ssum", [P, HJ])
        rsum = sb("rsum", [P, HJ])
        enc_t = sb("enc_t", [R, 2, N])
        lg = sb("lg", [P, X])
        pe_ = sb("pe_", [P, X])
        pr = sb("pr", [P, X])
        cand = sb("cand", [P, X])
        route = sb("route", [P, X])
        route_pad = sb("route_pad", [N, P])

        T = [bank(f"T{k}") for k in range(3)]
        ACC = [bank(f"ACC{k}") for k in range(4)]
        SM = bank("SM")

        arrived = [sem(f"arrived{k}") for k in range(RING)]
        ring_used = sem("ring_used")
        x_in, idx_in, type_in, bias_in, col_in, row_in = (sem(n) for n in ("x_in", "idx_in", "type_in", "bias_in", "col_in", "row_in"))
        slots_in, pair_in, ea_in, ew1_in, encw_in, sww_in = (sem(n) for n in ("slots_in", "pair_in", "ea_in", "ew1_in", "encw_in", "sww_in"))
        out_done = sem("out_done")
        consts_made, pool_link = sem("consts_made"), sem("pool_link")
        dve_link, act_link = sem("dve_link"), sem("act_link")
        stats_ready, combined, power_asked, power_done = sem("stats_ready"), sem("combined"), sem("power_asked"), sem("power_done")
        rows_ready, turned_a, turned_b, cols_a, cols_b = sem("rows_ready"), sem("turned_a"), sem("turned_b"), sem("cols_a"), sem("cols_b")
        onehots, onehot_copy, sums_made, spread_ready = sem("onehots"), sem("onehot_copy"), sem("sums_made"), sem("spread_ready")
        edges_made, edges_kept = sem("edges_made"), sem("edges_kept")
        nodes_ready, comb_made, comb_ready = sem("nodes_ready"), sem("comb_made"), sem("comb_ready")
        gate_made, gate_relu, gate_mult, gate_red = sem("gate_made"), sem("gate_relu"), sem("gate_mult"), sem("gate_red")
        gate_asked, gate_exp, gate_ready, gsum_made, gsum_ready = sem("gate_asked"), sem("gate_exp"), sem("gate_ready"), sem("gsum_made"), sem("gsum_ready")
        q_row, k_row, v_row, heads_turned, q_cols, k_cols = (sem(n) for n in ("q_row", "k_row", "v_row", "heads_turned", "q_cols", "k_cols"))
        scores_made, scores_shift, probs_made, probs_turned = sem("scores_made"), sem("scores_shift"), sem("probs_made"), sem("probs_turned")
        probs_a, probs_b, attn_made = sem("probs_a"), sem("probs_b"), sem("attn_made")
        logits_made, logits_max, soft_made, soft_ready, soft_turned = sem("logits_made"), sem("logits_max"), sem("soft_made"), sem("soft_ready"), sem("soft_turned")
        weights_act, weights_dve, mixed_made, mixed_a, mixed_b = sem("weights_act"), sem("weights_dve"), sem("mixed_made"), sem("mixed_a"), sem("mixed_b")
        hid_made, hid_turned, hid_masked, y_ready, mix_out = sem("hid_made"), sem("hid_turned"), sem("hid_masked"), sem("y_ready"), sem("mix_out")
        typed_ready, typesel_ready, pq_act, pq_dve = sem("typed_ready"), sem("typesel_ready"), sem("pq_act"), sem("pq_dve")
        pair_ready, gathered, msg_act, msg_dve, scattered = sem("pair_ready"), sem("gathered"), sem("msg_act"), sem("msg_dve"), sem("scattered")
        enc_made, enc_ready, route_made, route_max, route_exp = sem("enc_made"), sem("enc_ready"), sem("route_made"), sem("route_max"), sem("route_exp")
        route_ready, route_turned, routesel_ready = sem("route_ready"), sem("route_turned"), sem("routesel_ready")
        gelu_made, exp_turned, exp_cols, final_ready = sem("gelu_made"), sem("exp_turned"), sem("exp_cols"), sem("final_ready")

        def used(name, part=1):
            return LOAD[name, part] + 1

        def slot(name, part):
            k = LOAD[name, part]
            return ring[:, k % RING, 0:part_width(name)]

        def at(names, name):
            return names.index(name) + 1

        def halves(ap, n=HALF):
            return [(h, ap[h * N:(h + 1) * N, 0:n]) for h in range(2)]

        block = ctx.enter_context(nc.Block())

        @block.sync
        def _(sp):
            sp.dma_start(x0[:, :], ins["x"]).then_inc(x_in, 16)
            for k, (name, part) in enumerate(LOADS):
                if k >= RING:
                    sp.wait_ge(ring_used, k - RING + 1)
                src = ins[name]
                w = part_width(name)
                sp.dma_start(slot(name, part), src[:, part * w:(part + 1) * w]).then_inc(arrived[k % RING], 16)
            sp.wait_ge(final_ready, 1)
            sp.dma_start(out, row[:, :]).then_inc(out_done, 16)
            sp.wait_ge(out_done, 16)

        @block.gpsimd
        def _(pool):
            links = [0]

            def link(op):
                links[0] += 1
                op.then_inc(pool_link, 1)
                pool.wait_ge(pool_link, links[0])

            made = [0]

            def done(op):
                made[0] += 1
                op.then_inc(consts_made, 1)
                pool.wait_ge(consts_made, made[0])

            def diagonal(ap, base, pattern, fill):
                return nc.gpsimd.affine_select(out=ap, in_=ap, pattern=pattern, compare_op=ALU.not_equal, fill=fill,
                                               base=base, channel_multiplier=1)

            link(nc.gpsimd.memset(ident[:, :], 0.0))
            done(diagonal(ident[:, :], 0, [[-1, P]], 1.0))
            link(nc.gpsimd.memset(mean2[:, :], 0.0))
            link(nc.gpsimd.memset(diff2[:, :], 0.0))
            link(nc.gpsimd.memset(eps3[:, :], 0.0))
            link(nc.gpsimd.memset(eps3[:, 1:2], EPS))
            link(nc.gpsimd.memset(nhalf[:, :], -0.5))
            for h in range(2):
                lo = slice(h * N, (h + 1) * N)
                link(diagonal(mean2[lo, :].rearrange("p (a n) -> p a n", a=2), 0, [[0, 2], [-1, N]], 0.5))
                last = diagonal(diff2[lo, :].rearrange("p (a n) -> p a n", a=2), 0, [[0, 2], [-1, N]], 0.5 - h)
                (done if h else link)(last)
            link(nc.gpsimd.iota(irow_i[:, :], pattern=[[1, N]], base=0, channel_multiplier=0))
            for h in range(2):
                link(nc.gpsimd.iota(icol_i[h * N:(h + 1) * N, 0:1], pattern=[[0, 1]], base=0, channel_multiplier=1))
            link(nc.gpsimd.iota(icol_i[:, 1:2], pattern=[[0, 1]], base=-ROW_TYPE, channel_multiplier=1))
            done(nc.gpsimd.iota(ramp_i[:, :], pattern=[[-1, X]], base=X, channel_multiplier=0))
            link(nc.gpsimd.memset(pairup[:, :], 0.0))
            link(diagonal(pairup[0:N, :], 0, [[-1, N]], 1.0))
            done(diagonal(pairup[N:P, :], 0, [[-1, N]], 1.0))
            link(nc.gpsimd.memset(ones_b[:, :], 1.0))
            link(nc.gpsimd.memset(degsel[:, :], 0.0))
            done(nc.gpsimd.memset(gatesel[:, :], 0.0))
            link(nc.gpsimd.memset(spread[:, :, :], 0.0))
            link(diagonal(spread[0:N, 0, :], 0, [[-1, N]], 1.0))
            done(diagonal(spread[N:P, 2, :], 0, [[-1, N]], 1.0))
            link(nc.gpsimd.memset(sel[:, :, :], 0.0))
            link(diagonal(sel[:, 0:SELS, :], 0, [[-1, SELS], [0, N]], 1.0))
            done(diagonal(sel[:, SELS, :], -ROW_EDGE1, [[0, N]], 1.0))
            link(nc.gpsimd.memset(edges2[:, :, :, :], 0.0))
            link(nc.gpsimd.memset(probs, 0.0))
            link(nc.gpsimd.memset(spare[:, 0:2 * P], 0.0))
            done(nc.gpsimd.memset(route_pad[:, :], 0.0))

            def power(name):
                k = POWERS.index(name)
                pool.wait_ge(power_asked, k + 1)
                nc.gpsimd.tensor_tensor(pout[:, k:k + 1], pin[:, k:k + 1], nhalf[:, :], ALU.pow).then_inc(power_done, 1)

            power("x0")
            power("slots")
            link(nc.gpsimd.memset(slotmask[:, :, :], 1.0))
            for b in range(NB):
                for h in range(2):
                    v = slotmask[:, b * NI:(b + 1) * NI, :].rearrange("p (j h) n -> p j h n", h=2)[:, :, h, :]
                    link(nc.gpsimd.affine_select(out=v, in_=v, pattern=[[P, NJ], [-F, N]], compare_op=ALU.is_ge,
                                                 fill=0.0, base=b * D + h * HALF, channel_multiplier=1))
                    last = nc.gpsimd.affine_select(out=v, in_=v, pattern=[[-P, NJ], [F, N]], compare_op=ALU.is_ge,
                                                   fill=0.0, base=F - 1 - b * D - h * HALF, channel_multiplier=-1)
                    (done if (b, h) == (NB - 1, 1) else link)(last)
            pool.wait_ge(row_in, 32)
            u = 0
            for l in range(L):
                power(f"l{l}")
                for _ in range(sum(GATES[l])):
                    pool.wait_ge(gate_relu, u + 1)
                    if u >= 2:
                        pool.wait_ge(gate_red, u - 1)
                    nc.gpsimd.tensor_tensor(eprod[:, u % 2, :], ehid[:, u % 2, :], rowp[:, C_EW2:C_EW2 + 2 * H4],
                                            ALU.mult).then_inc(gate_mult, 1)
                    u += 1
            for name in POWERS[POWERS.index("f0"):]:
                power(name)

        @block.tensor
        def _(pe):
            def mm(o, lhsT, rhs, start=True, stop=True):
                return nc.tensor.matmul(o, lhsT, rhs, start=start, stop=stop)

            def ready(name, part):
                k = LOAD[name, part]
                pe.wait_ge(arrived[k % RING], 16 * (k // RING + 1))

            def combine(name, sums=False):
                k = COMBINES.index(name)
                pe.wait_ge(stats_ready, k + 1)
                last = mm(SM[:, 0:2], mean2[:, :], mv[:, k, :])
                if not sums:
                    last = mm(SM[:, 2:3], diff2[:, :], mv[:, k, 0:1])
                last.then_inc(combined, 1)

            def turn(name, src):
                pe.wait_ge(rows_ready, at(TURNS, name))
                for j in range(NJ):
                    o = T[j // 2][:, (j % 2) * P:(j % 2 + 1) * P]
                    last = nc.tensor.transpose(o, src[:, j * P:(j + 1) * P], ident[:, :])
                    if j == 1:
                        last.then_inc(turned_a, 1)
                last.then_inc(turned_b, 1)

            def add_bias(acc, k, stat=None, width=HALF, start=True):
                for h in range(2):
                    last = mm(acc[h * N:(h + 1) * N, 0:width], sel[:, k, :] if stat is None else stat,
                              bias[:, h * width:(h + 1) * width], start, False)
                return last

            def product(acc, stationary, name, turn_name=None, first=False, end=True, width=HALF, per=3, n=NI):
                for i in range(n):
                    if turn_name and i == 0:
                        pe.wait_ge(cols_a, at(TURNS, turn_name))
                    if turn_name and i == 4:
                        pe.wait_ge(cols_b, at(TURNS, turn_name))
                    if i % per == 0:
                        ready(name, i // per)
                    w = slot(name, i // per).rearrange("p (i c) -> p i c", i=per)
                    for h in range(2):
                        last = mm(acc[h * N:(h + 1) * N, 0:width], stationary(i),
                                  w[:, i % per, h * width:(h + 1) * width], first and i == 0, end and i == n - 1)
                    if i % per == per - 1:
                        last.then_inc(ring_used, 1)

            def chunks(t):
                return lambda i: t[:, i, :]

            pe.wait_ge(consts_made, at(CONSTS, "mix"))
            combine("x0")
            turn("x0", row)
            pe.wait_ge(onehots, 1)
            pe.wait_ge(onehot_copy, 1)
            for t in range(TE):
                mm(ACC[3][:, 0:N], both_b[:, t, :, :], to_dst_b[:, t, :], t == 0, t == TE - 1)
            pe.wait_ge(consts_made, at(CONSTS, "small"))
            for t in range(TE):
                last = mm(ACC[3][0:1, N:2 * N], ones_b[:, :], to_dst_b[:, t, :], t == 0, t == TE - 1)
            last.then_inc(sums_made, 1)
            for part in range(2):
                ready("ef", part)
                ef = slot("ef", part).rearrange("p (t c) -> p t c", c=DE)
                for t in range(TE // 2):
                    tt = part * TE // 2 + t
                    h = t % 2
                    last = mm(ACC[1][h * N:(h + 1) * N, 0:DE], to_dst[:, tt, :], ef[:, t, :], tt < 2, tt >= TE - 2)
                last.then_inc(ring_used, 1)
            pe.wait_ge(edges_kept, 1)
            pe.wait_ge(consts_made, at(CONSTS, "pair"))
            for c in range(2):
                last = mm(ACC[2][:, c * N:(c + 1) * N], tmp[:, c * P:(c + 1) * P], pairup[:, :])
            last.then_inc(edges_made, 1)
            pe.wait_ge(spread_ready, 1)
            pe.wait_ge(bias_in, 16)
            add_bias(ACC[1], None, degsel[:, :])
            pe.wait_ge(edges_kept, 2)
            ready("We", 0)
            we = slot("We", 0).rearrange("p (c n) -> p c n", c=2)
            for c in range(2):
                for h in range(2):
                    last = mm(ACC[1][h * N:(h + 1) * N, 0:HALF], hrow[:, c * N:(c + 1) * N],
                              we[:, c, h * HALF:(h + 1) * HALF], False, c == 1)
            last.then_inc(ring_used, 1)
            pe.wait_ge(cols_a, at(TURNS, "x0"))
            pe.wait_ge(cols_b, at(TURNS, "x0"))
            turn("edges", tmp)
            combine("slots", sums=True)
            pe.wait_ge(cols_a, at(TURNS, "edges"))
            pe.wait_ge(cols_b, at(TURNS, "edges"))
            turn("slots", slots)
            pe.wait_ge(consts_made, at(CONSTS, "sel"))
            add_bias(ACC[0], ROW_BN)
            product(ACC[0], chunks(cols), "Wn")
            pe.wait_ge(cols_a, at(TURNS, "slots"))
            pe.wait_ge(cols_b, at(TURNS, "slots"))

            def gate_hidden(count):
                for _ in range(count):
                    u = tiles[0]
                    acc = ACC[2 + u % 2]
                    if u == 0:
                        pe.wait_ge(ea_in, 16)
                        pe.wait_ge(ew1_in, 16)
                    if u >= 2:
                        pe.wait_ge(gate_relu, u - 1)
                    mm(acc[:, 0:2 * H4], sel[:, ROW_EDGE1:ROW_EDGE1 + 2, :], bias[:, 0:2 * H4], True, False)
                    mm(acc[:, 0:2 * H4], ea[:, u // 2, :], ew1[:, (u % 2) * 2 * H4:(u % 2 + 1) * 2 * H4], False, True)\
                        .then_inc(gate_made, 1)
                    tiles[0] += 1

            tiles = [0]
            for l in range(L):
                add_bias(ACC[1], ROW_B1 + l)
                pe.wait_ge(nodes_ready, l + 1)
                for j in range(NJ):
                    mm(T[j][:, 0:4 * N], nodes[:, j * P:(j + 1) * P], spread[:, :, :]).then_inc(comb_made, 1)
                pe.wait_ge(comb_ready, NJ * (l + 1))
                product(ACC[1], lambda i: comb[:, i // 2, 2 * (i % 2), :], f"W1a{l}", end=False)
                product(ACC[1], lambda i: comb[:, i // 2, 2 * (i % 2) + 1, :], f"W1b{l}")
                gate_hidden(GATES[l][0])
                combine(f"l{l}")
                turn(f"l{l}", row)
                add_bias(ACC[0], ROW_B2 + l)
                product(ACC[0], chunks(cols), f"W2{l}", f"l{l}")
                gate_hidden(GATES[l][1])

            turn("nodes", nodes)
            for k, c in enumerate("qkv"):
                if k == 2:
                    pe.wait_ge(gate_relu, 8)
                add_bias(ACC[k], ROW_BQKV + k)
                product(ACC[k], chunks(cols), f"W{c}", "nodes")
            for k, (src, there) in enumerate(((qrow, q_row), (krow, k_row))):
                pe.wait_ge(there, 1)
                for j in range(HJ):
                    last = nc.tensor.transpose(T[k][0:DH, j * P:(j + 1) * P], src[:, j * DH:(j + 1) * DH], ident[:, :])
                last.then_inc(heads_turned, 1)
            pe.wait_ge(q_cols, 1)
            pe.wait_ge(k_cols, 1)
            for j in range(HJ):
                for h in range(2):
                    last = mm(ACC[0][h * N:(h + 1) * N, j * N:(j + 1) * N], qt[:, j, h * N:(h + 1) * N],
                              kt[:, j, h * N:(h + 1) * N])
            last.then_inc(scores_made, 1)
            pe.wait_ge(probs_made, 2)
            for k in range(2):
                for j in range(2):
                    last = nc.tensor.transpose(T[k][:, j * P:(j + 1) * P], probs[:, 2 * k + j, :], ident[:, :])
                last.then_inc(probs_turned, 1)
            pe.wait_ge(v_row, 1)
            pe.wait_ge(probs_a, 1)
            pe.wait_ge(probs_b, 1)
            for j in range(HJ):
                last = mm(ACC[1][:, j * DH:(j + 1) * DH], probs_t[:, j, :], vrow[:, j * DH:(j + 1) * DH])
            last.then_inc(attn_made, 1)
            turn("attn", row)
            add_bias(ACC[2], ROW_BO)
            product(ACC[2], chunks(cols), "Wo", "attn")
            pe.wait_ge(gate_ready, 1)
            for t in range(TE):
                last = mm(ACC[3][ROW_MSG2:ROW_MSG2 + 1, 0:N], gate[:, t:t + 1], to_dst[:, t, :], t == 0, t == TE - 1)
            last.then_inc(gsum_made, 1)

            combine("f0")
            combine("tok", sums=True)
            turn("tok", row)
            pe.wait_ge(cols_a, at(TURNS, "tok"))
            pe.wait_ge(cols_b, at(TURNS, "tok"))
            for i in range(NI):
                mm(ACC[0][0:N, 0:N], cols[:, i, :], slots_t[:, i, :], i == 0, i == NI - 1)
                last = mm(ACC[0][N:P, 0:N], slots_t[:, i, :], cols[:, i, :], i == 0, i == NI - 1)
            last.then_inc(logits_made, 1)
            pe.wait_ge(soft_ready, 1)
            nc.tensor.transpose(T[0][:, 0:P], soft2[:, :, :], ident[:, :]).then_inc(soft_turned, 1)
            pe.wait_ge(weights_act, 2)
            pe.wait_ge(weights_dve, 2)
            for j in range(NJ):
                last = mm(T[1 + j // 2][:, (j % 2) * P:(j % 2 + 1) * P], keep[:, j * P:(j + 1) * P], dispatch_w)
            last.then_inc(mixed_made, 1)
            pe.wait_ge(gsum_ready, 1)
            for b in range(NB):
                add_bias(ACC[b], ROW_FC1 + b)
                if b == 0:
                    pe.wait_ge(mixed_a, 1)
                    pe.wait_ge(mixed_b, 1)
                product(ACC[b], chunks(cols), f"fc1{b}")
            for b in range(NB):
                pe.wait_ge(hid_made, b + 1)
                if b == 3:
                    pe.wait_ge(hid_masked, 1)
                for j in range(NJ):
                    last = nc.tensor.transpose(T[b % 3][:, j * P:(j + 1) * P], hid[:, b, j * P:(j + 1) * P], ident[:, :])
                last.then_inc(hid_turned, 1)
            for h in range(2):
                mm(ACC[0][h * N:(h + 1) * N, 0:HALF], ident[:, ROW_FC2:ROW_FC2 + N], bias[:, h * HALF:(h + 1) * HALF], True, False)
            for b in range(NB):
                pe.wait_ge(hid_masked, b + 1)
                product(ACC[0], lambda i: hid_t[:, b * NI + i, :], f"fc2{b}", end=b == NB - 1)
            pe.wait_ge(y_ready, 1)
            mm(ACC[1][:, 0:HALF], combine_w, tmp[:, :]).then_inc(mix_out, 1)

            combine("g1")
            turn("xn1", keep)
            pe.wait_ge(typesel_ready, 1)
            add_bias(ACC[0], None, typesel[:, :])
            for t in range(TYPES):
                pe.wait_ge(typed_ready, t + 1)
                product(ACC[0], lambda i: typed[:, t, i, :], f"Wt{t}", end=t == TYPES - 1)
            turn("h", hrow)
            for f in range(2):
                mm(ACC[1 + f][N:P, 0:HALF], sel[:, ROW_MSG1, :], bias[:, f * HALF:(f + 1) * HALF], True, False)
            pe.wait_ge(cols_a, at(TURNS, "h"))
            pe.wait_ge(cols_b, at(TURNS, "h"))
            for i in range(NI):
                if i % 3 == 0:
                    ready("Wma", i // 3)
                    ready("Wmb", i // 3)
                wa = slot("Wma", i // 3).rearrange("p (i c) -> p i c", i=3)
                wb = slot("Wmb", i // 3).rearrange("p (i c) -> p i c", i=3)
                for f in range(2):
                    cs = slice(f * HALF, (f + 1) * HALF)
                    last_a = mm(ACC[1 + f][0:N, 0:HALF], cols[:, i, :], wa[:, i % 3, cs], i == 0, i == NI - 1)
                    last_b = mm(ACC[1 + f][N:P, 0:HALF], cols[:, i, :], wb[:, i % 3, cs], False, i == NI - 1)
                if i % 3 == 2:
                    last_a.then_inc(ring_used, 1)
                    last_b.then_inc(ring_used, 1)
            banks = [(T[0], T[1]), (T[2], SM), (ACC[3], ACC[1])]

            def gather(t):
                if t >= 3:
                    pe.wait_ge(msg_act, t - 2)
                    pe.wait_ge(msg_dve, t - 2)
                for f in range(2):
                    last = mm(banks[t % 3][f][:, 0:HALF], pair[:, t * P:(t + 1) * P], pq[:, f * HALF:(f + 1) * HALF])
                last.then_inc(gathered, 1)

            def scatter(t):
                pe.wait_ge(msg_act, t + 1)
                pe.wait_ge(msg_dve, t + 1)
                for h in range(2):
                    last = mm(ACC[0][h * N:(h + 1) * N, 0:HALF], to_dst[:, t, :], msg[:, t % 3, h * HALF:(h + 1) * HALF],
                              t == 0, t == TE - 1)
                last.then_inc(scattered, 1)

            pe.wait_ge(pair_ready, 1)
            pe.wait_ge(pq_act, 1)
            pe.wait_ge(pq_dve, 1)
            gather(0)
            gather(1)
            for t in range(TE):
                if t + 2 < TE:
                    gather(t + 2)
                scatter(t)
            turn("msg", row)
            add_bias(ACC[1], None, gatesel[:, :])
            product(ACC[1], chunks(cols), "Wm2", "msg")
            turn("agg1", row)
            add_bias(ACC[2], ROW_AGG1)
            product(ACC[2], chunks(cols), "Wg1", "agg1")
            turn("agg2", row)
            add_bias(ACC[1], ROW_AGG2)
            product(ACC[1], chunks(cols), "Wg2", "agg2")
            turn("h2", row)
            add_bias(ACC[2], ROW_OUT)
            product(ACC[2], chunks(cols), "Wout", "h2")
            combine("go")

            combine("f1")
            turn("x3", row)
            pe.wait_ge(encw_in, 16)
            pe.wait_ge(cols_a, at(TURNS, "x3"))
            pe.wait_ge(cols_b, at(TURNS, "x3"))
            for i in range(NI):
                last = mm(ACC[3][0:R, 0:N], encw[:, i, :], cols[:, i, :], i == 0, i == NI - 1)
            last.then_inc(enc_made, 1)
            add_bias(ACC[0], ROW_FFN1, width=4 * R)
            product(ACC[0], chunks(cols), "w1", width=4 * R)
            pe.wait_ge(enc_ready, 1)
            pe.wait_ge(sww_in, 16)
            mm(T[2][:, 0:X], enc_t[:, :, :], sww[:, :]).then_inc(route_made, 1)
            pe.wait_ge(route_ready, 1)
            nc.tensor.transpose(ACC[3][:, 0:N], route_pad[:, :], ident[0:N, 0:N]).then_inc(route_turned, 1)
            pe.wait_ge(gelu_made, 1)
            for j in range(2):
                last = nc.tensor.transpose(T[0][:, j * P:(j + 1) * P], tmp[:, j * P:(j + 1) * P], ident[:, :])
            last.then_inc(exp_turned, 1)
            pe.wait_ge(routesel_ready, 1)
            add_bias(ACC[1], None, routesel[:, :])
            pe.wait_ge(exp_cols, 1)
            product(ACC[1], chunks(cols), "w2", per=2, n=4)

        @block.vector
        def _(dve):
            v = nc.vector
            links = [0]

            def link(op):
                links[0] += 1
                op.then_inc(dve_link, 1)
                dve.wait_ge(dve_link, links[0])

            def moments(name, src):
                k = COMBINES.index(name)
                link(v.bn_stats(stat6[:, :], src))
                v.bn_aggr(mv[:, k, :], stat6[:, :]).then_inc(stats_ready, 1)
                dve.wait_ge(combined, k + 1)
                link(v.tensor_tensor(sc[:, k, 0:3], SM[:, 0:3], eps3[:, :], ALU.add))
                q = POWERS.index(name)
                v.scalar_tensor_tensor(out=pin[:, q:q + 1], in0=sc[:, k, 2:3], scalar=sc[:, k, 2:3], in1=sc[:, k, 1:2],
                                       op0=ALU.mult, op1=ALU.add).then_inc(power_asked, 1)

            def root(name):
                q = POWERS.index(name)
                dve.wait_ge(power_done, q + 1)
                return pout[:, q:q + 1]

            def normalise(dst, name, src):
                r = root(name)
                k = COMBINES.index(name)
                return v.tensor_scalar(dst, src, sc[:, k, 0:1], r, ALU.subtract, ALU.mult)

            def collect(name, dst=None):
                dve.wait_ge(turned_a, at(TURNS, name))
                v.tensor_copy(cols[:, 0:4, :] if dst is None else dst, T[0][:, 0:4 * N]).then_inc(cols_a, 1)

            def sums_root(name, src):
                k, q = COMBINES.index(name), POWERS.index(name)
                link(v.tensor_tensor_reduce(out=tmp[:, :], in0=src, in1=src, scale=1.0, scalar=0.0, op0=ALU.mult,
                                            op1=ALU.add, accum_out=mv[:, k, 0:1]))
                v.tensor_copy(mv[:, k, 1:2], mv[:, k, 0:1]).then_inc(stats_ready, 1)
                dve.wait_ge(combined, k + 1)
                v.tensor_scalar(pin[:, q:q + 1], SM[:, 0:1], 2.0, EPS * EPS, ALU.mult, ALU.max).then_inc(power_asked, 1)

            dve.wait_ge(x_in, 16)
            dve.wait_ge(consts_made, at(CONSTS, "mix"))
            moments("x0", x0[:, :])
            dve.wait_ge(idx_in, 16)
            dve.wait_ge(consts_made, at(CONSTS, "iota"))
            v.tensor_copy(idxf[:, :], idx[:, :])
            link(v.tensor_copy(irow[:, :], irow_i[:, :]))
            normalise(row[:, :], "x0", x0[:, :]).then_inc(rows_ready, 1)

            def onehot(o, c0):
                return v.tensor_tensor(o, idxf[:, c0:c0 + TE].unsqueeze(2).to_broadcast([P, TE, N]),
                                       irow[:, :].unsqueeze(1).to_broadcast([P, TE, N]), ALU.is_equal)

            onehot(to_dst[:, :, :], TE).then_inc(onehot_copy, 1)
            onehot(to_dst_b[:, :, :], TE)
            link(onehot(from_src_b[:, :, :], 0))
            for a in range(2):
                last = v.tensor_tensor(both_b[:, :, a, :], from_src_b[:, :, :], to_dst_b[:, :, :], ALU.add)
            last.then_inc(onehots, 1)
            collect("x0")
            dve.wait_ge(consts_made, at(CONSTS, "blocks"))
            dve.wait_ge(sums_made, 1)
            v.tensor_copy(spread[0:N, 1, :], ACC[3][0:N, 0:N])
            v.tensor_copy(spread[N:P, 3, :], ACC[3][N:P, 0:N])
            v.tensor_copy(degsel[0:1, :], ACC[3][0:1, N:2 * N]).then_inc(spread_ready, 1)
            dve.wait_ge(consts_made, at(CONSTS, "fills"))
            e2 = edges2[:, :, :, :].rearrange("p j (h q) n -> p j h q n", q=2)[:, :, :, 1, :]
            dve.wait_ge(turned_a, at(TURNS, "edges"))
            v.tensor_copy(e2[:, 0:2], T[0][:, 0:4 * N].rearrange("p (j h n) -> p j h n", j=2, h=2)).then_inc(cols_a, 1)
            dve.wait_ge(slots_in, 16)
            dve.wait_ge(col_in, 16)
            dve.wait_ge(turned_b, at(TURNS, "edges"))
            sums_root("slots", slots[:, :])
            r = root("slots")
            v.tensor_scalar(slots[:, :], slots[:, :], r, colp[:, C_SCALE:C_SCALE + 1], ALU.mult, ALU.mult)\
                .then_inc(rows_ready, 1)
            collect("slots", slots_t[:, 0:4, :])
            dve.wait_ge(type_in, 16)
            v.tensor_copy(ramp[:, :], ramp_i[:, :])
            v.tensor_copy(icol[:, 0:2], icol_i[:, 0:2])
            link(v.tensor_copy(typesf[:, :], types[:, :]))
            for t in range(TYPES):
                v.tensor_scalar(typemask[:, t, :], typesf[:, :], float(t), None, ALU.is_equal)
            v.tensor_scalar(typesel[:, :], typesf[:, :], icol[:, 1:2], None, ALU.is_equal).then_inc(typesel_ready, 1)
            dve.wait_ge(ring_used, used("Wn"))
            v.tensor_copy(nodes[:, :], ACC[0][:, 0:HALF]).then_inc(nodes_ready, 1)
            dve.wait_ge(cols_b, at(TURNS, "edges"))

            u = 0
            for l in range(L):
                for j in range(NJ):
                    dve.wait_ge(comb_made, NJ * l + j + 1)
                    v.tensor_tensor(comb[:, j, :, :], T[j][:, 0:4 * N].rearrange("p (q n) -> p q n", q=4),
                                    edges2[:, j, :, :], ALU.add).then_inc(comb_ready, 1)
                if l == 0:
                    dve.wait_ge(pair_in, 32)
                    v.tensor_scalar(pair[:, :], pair[:, :].bitcast(i32), icol[:, 0:1], None, ALU.is_equal)\
                        .then_inc(pair_ready, 1)
                while u < (0, 3, 6)[l]:
                    dve.wait_ge(gate_mult, u + 1)
                    v.tensor_reduce(gate_in[:, 2 * u:2 * u + 2], eprod[:, u % 2, :].rearrange("p (a c) -> p a c", a=2),
                                    AX.X, ALU.add).then_inc(gate_red, 1)
                    u += 1
                dve.wait_ge(ring_used, used(f"W1b{l}"))
                moments(f"l{l}", ACC[1][:, 0:HALF])
                normalise(row[:, :], f"l{l}", ACC[1][:, 0:HALF]).then_inc(rows_ready, 1)
                dve.wait_ge(turned_b, at(TURNS, f"l{l}"))
                for i in (4, 5):
                    op = v.tensor_scalar(cols[:, i, :], T[1][:, (i - 4) * N:(i - 3) * N], colp[:, C_G + l * NI + i:C_G + l * NI + i + 1],
                                         colp[:, C_B + l * NI + i:C_B + l * NI + i + 1], ALU.mult, ALU.add)
                link(op)
                v.tensor_scalar(cols[:, 4:6, :], cols[:, 4:6, :], 0.0, None, ALU.max).then_inc(cols_b, 1)
                dve.wait_ge(ring_used, used(f"W2{l}"))
                last = v.tensor_tensor(nodes[:, :], ACC[0][:, 0:HALF], nodes[:, :], ALU.add)
                if l < L - 1:
                    last.then_inc(nodes_ready, 1)
                else:
                    last.then_inc(rows_ready, 1)
            while u < 8:
                dve.wait_ge(gate_mult, u + 1)
                op = v.tensor_reduce(gate_in[:, 2 * u:2 * u + 2], eprod[:, u % 2, :].rearrange("p (a c) -> p a c", a=2),
                                     AX.X, ALU.add)
                op.then_inc(gate_red, 1)
                u += 1
            collect("nodes")
            dve.wait_ge(gate_red, 8)
            v.tensor_scalar(gate_z[:, :], gate_in[:, :], rowp[:, C_EB2:C_EB2 + 1], None, ALU.add).then_inc(gate_asked, 1)
            link(v.tensor_tensor(x1[:, :], nodes[:, :], x0[:, :], ALU.add))
            dve.wait_ge(gate_exp, 1)
            link(v.tensor_scalar(gate_d[:, :], gate_e[:, :], 1.0, None, ALU.add))
            v.reciprocal(gate[:, :], gate_d[:, :]).then_inc(gate_ready, 1)
            dve.wait_ge(ring_used, used("Wk"))
            v.tensor_copy(krow, ACC[1][:, 0:HALF]).then_inc(k_row, 1)
            dve.wait_ge(heads_turned, 2)
            v.tensor_copy(kt, T[1][0:DH, 0:HJ * P].rearrange("p (j n) -> p j n", j=HJ)).then_inc(k_cols, 1)
            dve.wait_ge(scores_made, 1)
            s3 = ACC[0][:, 0:HJ * N].rearrange("p (j m) -> p j m", j=HJ)
            link(v.tensor_reduce(mx[:, :], s3, AX.X, ALU.max))
            v.tensor_tensor(shifted, s3, mx[:, :].unsqueeze(2).to_broadcast([P, HJ, N]), ALU.subtract)\
                .then_inc(scores_shift, 1)
            dve.wait_ge(probs_made, 2)
            link(v.tensor_reduce(ssum[:, :], probs, AX.X, ALU.add))
            link(v.reciprocal(rsum[:, :], ssum[:, :]))
            dve.wait_ge(probs_turned, 1)
            v.tensor_copy(probs_t[:, 0:2, :], T[0][:, 0:2 * P].rearrange("p (j n) -> p j n", j=2)).then_inc(probs_a, 1)
            dve.wait_ge(attn_made, 1)
            v.tensor_tensor(row[:, :].rearrange("p (j c) -> p j c", j=HJ), ACC[1][:, 0:HALF].rearrange("p (j c) -> p j c", j=HJ),
                            rsum[:, :].unsqueeze(2).to_broadcast([P, HJ, DH]), ALU.mult).then_inc(rows_ready, 1)
            collect("attn")
            dve.wait_ge(ring_used, used("Wo"))
            link(v.tensor_tensor(x1[:, :], ACC[2][:, 0:HALF], x1[:, :], ALU.add))

            moments("f0", x1[:, :])
            rs = root("f0")
            kf, kr = POWERS.index("f0"), POWERS.index("rms")
            link(v.scalar_tensor_tensor(out=small[:, 0:1], in0=pin[:, kf:kf + 1], scalar=-EPS, in1=rs, op0=ALU.add, op1=ALU.mult))
            v.tensor_scalar(pin[:, kr:kr + 1], small[:, 0:1], rs, EPS, ALU.mult, ALU.add).then_inc(power_asked, 1)
            link(normalise(tmp[:, :], "f0", x1[:, :]))
            dve.wait_ge(row_in, 32)
            r2 = root("rms")
            link(v.scalar_tensor_tensor(out=keep[:, :], in0=tmp[:, :], scalar=r2, in1=rowp[:, C_NW:C_NW + HALF],
                                        op0=ALU.mult, op1=ALU.mult))
            sums_root("tok", keep[:, :])
            v.tensor_scalar(row[:, :], keep[:, :], root("tok"), None, ALU.mult).then_inc(rows_ready, 1)
            collect("tok")
            dve.wait_ge(logits_made, 1)
            v.tensor_reduce(small[:, 1:2], ACC[0][:, 0:N], AX.X, ALU.max, negate=True).then_inc(logits_max, 1)
            dve.wait_ge(soft_made, 1)
            link(v.reciprocal(small[:, 3:4], small[:, 2:3]))
            v.tensor_scalar(soft2[:, :, :], soft[:, :].unsqueeze(1).to_broadcast([P, 2, N]), small[:, 3:4], None, ALU.mult)\
                .then_inc(soft_ready, 1)
            dve.wait_ge(soft_turned, 1)
            v.tensor_copy(dispatch_w[N:P, N:P], T[0][N:P, N:P]).then_inc(weights_dve, 1)
            v.tensor_copy(combine_w[N:P, N:P], T[0][N:P, 0:N]).then_inc(weights_dve, 1)
            dve.wait_ge(gsum_made, 1)
            v.tensor_copy(gatesel[ROW_MSG2:ROW_MSG2 + 1, :], ACC[3][ROW_MSG2:ROW_MSG2 + 1, 0:N]).then_inc(gsum_ready, 1)
            dve.wait_ge(mixed_made, 1)
            v.tensor_copy(cols[:, 0:4, :], T[1][:, 0:4 * N].rearrange("p (i n) -> p i n", n=N)).then_inc(mixed_a, 1)
            for b in range(NB):
                dve.wait_ge(hid_turned, b + 1)
                v.tensor_tensor(hid_t[:, b * NI:(b + 1) * NI, :], T[b % 3][:, 0:HALF].rearrange("p (i n) -> p i n", n=N),
                                slotmask[:, b * NI:(b + 1) * NI, :], ALU.mult).then_inc(hid_masked, 1)
            dve.wait_ge(mix_out, 1)
            link(v.tensor_tensor(x2[:, :], ACC[1][:, 0:HALF], x1[:, :], ALU.add))

            moments("g1", x2[:, :])
            normalise(keep[:, :], "g1", x2[:, :]).then_inc(rows_ready, 1)
            collect("xn1")
            dve.wait_ge(cols_a, at(TURNS, "xn1"))
            dve.wait_ge(cols_b, at(TURNS, "xn1"))
            for t in range(TYPES):
                v.tensor_tensor(typed[:, t, :, :], cols[:, :, :], typemask[:, t, :].unsqueeze(1).to_broadcast([P, NI, N]),
                                ALU.mult).then_inc(typed_ready, 1)
            dve.wait_ge(ring_used, used(f"Wt{TYPES - 1}"))
            v.tensor_copy(hrow[:, :], ACC[0][:, 0:HALF]).then_inc(rows_ready, 1)
            collect("h")
            dve.wait_ge(ring_used, used("Wmb"))
            v.tensor_copy(pq[:, HALF:D], ACC[2][:, 0:HALF]).then_inc(pq_dve, 1)
            second = [T[1], SM, ACC[1]]
            for t in range(TE):
                dve.wait_ge(gathered, t + 1)
                if t >= 3:
                    dve.wait_ge(scattered, t - 2)
                v.tensor_scalar(msg[:, t % 3, HALF:D], second[t % 3][:, 0:HALF], gate[:, t:t + 1], 0.0, ALU.mult, ALU.max)\
                    .then_inc(msg_dve, 1)
            dve.wait_ge(scattered, TE)
            v.tensor_copy(row[:, :], ACC[0][:, 0:HALF]).then_inc(rows_ready, 1)
            collect("msg")
            dve.wait_ge(ring_used, used("Wm2"))
            v.tensor_copy(row[:, :], ACC[1][:, 0:HALF]).then_inc(rows_ready, 1)
            collect("agg1")
            dve.wait_ge(ring_used, used("Wg1"))
            v.tensor_scalar(row[:, :], ACC[2][:, 0:HALF], 0.0, None, ALU.max).then_inc(rows_ready, 1)
            collect("agg2")
            dve.wait_ge(ring_used, used("Wg2"))
            v.tensor_tensor(row[:, :], ACC[1][:, 0:HALF], hrow[:, :], ALU.add).then_inc(rows_ready, 1)
            collect("h2")
            dve.wait_ge(ring_used, used("Wout"))
            link(v.tensor_tensor(tmp[:, :], ACC[2][:, 0:HALF], keep[:, :], ALU.add))
            moments("go", tmp[:, :])
            link(v.tensor_tensor(x2[:, :], x2[:, :], rowp[:, C_LNB:C_LNB + HALF], ALU.add))
            link(normalise(hrow[:, :], "go", tmp[:, :]))
            link(v.tensor_tensor(tmp[:, :], hrow[:, :], rowp[:, C_LNG:C_LNG + HALF], ALU.mult))
            link(v.tensor_tensor(x3[:, :], tmp[:, :], x2[:, :], ALU.add))

            moments("f1", x3[:, :])
            normalise(row[:, :], "f1", x3[:, :]).then_inc(rows_ready, 1)
            collect("x3")
            dve.wait_ge(enc_made, 1)
            v.tensor_scalar(enc_t[:, :, :], ACC[3][0:R, 0:N].unsqueeze(1).to_broadcast([R, 2, N]),
                            colp[0:R, C_ENCB:C_ENCB + 1], None, ALU.add).then_inc(enc_ready, 1)
            dve.wait_ge(route_made, 1)
            link(v.tensor_tensor(lg[:, :], T[2][:, 0:X], rowp[:, C_SWB:C_SWB + X], ALU.add))
            v.tensor_reduce(small[:, 4:5], lg[:, :], AX.X, ALU.max, negate=True).then_inc(route_max, 1)
            dve.wait_ge(route_exp, 1)
            link(v.reciprocal(small[:, 6:7], small[:, 5:6]))
            link(v.tensor_scalar(pr[:, :], pe_[:, :], small[:, 6:7], None, ALU.mult))
            link(v.tensor_reduce(small[:, 7:8], pr[:, :], AX.X, ALU.max))
            link(v.scalar_tensor_tensor(out=cand[:, :], in0=pr[:, :], scalar=small[:, 7:8], in1=ramp[:, :],
                                        op0=ALU.is_equal, op1=ALU.mult))
            link(v.tensor_reduce(mx[:, 0:1], cand[:, :], AX.X, ALU.max))
            link(v.tensor_scalar(route[:, :], cand[:, :], mx[:, 0:1], small[:, 7:8], ALU.is_equal, ALU.mult))
            v.tensor_copy(route_pad[:, ROW_FFN2:ROW_FFN2 + X], route[0:N, :]).then_inc(route_ready, 1)
            dve.wait_ge(act_link, 1)
            for h in range(2):
                rows = slice(h * N, (h + 1) * N)
                last = v.tensor_tensor(tmp[rows, 0:4 * R].rearrange("p (e r) -> p e r", e=4),
                                       hrow[rows, 0:4 * R].rearrange("p (e r) -> p e r", e=4),
                                       route[rows, 4 * h:4 * h + 4].unsqueeze(2).to_broadcast([N, 4, R]), ALU.mult)
            last.then_inc(gelu_made, 1)
            dve.wait_ge(route_turned, 1)
            v.tensor_copy(routesel[:, :], ACC[3][:, 0:N]).then_inc(routesel_ready, 1)
            dve.wait_ge(exp_turned, 1)
            v.tensor_copy(cols[:, 0:4, :], T[0][:, 0:4 * N].rearrange("p (i n) -> p i n", n=N)).then_inc(exp_cols, 1)
            dve.wait_ge(ring_used, used("w2"))
            v.tensor_tensor(row[:, :], ACC[1][:, 0:HALF], x3[:, :], ALU.add).then_inc(final_ready, 1)

        @block.scalar
        def _(act):
            a = nc.scalar

            def copy(dst, src):
                return a.activation(dst, src, ACT.Copy)

            def collect(name, dst=None):
                act.wait_ge(turned_b, at(TURNS, name))
                copy(cols[:, 4:6, :] if dst is None else dst,
                     T[1][:, 0:2 * N].rearrange("p (i n) -> p i n", n=N)).then_inc(cols_b, 1)

            act.dma_start(idx[:, :], ins["idx"]).then_inc(idx_in, 16)
            act.dma_start(bias[:, :], ins["bias"]).then_inc(bias_in, 16)
            act.dma_start(slots[:, :], ins["slots"]).then_inc(slots_in, 16)
            act.dma_start(colp[:, :], ins["colp"]).then_inc(col_in, 16)
            act.dma_start(types[:, :], ins["types"].to_broadcast([P, N])).then_inc(type_in, 16)
            for h in range(2):
                rows = slice(h * N, (h + 1) * N)
                act.dma_start(pair[rows, :].bitcast(i32), ins["ends"][h:h + 1, :].to_broadcast([N, E])).then_inc(pair_in, 16)
                act.dma_start(rowp[rows, :], ins["rowp"][h:h + 1, :].to_broadcast([N, ROW_PACK])).then_inc(row_in, 16)
            act.dma_start(ea[:, :, :], ins["ea"].rearrange("p (g e) -> p g e", g=4)).then_inc(ea_in, 16)
            act.dma_start(ew1[:, :], ins["ew1"]).then_inc(ew1_in, 16)
            act.dma_start(encw[:, :, :], ins["encw"].rearrange("p (i r) -> p i r", i=NI)).then_inc(encw_in, 16)
            act.dma_start(sww[:, :], ins["sww"]).then_inc(sww_in, 16)
            collect("x0")
            act.wait_ge(ring_used, used("ef"))
            copy(tmp[:, 0:DE], ACC[1][:, 0:DE]).then_inc(edges_kept, 1)
            act.wait_ge(edges_made, 1)
            copy(hrow[:, 0:2 * N], ACC[2][:, 0:2 * N]).then_inc(edges_kept, 1)
            act.wait_ge(ring_used, used("We", 0))
            copy(tmp[:, :], ACC[1][:, 0:HALF]).then_inc(rows_ready, 1)
            e2 = edges2[:, :, :, :].rearrange("p j (h q) n -> p j h q n", q=2)[:, :, :, 1, :]
            act.wait_ge(consts_made, at(CONSTS, "fills"))
            act.wait_ge(turned_b, at(TURNS, "edges"))
            copy(e2[:, 2], T[1][:, 0:2 * N].rearrange("p (h n) -> p h n", h=2)).then_inc(cols_b, 1)
            collect("slots", slots_t[:, 4:6, :])
            act.wait_ge(col_in, 16)
            tiles = [0]

            def gate_hidden(count):
                for _ in range(count):
                    u = tiles[0]
                    act.wait_ge(gate_made, u + 1)
                    if u >= 2:
                        act.wait_ge(gate_mult, u - 1)
                    a.activation(ehid[:, u % 2, :], ACC[2 + u % 2][:, 0:2 * H4], ACT.Relu).then_inc(gate_relu, 1)
                    tiles[0] += 1

            for l in range(L):
                gate_hidden(GATES[l][0])
                act.wait_ge(turned_a, at(TURNS, f"l{l}"))
                for i in range(4):
                    op = a.activation(cols[:, i, :], T[0][:, i * N:(i + 1) * N], ACT.Relu,
                                      scale=colp[:, C_G + l * NI + i:C_G + l * NI + i + 1],
                                      bias=colp[:, C_B + l * NI + i:C_B + l * NI + i + 1])
                op.then_inc(cols_a, 1)
                gate_hidden(GATES[l][1])
            collect("nodes")
            act.wait_ge(gate_asked, 1)
            a.activation(gate_e[:, :], gate_z[:, :], ACT.Exp, scale=-1.0).then_inc(gate_exp, 1)
            act.wait_ge(ring_used, used("Wq"))
            copy(qrow, ACC[0][:, 0:HALF]).then_inc(q_row, 1)
            act.wait_ge(heads_turned, 1)
            copy(qt, T[0][0:DH, 0:HJ * P].rearrange("p (j n) -> p j n", j=HJ)).then_inc(q_cols, 1)
            act.wait_ge(ring_used, used("Wv"))
            copy(vrow, ACC[2][:, 0:HALF]).then_inc(v_row, 1)
            act.wait_ge(scores_shift, 1)
            act.wait_ge(consts_made, at(CONSTS, "fills"))
            for h in range(2):
                rows = slice(h * N, (h + 1) * N)
                a.activation(probs[rows, :, h * N:(h + 1) * N], shifted[rows, :, :], ACT.Exp, scale=DH ** -0.5)\
                    .then_inc(probs_made, 1)
            act.wait_ge(probs_turned, 2)
            copy(probs_t[:, 2:4, :], T[1][:, 0:2 * P].rearrange("p (j n) -> p j n", j=2)).then_inc(probs_b, 1)
            collect("attn")
            collect("tok")
            act.wait_ge(logits_max, 1)
            a.activation(soft[:, :], ACC[0][:, 0:N], ACT.Exp, bias=small[:, 1:2], accum_out=small[:, 2:3]).then_inc(soft_made, 1)
            act.wait_ge(soft_turned, 1)
            copy(dispatch_w[0:N, 0:N], T[0][0:N, N:P]).then_inc(weights_act, 1)
            copy(combine_w[0:N, 0:N], T[0][0:N, 0:N]).then_inc(weights_act, 1)
            act.wait_ge(mixed_made, 1)
            copy(cols[:, 4:6, :], T[2][:, 0:2 * N].rearrange("p (i n) -> p i n", n=N)).then_inc(mixed_b, 1)
            for b in range(NB):
                act.wait_ge(ring_used, used(f"fc1{b}"))
                a.activation(hid[:, b, :], ACC[b][:, 0:HALF], ACT.Gelu).then_inc(hid_made, 1)
            act.wait_ge(ring_used, used(f"fc2{NB - 1}"))
            copy(tmp[:, :], ACC[0][:, 0:HALF]).then_inc(y_ready, 1)
            collect("xn1")
            collect("h")
            act.wait_ge(ring_used, used("Wmb"))
            copy(pq[:, 0:HALF], ACC[1][:, 0:HALF]).then_inc(pq_act, 1)
            first = [T[0], T[2], ACC[3]]
            act.wait_ge(gate_ready, 1)
            for t in range(TE):
                act.wait_ge(gathered, t + 1)
                if t >= 3:
                    act.wait_ge(scattered, t - 2)
                a.activation(msg[:, t % 3, 0:HALF], first[t % 3][:, 0:HALF], ACT.Relu, scale=gate[:, t:t + 1]).then_inc(msg_act, 1)
            for name in ("msg", "agg1", "agg2", "h2", "x3"):
                collect(name)
            act.wait_ge(route_max, 1)
            a.activation(pe_[:, :], lg[:, :], ACT.Exp, bias=small[:, 4:5], accum_out=small[:, 5:6]).then_inc(route_exp, 1)
            act.wait_ge(ring_used, used("w1"))
            a.activation(hrow[:, 0:4 * R], ACC[0][:, 0:4 * R], ACT.Gelu).then_inc(act_link, 1)


def _weight(w, groups=1):
    import numpy as np
    rows, cols = w.shape
    n = rows // P
    half = n // 2
    order = [half * (i % 2) + i // 2 for i in range(n)]
    return np.ascontiguousarray(w.reshape(n, P, cols)[order].transpose(1, 0, 2)).reshape(P, n * cols)


def _halves(x):
    import numpy as np
    return np.ascontiguousarray(x.reshape(N, 2, HALF).transpose(1, 0, 2)).reshape(P, HALF)


def kernel(**inputs):
    import numpy as np
    import concourse.bacc as bacc
    from concourse.bass_utils import run_bass_kernel_spmd

    g = {k: np.asarray(v) for k, v in inputs.items()}
    a = {"x": _halves(g["x"]), "slots": _halves(g["L0_ffn_slots"])}
    a["idx"] = np.concatenate([g["src"].reshape(P, TE), g["dst"].reshape(P, TE)], axis=1)
    a["ends"] = np.stack([g["src"].reshape(P, TE).T.reshape(E), g["dst"].reshape(P, TE).T.reshape(E)])
    a["types"] = g["node_type_6"].reshape(1, N)
    a["ef"] = g["edge_attr_256"].reshape(P, TE * DE)
    a["ea"] = np.ascontiguousarray(g["edge_attr_32"].reshape(P, 4, 4, DA).transpose(2, 3, 1, 0)).reshape(P, 4 * P)
    ew1 = np.zeros((4, DA, 4, H4), np.float32)
    for t in range(4):
        ew1[t, :, t, :] = g["L1_gnn_edge_W1"]
    a["ew1"] = ew1.reshape(P, 4 * H4)
    a["We"] = np.ascontiguousarray(g["L0_gnn_We"].T.reshape(2, P, D).transpose(1, 0, 2)).reshape(P, 2 * D)
    a["Wn"] = _weight(g["L0_gnn_Wn"].T)
    for l in range(L):
        w = g["L0_gnn_W1"][l].T
        a[f"W1a{l}"], a[f"W1b{l}"], a[f"W2{l}"] = _weight(w[:D]), _weight(w[D:]), _weight(g["L0_gnn_W2"][l].T)
    for k, c in enumerate("qkv"):
        a[f"W{c}"] = _weight(g["L0_gnn_Wqkv"][k * D:(k + 1) * D].T)
    a["Wo"] = _weight(g["L0_gnn_Wo"].T)
    fc1 = g["L0_ffn_fc1_weight"].transpose(1, 0, 2).reshape(D, N * F)
    fc2 = g["L0_ffn_fc2_weight"].reshape(N * F, D)
    for b in range(NB):
        a[f"fc1{b}"] = _weight(fc1[:, b * D:(b + 1) * D])
        a[f"fc2{b}"] = _weight(fc2[b * D:(b + 1) * D])
    for t in range(TYPES):
        a[f"Wt{t}"] = _weight(g["L1_gnn_W_type"][t])
    a["Wma"], a["Wmb"] = _weight(g["L1_gnn_msg_W1"][:D]), _weight(g["L1_gnn_msg_W1"][D:])
    for k, n in (("Wm2", "msg_W2"), ("Wg1", "agg_W1"), ("Wg2", "agg_W2"), ("Wout", "out_W")):
        a[k] = _weight(g["L1_gnn_" + n])
    a["w1"] = _weight(g["L1_ffn_w1"].transpose(1, 0, 2).reshape(D, X * R))
    a["w2"] = _weight(g["L1_ffn_w2"].reshape(X * R, D))
    a["encw"] = _weight(g["L1_ffn_enc_w"])
    a["sww"] = g["L1_ffn_sw_w"]

    bias = np.zeros((P, D), np.float32)
    bias[ROW_BE], bias[ROW_BN], bias[ROW_BO] = g["L0_gnn_be"], g["L0_gnn_bn"], g["L0_gnn_bo"]
    bias[ROW_B1:ROW_B1 + L], bias[ROW_B2:ROW_B2 + L] = g["L0_gnn_b1"], g["L0_gnn_b2"]
    bias[ROW_BQKV:ROW_BQKV + 3] = g["L0_gnn_bqkv"].reshape(3, D)
    bias[ROW_FC1:ROW_FC1 + NB] = g["L0_ffn_fc1_bias"].reshape(NB, D)
    bias[ROW_TYPE:ROW_TYPE + TYPES] = g["L1_gnn_b_type"]
    bias[ROW_MSG1], bias[ROW_MSG2] = g["L1_gnn_msg_b1"], g["L1_gnn_msg_b2"]
    bias[ROW_AGG1], bias[ROW_AGG2], bias[ROW_OUT] = g["L1_gnn_agg_b1"], g["L1_gnn_agg_b2"], g["L1_gnn_out_b"]
    bias[ROW_FFN1, 0:X * R] = g["L1_ffn_b1"].reshape(X * R)
    bias[ROW_EDGE1, 0:H4] = g["L1_gnn_edge_b1"]
    bias[ROW_EDGE1, H4:2 * H4] = g["L1_gnn_edge_b1"]
    bias[ROW_FFN2:ROW_FFN2 + X] = g["L1_ffn_b2"]
    bias[ROW_FC2:ROW_FC2 + N] = g["L0_ffn_fc2_bias"]
    a["bias"] = bias

    rowp = np.zeros((2, ROW_PACK), np.float32)
    rowp[:, C_NW:C_NW + HALF] = g["L0_ffn_norm_weight"].reshape(2, HALF)
    rowp[:, C_LNG:C_LNG + HALF] = g["L1_gnn_ln_g"].reshape(2, HALF)
    rowp[:, C_LNB:C_LNB + HALF] = g["L1_gnn_ln_b"].reshape(2, HALF)
    rowp[:, C_EW2:C_EW2 + H4] = g["L1_gnn_edge_W2"].reshape(1, H4)
    rowp[:, C_EW2 + H4:C_EW2 + 2 * H4] = g["L1_gnn_edge_W2"].reshape(1, H4)
    rowp[:, C_SWB:C_SWB + X] = g["L1_ffn_sw_b"].reshape(1, X)
    rowp[:, C_EB2:C_EB2 + 1] = g["L1_gnn_edge_b2"].reshape(1, 1)
    a["rowp"] = rowp

    colp = np.zeros((P, COL_PACK), np.float32)
    for l in range(L):
        for i in range(NI):
            c = chunk(i)
            colp[:, C_G + l * NI + i] = g["L0_gnn_ln_g"][l, c * P:(c + 1) * P]
            colp[:, C_B + l * NI + i] = g["L0_gnn_ln_b"][l, c * P:(c + 1) * P]
    colp[0:R, C_ENCB] = g["L1_ffn_enc_b"]
    colp[0:N, C_SCALE] = g["L0_ffn_scale"]
    colp[N:P, C_SCALE] = g["L0_ffn_scale"]
    a["colp"] = colp

    nc = bacc.Bacc("TRN2", target_bir_lowering=False, num_devices=1)
    arrays, ins = {}, {}
    for name, v in a.items():
        v = np.ascontiguousarray(v)
        arrays[f"in_{name}"] = v
        ins[name] = nc.dram_tensor(f"in_{name}", v.shape, mybir.dt.from_np(v.dtype), kind="ExternalInput").ap()
    out = nc.dram_tensor("out", (P, HALF), mybir.dt.float32, kind="ExternalOutput").ap()
    build(nc, ins, out)
    r = run_bass_kernel_spmd(nc, [arrays], core_ids=[0])
    got = np.asarray(r.results[0]["out"])
    return np.ascontiguousarray(got.reshape(2, N, HALF).transpose(1, 0, 2)).reshape(N, D)
```

```python
import concourse.bass as bass
from concourse import mybir
from contextlib import ExitStack

N = 64
E = 2048
D = 768
HALF = D // 2
P = 128
NI = D // P
NJ = NI // 2
L = 3
DE = 256
DA = 32
H4 = D // 4
HEADS = 8
DH = D // HEADS
HJ = HEADS // 2
F = 48
TYPES = 6
R = 64
X = 8
TE = E // P
NB = N * F // D
SB = N // 32
Q = D // 4
SLOT = 3 * D
RING = 12
EPS = 1e-5

ROW_BE, ROW_BN, ROW_B1, ROW_B2, ROW_BQKV, ROW_BO, ROW_FC1 = 0, 1, 2, 5, 8, 11, 12
ROW_TYPE, ROW_MSG1, ROW_AGG1, ROW_AGG2, ROW_OUT, ROW_FFN1, ROW_EDGE1 = 16, 22, 23, 24, 25, 26, 27
ROW_NORM, ROW_LNG, ROW_LNB, ROW_EDGE2 = 28, 29, 30, 31
ROW_MSG2, ROW_FFN2, ROW_FC2 = 32, 33, 64

C_G, C_B, C_ENCB, C_SCALE = 0, L * NI, 2 * L * NI, 2 * L * NI + 1
COL_PACK = 2 * L * NI + 2


def chunk(i):
    return 3 * (i % 2) + i // 2


def load_order():
    order = [("ef", 0), ("ef", 1), ("We", 0), ("Wn", 0), ("Wn", 1)]
    for l in range(L):
        order += [(f"W1a{l}", 0), (f"W1a{l}", 1), (f"W1b{l}", 0), (f"W1b{l}", 1), (f"W2{l}", 0), (f"W2{l}", 1)]
    order += [(f"W{c}", k) for c in "qkvo" for k in range(2)]
    order += [(f"fc1{b}", k) for b in range(NB) for k in range(2)]
    order += [(f"fc2{b}", k) for b in range(NB) for k in range(2)]
    order += [(f"Wt{t}", k) for t in range(TYPES) for k in range(2)]
    order += [("Wma", 0), ("Wmb", 0), ("Wma", 1), ("Wmb", 1)]
    order += [(w, k) for w in ("Wm2", "Wg1", "Wg2", "Wout", "w1", "w2") for k in range(2)]
    return order


def part_width(name):
    return {"ef": TE // 2 * DE, "We": 2 * D, "w1": 3 * X * R, "w2": 2 * D}.get(name, SLOT)


LOADS = load_order()
LOAD = {part: k for k, part in enumerate(LOADS)}

COMBINES = ["x0", "slots", "l0", "l1", "l2", "f0", "tok", "g1", "go", "f1"]
POWERS = ["x0", "slots", "l0", "l1", "l2", "f0", "tok", "g1", "go", "f1"]
TURNS = ["x0", "edges", "slots", "l0", "l1", "l2", "nodes", "attn", "tok", "xn1", "h", "msg", "agg1", "agg2", "h2", "x3"]
GATES = [2, 4, 6, 8]
CONSTS = ["ident", "mix", "iota", "blocks", "small", "pair", "fills", "slotmask", "probs"]


def build(nc, ins, out):
    fp32, bf16, i32, f32r = mybir.dt.float32, mybir.dt.bfloat16, mybir.dt.int32, mybir.dt.float32r
    ALU, ACT, AX = mybir.AluOpType, mybir.ActivationFunctionType, mybir.AxisListType
    ctx = ExitStack()
    with ctx:
        def sb(name, shape, dt=fp32):
            return ctx.enter_context(nc.sbuf_tensor(name, shape, dt))

        def bank(name):
            return ctx.enter_context(nc.psum_tensor(name, [P, 512], fp32))

        def sem(name):
            return ctx.enter_context(nc.semaphore(name))

        ring = sb("ring", [P, RING, SLOT])
        bias = sb("bias", [P, D])
        rows4 = sb("rows4", [P, 4, HALF])
        tail = sb("tail", [P, X + 1])
        colp = sb("colp", [P, COL_PACK])
        x0 = sb("x0", [P, HALF])
        x1 = sb("x1", [P, HALF])
        x2 = sb("x2", [P, HALF])
        x3 = sb("x3", [P, HALF])
        nodes = sb("nodes", [P, HALF])
        row = sb("row", [P, HALF])
        keep = sb("keep", [P, HALF])
        hrow = sb("hrow", [P, HALF])
        tmp = sb("tmp", [P, HALF])
        cols = sb("cols", [P, NI, N])
        slots = sb("slots", [P, HALF])
        slots_t = sb("slots_t", [P, NI, N])
        edges2 = sb("edges2", [P, NJ, 4, N])
        comb = sb("comb", [P, NJ, 4, N])
        spread = sb("spread", [P, 4, N])
        idx = sb("idx", [P, 2 * TE], i32)
        idxf = sb("idxf", [P, 2 * TE])
        types = sb("types", [P, N], i32)
        typesf = sb("typesf", [P, N])
        typemask = sb("typemask", [P, TYPES, N])
        typesel = sb("typesel", [P, N])
        irow_i = sb("irow_i", [P, N], i32)
        irow = sb("irow", [P, N])
        icol_i = sb("icol_i", [P, 1], i32)
        icol = sb("icol", [P, 1])
        ramp_i = sb("ramp_i", [P, X], i32)
        ramp = sb("ramp", [P, X])
        pair = sb("pair", [P, E], f32r)
        pq = sb("pq", [P, 2, D], f32r)
        ident_b = sb("ident_b", [P, P], bf16)
        to_dst = sb("to_dst", [P, TE, N])
        ones_b = sb("ones_b", [P, 1], bf16)
        degsel = sb("degsel", [P, N])
        gatesel = sb("gatesel", [P, N])
        routesel = sb("routesel", [P, N])
        ident = sb("ident", [P, P])
        mean2 = sb("mean2", [P, P])
        diff2 = sb("diff2", [P, P])
        pairup = sb("pairup", [P, N])
        eps3 = sb("eps3", [P, 3])
        nhalf = sb("nhalf", [P, 1])
        slotmask = sb("slotmask", [P, NJ, P], bf16)
        scratch = sb("scratch", [P, 1])
        stat6 = sb("stat6", [P, 6])
        mv = sb("mv", [P, len(COMBINES), 2])
        sc = sb("sc", [P, len(COMBINES), 4])
        pin = sb("pin", [P, len(POWERS)])
        pout = sb("pout", [P, len(POWERS)])
        small = sb("small", [P, 8])
        ea = sb("ea", [P, 4, P])
        ew1 = sb("ew1", [P, 4 * H4])
        gate_in = sb("gate_in", [P, TE])
        gate_z = sb("gate_z", [P, TE])
        gate_e = sb("gate_e", [P, TE])
        gate_d = sb("gate_d", [P, TE])
        gate = sb("gate", [P, TE])
        encw = sb("encw", [P, NI, R])
        sww = sb("sww", [R, X])
        big = sb("big", [P, 2048 + 4 * HALF])
        ends_b = big[:, 0:1024].bitcast(bf16).rearrange("p (t a n) -> p t a n", t=TE, a=2)
        both_b = big[:, 1024:2048].bitcast(bf16).rearrange("p (t a n) -> p t a n", t=TE, a=2)
        ehid = big[:, 2048:2048 + 4 * H4].rearrange("p (k c) -> p k c", k=2)
        eprod = big[:, 2048 + 4 * H4:2048 + 8 * H4].rearrange("p (k c) -> p k c", k=2)
        qt = big[0:DH, 0:HJ * P].rearrange("p (j n) -> p j n", j=HJ)
        kt = big[0:DH, HJ * P:2 * HJ * P].rearrange("p (j n) -> p j n", j=HJ)
        qrow = big[:, 1024:1024 + HALF]
        krow = big[:, 1408:1408 + HALF]
        vrow = big[:, 1792:1792 + HALF]
        shifted = big[:, 2176:2432].rearrange("p (j m) -> p j m", j=HJ)
        probs = big[:, 2432:2944].rearrange("p (j m) -> p j m", j=HJ)
        probs_t = big[:, 2944:3456].rearrange("p (j m) -> p j m", j=HJ)
        hid = big[:, 0:SB * HALF].rearrange("p (b c) -> p b c", b=SB)
        hid_t = big[:, SB * HALF:2 * SB * HALF].rearrange("p (b j n) -> p b j n", b=SB, j=NJ)
        mixed = big[:, 2 * SB * HALF:2 * SB * HALF + SB * Q].rearrange("p (b c) -> p b c", b=SB)
        typed = big[:, 0:TYPES * HALF].rearrange("p (t i n) -> p t i n", t=TYPES, i=NI)
        msg = big[:, 0:3 * D].rearrange("p (k c) -> p k c", k=3)
        combine_w = sb("combine_w", [P, 2, SB, P])
        dispatch_w = sb("dispatch_w", [P, P])
        soft = sb("soft", [P, N])
        soft2 = sb("soft2", [P, 1 + SB, P])
        mx = sb("mx", [P, HJ])
        ssum = sb("ssum", [P, HJ])
        rsum = sb("rsum", [P, HJ])
        enc_t = sb("enc_t", [R, 2, N])
        lg = sb("lg", [P, X])
        pe_ = sb("pe_", [P, X])
        pr = sb("pr", [P, X])
        cand = sb("cand", [P, X])
        route = sb("route", [P, X])
        route_pad = sb("route_pad", [N, P])

        T = [bank(f"T{k}") for k in range(3)]
        ACC = [bank(f"ACC{k}") for k in range(4)]
        SM = bank("SM")

        arrived = [sem(f"arrived{k}") for k in range(RING)]
        ring_used = sem("ring_used")
        x_in, idx_in, type_in, bias_in, col_in, tail_in = (sem(n) for n in ("x_in", "idx_in", "type_in", "bias_in", "col_in", "tail_in"))
        ew1_clear = sem("ew1_clear")
        rows_made, rows_kept = sem("rows_made"), sem("rows_kept")
        slots_in, ea_in, ew1_in, encw_in, sww_in = (sem(n) for n in ("slots_in", "ea_in", "ew1_in", "encw_in", "sww_in"))
        out_done = sem("out_done")
        consts_made, pool_link = sem("consts_made"), sem("pool_link")
        dve_link, act_link = sem("dve_link"), sem("act_link")
        stats_ready, combined, power_asked, power_done = sem("stats_ready"), sem("combined"), sem("power_asked"), sem("power_done")
        rows_ready, turned_a, turned_b, cols_a, cols_b = sem("rows_ready"), sem("turned_a"), sem("turned_b"), sem("cols_a"), sem("cols_b")
        onehots, onehot_copy, sums_made, spread_ready = sem("onehots"), sem("onehot_copy"), sem("sums_made"), sem("spread_ready")
        edges_made, edges_kept = sem("edges_made"), sem("edges_kept")
        nodes_ready, comb_made, comb_ready = sem("nodes_ready"), sem("comb_made"), sem("comb_ready")
        gate_made, gate_relu, gate_mult, gate_red = sem("gate_made"), sem("gate_relu"), sem("gate_mult"), sem("gate_red")
        gate_asked, gate_exp, gate_ready, gsum_made, gsum_ready = sem("gate_asked"), sem("gate_exp"), sem("gate_ready"), sem("gsum_made"), sem("gsum_ready")
        q_row, k_row, v_row, heads_turned, q_cols, k_cols = (sem(n) for n in ("q_row", "k_row", "v_row", "heads_turned", "q_cols", "k_cols"))
        scores_made, scores_shift, probs_made, probs_turned = sem("scores_made"), sem("scores_shift"), sem("probs_made"), sem("probs_turned")
        probs_a, probs_b, attn_made = sem("probs_a"), sem("probs_b"), sem("attn_made")
        logits_made, logits_max, soft_made, soft_ready, soft_turned = sem("logits_made"), sem("logits_max"), sem("soft_made"), sem("soft_ready"), sem("soft_turned")
        weights_act, weights_dve, mixed_made, mixed_a, mixed_b = sem("weights_act"), sem("weights_dve"), sem("mixed_made"), sem("mixed_a"), sem("mixed_b")
        hid_made, hid_turned, hid_masked, y_ready, mix_out = sem("hid_made"), sem("hid_turned"), sem("hid_masked"), sem("y_ready"), sem("mix_out")
        typed_ready, typesel_ready, pq_dve = sem("typed_ready"), sem("typesel_ready"), sem("pq_dve")
        pair_turned, pq_round = sem("pair_turned"), sem("pq_round")
        pair_ready, gathered, msg_act, msg_dve, scattered = sem("pair_ready"), sem("gathered"), sem("msg_act"), sem("msg_dve"), sem("scattered")
        enc_made, enc_ready, route_made, route_max, route_exp = sem("enc_made"), sem("enc_ready"), sem("route_made"), sem("route_max"), sem("route_exp")
        route_ready, route_turned, routesel_ready = sem("route_ready"), sem("route_turned"), sem("routesel_ready")
        gelu_made, exp_turned, exp_cols, final_ready = sem("gelu_made"), sem("exp_turned"), sem("exp_cols"), sem("final_ready")

        def used(name, part=1):
            return LOAD[name, part] + 1

        def slot(name, part):
            k = LOAD[name, part]
            return ring[:, k % RING, 0:part_width(name)]

        def at(names, name):
            return names.index(name) + 1

        def halves(ap, n=HALF):
            return [(h, ap[h * N:(h + 1) * N, 0:n]) for h in range(2)]

        block = ctx.enter_context(nc.Block())

        @block.sync
        def _(sp):
            sp.dma_start(x0[:, :], ins["x"]).then_inc(x_in, 16)
            for k, (name, part) in enumerate(LOADS):
                if k >= RING:
                    sp.wait_ge(ring_used, k - RING + 1)
                src = ins[name]
                w = part_width(name)
                sp.dma_start(slot(name, part), src[:, part * w:(part + 1) * w]).then_inc(arrived[k % RING], 16)
            sp.wait_ge(final_ready, 1)
            sp.dma_start(out, row[:, :]).then_inc(out_done, 16)
            sp.wait_ge(out_done, 16)

        @block.gpsimd
        def _(pool):
            links = [0]

            def link(op):
                links[0] += 1
                op.then_inc(pool_link, 1)
                pool.wait_ge(pool_link, links[0])

            made = [0]

            def done(op):
                made[0] += 1
                op.then_inc(consts_made, 1)
                pool.wait_ge(consts_made, made[0])

            def diagonal(ap, base, pattern, fill):
                return nc.gpsimd.affine_select(out=ap, in_=ap, pattern=pattern, compare_op=ALU.not_equal, fill=fill,
                                               base=base, channel_multiplier=1)

            link(nc.gpsimd.memset(ident[:, :], 0.0))
            done(diagonal(ident[:, :], 0, [[-1, P]], 1.0))
            link(nc.gpsimd.memset(mean2[:, :], 0.0))
            link(nc.gpsimd.memset(diff2[:, :], 0.0))
            link(nc.gpsimd.memset(eps3[:, :], 0.0))
            link(nc.gpsimd.memset(eps3[:, 1:2], EPS))
            link(nc.gpsimd.memset(nhalf[:, :], -0.5))
            for h in range(2):
                lo = slice(h * N, (h + 1) * N)
                link(diagonal(mean2[lo, :].rearrange("p (a n) -> p a n", a=2), 0, [[0, 2], [-1, N]], 0.5))
                last = diagonal(diff2[lo, :].rearrange("p (a n) -> p a n", a=2), 0, [[0, 2], [-1, N]], 0.5 - h)
                (done if h else link)(last)
            link(nc.gpsimd.iota(irow_i[:, :], pattern=[[1, N]], base=0, channel_multiplier=0))
            link(nc.gpsimd.iota(icol_i[:, :], pattern=[[0, 1]], base=-ROW_TYPE, channel_multiplier=1))
            done(nc.gpsimd.iota(ramp_i[:, :], pattern=[[-1, X]], base=X, channel_multiplier=0))

            def power(name):
                k = POWERS.index(name)
                pool.wait_ge(power_asked, k + 1)
                nc.gpsimd.tensor_tensor(pout[:, k:k + 1], pin[:, k:k + 1], nhalf[:, :], ALU.pow).then_inc(power_done, 1)

            power("x0")
            link(nc.gpsimd.memset(spread[:, :, :], 0.0))
            link(diagonal(spread[0:N, 0, :], 0, [[-1, N]], 1.0))
            done(diagonal(spread[N:P, 2, :], 0, [[-1, N]], 1.0))
            link(nc.gpsimd.memset(ones_b[:, :], 1.0))
            link(nc.gpsimd.memset(degsel[:, :], 0.0))
            done(nc.gpsimd.memset(gatesel[:, :], 0.0))
            link(nc.gpsimd.memset(pairup[:, :], 0.0))
            link(diagonal(pairup[0:N, :], 0, [[-1, N]], 1.0))
            done(diagonal(pairup[N:P, :], 0, [[-1, N]], 1.0))
            done(nc.gpsimd.memset(edges2[:, :, :, :], 0.0))
            power("slots")
            link(nc.gpsimd.memset(combine_w[:, :, :, :], 0.0))
            link(nc.gpsimd.memset(dispatch_w[:, :], 0.0))
            link(nc.gpsimd.memset(route_pad[:, :], 0.0))
            link(nc.gpsimd.memset(slotmask[:, :, :], 1.0))
            mask4 = slotmask[:, :, :].rearrange("p j (g s) -> p j g s", g=4)
            link(nc.gpsimd.affine_select(out=mask4, in_=mask4, pattern=[[P, NJ], [HALF, 4], [-F, 32]],
                                         compare_op=ALU.is_ge, fill=0.0, base=0, channel_multiplier=1))
            done(nc.gpsimd.affine_select(out=mask4, in_=mask4, pattern=[[-P, NJ], [-HALF, 4], [F, 32]],
                                         compare_op=ALU.is_ge, fill=0.0, base=F - 1, channel_multiplier=-1))

            def gate_products(first, last):
                for u in range(first, last):
                    pool.wait_ge(gate_relu, u + 1)
                    if u >= 2:
                        pool.wait_ge(gate_red, u - 1)
                    nc.gpsimd.tensor_tensor(eprod[:, u % 2, :], ehid[:, u % 2, :], rows4[:, 3, :], ALU.mult).then_inc(gate_mult, 1)

            pool.wait_ge(rows_kept, 1)
            gate_products(0, GATES[0])
            for l in range(L):
                power(f"l{l}")
                gate_products(GATES[l], GATES[l + 1])
            pool.wait_ge(gate_red, TE // 2)
            done(nc.gpsimd.memset(probs, 0.0))
            for name in POWERS[POWERS.index("f0"):]:
                power(name)

        @block.tensor
        def _(pe):
            def mm(o, lhsT, rhs, start=True, stop=True):
                return nc.tensor.matmul(o, lhsT, rhs, start=start, stop=stop)

            def ready(name, part):
                k = LOAD[name, part]
                pe.wait_ge(arrived[k % RING], 16 * (k // RING + 1))

            def combine(name, sums=False):
                k = COMBINES.index(name)
                pe.wait_ge(stats_ready, k + 1)
                last = mm(SM[:, 0:2], mean2[:, :], mv[:, k, :])
                if not sums:
                    last = mm(SM[:, 2:3], diff2[:, :], mv[:, k, 0:1])
                last.then_inc(combined, 1)

            def turn(name, src):
                pe.wait_ge(rows_ready, at(TURNS, name))
                for j in range(NJ):
                    o = T[j // 2][:, (j % 2) * P:(j % 2 + 1) * P]
                    last = nc.tensor.transpose(o, src[:, j * P:(j + 1) * P], ident[:, :])
                    if j == 1:
                        last.then_inc(turned_a, 1)
                last.then_inc(turned_b, 1)

            def pick(k, n=N):
                return ident[:, k:k + 1].to_broadcast([P, n])

            def add_bias(acc, k, stat=None, width=HALF, end=False):
                for h in range(2):
                    last = mm(acc[h * N:(h + 1) * N, 0:width], pick(k) if stat is None else stat,
                              bias[:, h * width:(h + 1) * width], True, end)
                return last

            def product(acc, stationary, name, turn_name=None, first=False, end=True, width=HALF, per=3, n=NI):
                for i in range(n):
                    if turn_name and i == 0:
                        pe.wait_ge(cols_a, at(TURNS, turn_name))
                    if turn_name and i == 4:
                        pe.wait_ge(cols_b, at(TURNS, turn_name))
                    if i % per == 0:
                        ready(name, i // per)
                    w = slot(name, i // per).rearrange("p (i c) -> p i c", i=per)
                    for h in range(2):
                        last = mm(acc[h * N:(h + 1) * N, 0:width], stationary(i),
                                  w[:, i % per, h * width:(h + 1) * width], first and i == 0, end and i == n - 1)
                    if i % per == per - 1:
                        last.then_inc(ring_used, 1)

            def chunks(t):
                return lambda i: t[:, i, :]

            pe.wait_ge(consts_made, at(CONSTS, "mix"))
            combine("x0")
            turn("x0", row)
            pe.wait_ge(onehots, 1)
            for t in range(TE):
                mm(ACC[3][:, 0:N], both_b[:, t, :, :], ends_b[:, t, 1, :], t == 0, t == TE - 1)
            pe.wait_ge(consts_made, at(CONSTS, "small"))
            for t in range(TE):
                last = mm(ACC[3][0:1, N:2 * N], ones_b[:, :], ends_b[:, t, 1, :], t == 0, t == TE - 1)
            last.then_inc(sums_made, 1)
            pe.wait_ge(onehot_copy, 1)
            for part in range(2):
                ready("ef", part)
                ef = slot("ef", part).rearrange("p (t c) -> p t c", c=DE)
                for t in range(TE // 2):
                    tt = part * TE // 2 + t
                    h = t % 2
                    last = mm(ACC[1][h * N:(h + 1) * N, 0:DE], to_dst[:, tt, :], ef[:, t, :], tt < 2, tt >= TE - 2)
                last.then_inc(ring_used, 1)
            pe.wait_ge(edges_kept, 1)
            pe.wait_ge(consts_made, at(CONSTS, "pair"))
            for c in range(2):
                last = mm(ACC[2][:, c * N:(c + 1) * N], tmp[:, c * P:(c + 1) * P], pairup[:, :])
            last.then_inc(edges_made, 1)
            pe.wait_ge(spread_ready, 1)
            pe.wait_ge(bias_in, 16)
            add_bias(ACC[1], None, degsel[:, :])
            pe.wait_ge(edges_kept, 2)
            ready("We", 0)
            we = slot("We", 0).rearrange("p (c n) -> p c n", c=2)
            for c in range(2):
                for h in range(2):
                    last = mm(ACC[1][h * N:(h + 1) * N, 0:HALF], hrow[:, c * N:(c + 1) * N],
                              we[:, c, h * HALF:(h + 1) * HALF], False, c == 1)
            last.then_inc(ring_used, 1)
            pe.wait_ge(cols_a, at(TURNS, "x0"))
            pe.wait_ge(cols_b, at(TURNS, "x0"))
            turn("edges", tmp)
            add_bias(ACC[0], ROW_BN)
            combine("slots", sums=True)
            mm(ACC[3][:, 0:2 * H4], pick(ROW_EDGE2, P), bias[:, 0:2 * H4]).then_inc(rows_made, 1)
            pe.wait_ge(cols_a, at(TURNS, "edges"))
            pe.wait_ge(cols_b, at(TURNS, "edges"))
            turn("slots", slots)
            pe.wait_ge(onehots, 2)
            for k in range(2):
                for t in range(TE // 2):
                    last = nc.tensor.transpose(ACC[1 + k][:, :].bitcast(bf16)[:, t * P:(t + 1) * P],
                                               ends_b[:, k * TE // 2 + t, :, :], ident_b[:, :])
                last.then_inc(pair_turned, 1)
            product(ACC[0], chunks(cols), "Wn")
            pe.wait_ge(cols_a, at(TURNS, "slots"))
            pe.wait_ge(cols_b, at(TURNS, "slots"))

            def gate_hidden(first, last):
                for u in range(first, last):
                    acc = ACC[2 + u % 2]
                    if u >= 2:
                        pe.wait_ge(gate_relu, u - 1)
                    mm(acc[:, 0:2 * H4], pick(ROW_EDGE1, P), bias[:, 0:2 * H4], True, False)
                    mm(acc[:, 0:2 * H4], ea[:, u // 2, :], ew1[:, (u % 2) * 2 * H4:(u % 2 + 1) * 2 * H4], False, True)\
                        .then_inc(gate_made, 1)

            pe.wait_ge(pair_ready, 2)
            pe.wait_ge(rows_kept, 1)
            pe.wait_ge(ea_in, 16)
            pe.wait_ge(ew1_in, 64)
            for l in range(L):
                add_bias(ACC[1], ROW_B1 + l)
                if l == 0:
                    gate_hidden(0, GATES[0])
                pe.wait_ge(nodes_ready, l + 1)
                for j in range(NJ):
                    mm(T[j][:, 0:4 * N], nodes[:, j * P:(j + 1) * P], spread[:, :, :]).then_inc(comb_made, 1)
                pe.wait_ge(comb_ready, NJ * (l + 1))
                product(ACC[1], lambda i: comb[:, i // 2, 2 * (i % 2), :], f"W1a{l}", end=False)
                product(ACC[1], lambda i: comb[:, i // 2, 2 * (i % 2) + 1, :], f"W1b{l}")
                gate_hidden(GATES[l], GATES[l] + 1)
                combine(f"l{l}")
                gate_hidden(GATES[l] + 1, GATES[l + 1])
                add_bias(ACC[0], ROW_B2 + l)
                turn(f"l{l}", row)
                product(ACC[0], chunks(cols), f"W2{l}", f"l{l}")

            add_bias(ACC[1], ROW_BQKV + 1)
            turn("nodes", nodes)
            add_bias(ACC[0], ROW_BQKV)
            for k, c in enumerate("qkv"):
                if k == 2:
                    pe.wait_ge(gate_relu, TE // 2)
                    add_bias(ACC[2], ROW_BQKV + 2)
                product(ACC[k], chunks(cols), f"W{c}", "nodes")
            for k, (src, there) in enumerate(((qrow, q_row), (krow, k_row))):
                pe.wait_ge(there, 1)
                for j in range(HJ):
                    last = nc.tensor.transpose(T[k][0:DH, j * P:(j + 1) * P], src[:, j * DH:(j + 1) * DH], ident[:, :])
                last.then_inc(heads_turned, 1)
            pe.wait_ge(q_cols, 1)
            pe.wait_ge(k_cols, 1)
            for j in range(HJ):
                for h in range(2):
                    last = mm(ACC[0][h * N:(h + 1) * N, j * N:(j + 1) * N], qt[:, j, h * N:(h + 1) * N],
                              kt[:, j, h * N:(h + 1) * N])
            last.then_inc(scores_made, 1)
            pe.wait_ge(probs_made, 2)
            for k in range(2):
                for j in range(2):
                    last = nc.tensor.transpose(T[k][:, j * P:(j + 1) * P], probs[:, 2 * k + j, :], ident[:, :])
                last.then_inc(probs_turned, 1)
            pe.wait_ge(v_row, 1)
            pe.wait_ge(probs_a, 1)
            pe.wait_ge(probs_b, 1)
            for j in range(HJ):
                last = mm(ACC[1][:, j * DH:(j + 1) * DH], probs_t[:, j, :], vrow[:, j * DH:(j + 1) * DH])
            last.then_inc(attn_made, 1)
            add_bias(ACC[2], ROW_BO)
            turn("attn", row)
            product(ACC[2], chunks(cols), "Wo", "attn")
            for k in range(2):
                add_bias(ACC[3 * (1 - k)], ROW_NORM + k, end=True).then_inc(rows_made, 1)
            combine("f0")
            pe.wait_ge(rows_kept, 2)
            add_bias(ACC[3], ROW_NORM + 2, end=True).then_inc(rows_made, 1)
            combine("tok", sums=True)
            turn("tok", row)
            pe.wait_ge(cols_a, at(TURNS, "tok"))
            pe.wait_ge(cols_b, at(TURNS, "tok"))
            pe.wait_ge(rows_kept, 3)
            for i in range(NI):
                mm(ACC[0][0:N, 0:N], cols[:, i, :], slots_t[:, i, :], i == 0, i == NI - 1)
                last = mm(ACC[0][N:P, 0:N], slots_t[:, i, :], cols[:, i, :], i == 0, i == NI - 1)
            last.then_inc(logits_made, 1)
            pe.wait_ge(gate_ready, 1)
            for t in range(TE):
                last = mm(SM[ROW_MSG2:ROW_MSG2 + 1, 0:N], gate[:, t:t + 1], to_dst[:, t, :], t == 0, t == TE - 1)
            last.then_inc(gsum_made, 1)
            pe.wait_ge(soft_ready, 1)
            for k in range(1 + SB):
                last = nc.tensor.transpose(T[0][:, k * P:(k + 1) * P], soft2[:, k, :], ident[:, :])
            last.then_inc(soft_turned, 1)
            pe.wait_ge(weights_act, 1)
            pe.wait_ge(weights_dve, 1)
            for j in range(NJ):
                last = mm(T[1 + j // 2][:, (j % 2) * P:(j % 2 + 1) * P], keep[:, j * P:(j + 1) * P], dispatch_w[:, :])
            last.then_inc(mixed_made, 1)

            def fc1(b):
                for g in range(4):
                    mm(ACC[b][32 * g:32 * g + 32, 0:Q], pick(ROW_FC1 + b, 32), bias[:, g * Q:(g + 1) * Q], True, False)
                if b == 0:
                    pe.wait_ge(mixed_a, 1)
                    pe.wait_ge(mixed_b, 1)
                for i in range(NI):
                    if i % 3 == 0:
                        ready(f"fc1{b}", i // 3)
                    w = slot(f"fc1{b}", i // 3).rearrange("p (i c) -> p i c", i=3)
                    for g in range(4):
                        last = mm(ACC[b][32 * g:32 * g + 32, 0:Q], cols[:, i, b // 2 * 32:b // 2 * 32 + 32],
                                  w[:, i % 3, g * Q:(g + 1) * Q], False, i == NI - 1)
                    if i % 3 == 2:
                        last.then_inc(ring_used, 1)

            def turn_hidden(k):
                pe.wait_ge(hid_made, 2 * k + 2)
                for j in range(NJ):
                    last = nc.tensor.transpose(T[1 + k][:, j * P:(j + 1) * P], hid[:, k, j * P:(j + 1) * P], ident[:, :])
                last.then_inc(hid_turned, 1)

            fc1(0)
            fc1(1)
            fc1(2)
            turn_hidden(0)
            pe.wait_ge(rows_kept, 4)
            fc1(3)
            for k in range(SB):
                pe.wait_ge(hid_made, 2 * k + 2)
                for c in range(4):
                    mm(ACC[k][32 * c:32 * c + 32, 0:Q], ident[:, ROW_FC2 + 32 * k:ROW_FC2 + 32 * k + 32],
                       bias[:, c * Q:(c + 1) * Q], True, False)
                pe.wait_ge(hid_masked, k + 1)
                for g in range(4):
                    name, part = f"fc2{2 * k + g // 2}", g % 2
                    ready(name, part)
                    w = slot(name, part).rearrange("p (j c) -> p j c", j=NJ)
                    for j in range(NJ):
                        for c in range(4):
                            last = mm(ACC[k][32 * c:32 * c + 32, 0:Q], hid_t[:, k, j, 32 * g:32 * g + 32],
                                      w[:, j, c * Q:(c + 1) * Q], False, g == 3 and j == NJ - 1)
                    last.then_inc(ring_used, 1)
                    if k == 0 and g == 0:
                        turn_hidden(1)
            pe.wait_ge(weights_act, 5)
            for k in range(SB):
                pe.wait_ge(y_ready, k + 1)
                for q in range(2):
                    last = mm(ACC[2 + q][:, 0:Q], combine_w[:, q, k, :], mixed[:, k, :], k == 0, k == SB - 1)
            last.then_inc(mix_out, 1)

            pe.wait_ge(typesel_ready, 1)
            add_bias(ACC[0], None, typesel[:, :])
            combine("g1")
            turn("xn1", keep)
            for t in range(TYPES):
                pe.wait_ge(typed_ready, t + 1)
                product(ACC[0], lambda i: typed[:, t, i, :], f"Wt{t}", end=t == TYPES - 1)
            for f in range(2):
                mm(ACC[1 + f][N:P, 0:HALF], pick(ROW_MSG1), bias[:, f * HALF:(f + 1) * HALF], True, False)
            turn("h", hrow)
            pe.wait_ge(cols_a, at(TURNS, "h"))
            pe.wait_ge(cols_b, at(TURNS, "h"))
            for i in range(NI):
                if i % 3 == 0:
                    ready("Wma", i // 3)
                    ready("Wmb", i // 3)
                wa = slot("Wma", i // 3).rearrange("p (i c) -> p i c", i=3)
                wb = slot("Wmb", i // 3).rearrange("p (i c) -> p i c", i=3)
                for f in range(2):
                    cs = slice(f * HALF, (f + 1) * HALF)
                    last_a = mm(ACC[1 + f][0:N, 0:HALF], cols[:, i, :], wa[:, i % 3, cs], i == 0, i == NI - 1)
                    last_b = mm(ACC[1 + f][N:P, 0:HALF], cols[:, i, :], wb[:, i % 3, cs], False, i == NI - 1)
                if i % 3 == 2:
                    last_a.then_inc(ring_used, 1)
                    last_b.then_inc(ring_used, 1)
            banks = [(T[0], T[1]), (T[2], SM), (ACC[3], ACC[1])]

            def gather(t):
                if t >= 3:
                    pe.wait_ge(msg_act, t - 2)
                    pe.wait_ge(msg_dve, t - 2)
                for f in range(2):
                    for k in range(2):
                        last = mm(banks[t % 3][f][:, 0:HALF], pair[:, t * P:(t + 1) * P],
                                  pq[:, k, f * HALF:(f + 1) * HALF], k == 0, k == 1)
                last.then_inc(gathered, 1)

            def scatter(t):
                pe.wait_ge(msg_act, t + 1)
                pe.wait_ge(msg_dve, t + 1)
                for h in range(2):
                    last = mm(ACC[0][h * N:(h + 1) * N, 0:HALF], to_dst[:, t, :], msg[:, t % 3, h * HALF:(h + 1) * HALF],
                              t == 0, t == TE - 1)
                last.then_inc(scattered, 1)

            pe.wait_ge(pq_dve, 1)
            gather(0)
            gather(1)
            for t in range(TE):
                if t + 2 < TE:
                    gather(t + 2)
                scatter(t)
            pe.wait_ge(gsum_ready, 1)
            add_bias(ACC[1], None, gatesel[:, :])
            turn("msg", row)
            product(ACC[1], chunks(cols), "Wm2", "msg")
            add_bias(ACC[2], ROW_AGG1)
            turn("agg1", row)
            product(ACC[2], chunks(cols), "Wg1", "agg1")
            add_bias(ACC[1], ROW_AGG2)
            turn("agg2", row)
            product(ACC[1], chunks(cols), "Wg2", "agg2")
            add_bias(ACC[2], ROW_OUT)
            turn("h2", row)
            product(ACC[2], chunks(cols), "Wout", "h2")
            add_bias(ACC[0], ROW_FFN1, width=4 * R)
            combine("go")

            combine("f1")
            turn("x3", row)
            pe.wait_ge(encw_in, 16)
            pe.wait_ge(cols_a, at(TURNS, "x3"))
            pe.wait_ge(cols_b, at(TURNS, "x3"))
            for i in range(NI):
                last = mm(ACC[3][0:R, 0:N], encw[:, i, :], cols[:, i, :], i == 0, i == NI - 1)
            last.then_inc(enc_made, 1)
            pe.wait_ge(enc_ready, 1)
            pe.wait_ge(sww_in, 16)
            mm(T[2][:, 0:X], enc_t[:, :, :], sww[:, :]).then_inc(route_made, 1)
            product(ACC[0], chunks(cols), "w1", width=4 * R)
            pe.wait_ge(route_ready, 1)
            nc.tensor.transpose(ACC[3][:, 0:N], route_pad[:, :], ident[0:N, 0:N]).then_inc(route_turned, 1)
            pe.wait_ge(gelu_made, 1)
            for j in range(2):
                last = nc.tensor.transpose(T[0][:, j * P:(j + 1) * P], tmp[:, j * P:(j + 1) * P], ident[:, :])
            last.then_inc(exp_turned, 1)
            pe.wait_ge(routesel_ready, 1)
            add_bias(ACC[1], None, routesel[:, :])
            pe.wait_ge(exp_cols, 1)
            product(ACC[1], chunks(cols), "w2", per=2, n=4)

        @block.vector
        def _(dve):
            v = nc.vector
            links = [0]

            def link(op):
                links[0] += 1
                op.then_inc(dve_link, 1)
                dve.wait_ge(dve_link, links[0])

            def statistics(name, src, eps):
                k = COMBINES.index(name)
                link(v.bn_stats(stat6[:, :], src))
                v.bn_aggr(mv[:, k, :], stat6[:, :]).then_inc(stats_ready, 1)
                dve.wait_ge(combined, k + 1)
                if eps is None:
                    link(v.tensor_copy(sc[:, k, 0:3], SM[:, 0:3]))
                else:
                    link(v.tensor_tensor(sc[:, k, 0:3], SM[:, 0:3], eps[:, :], ALU.add))

            def moments(name, src):
                k = COMBINES.index(name)
                statistics(name, src, eps3)
                q = POWERS.index(name)
                v.scalar_tensor_tensor(out=pin[:, q:q + 1], in0=sc[:, k, 2:3], scalar=sc[:, k, 2:3], in1=sc[:, k, 1:2],
                                       op0=ALU.mult, op1=ALU.add).then_inc(power_asked, 1)

            def root(name):
                q = POWERS.index(name)
                dve.wait_ge(power_done, q + 1)
                return pout[:, q:q + 1]

            def normalise(dst, name, src):
                r = root(name)
                k = COMBINES.index(name)
                return v.tensor_scalar(dst, src, sc[:, k, 0:1], r, ALU.subtract, ALU.mult)

            def collect(name, dst=None):
                dve.wait_ge(turned_a, at(TURNS, name))
                v.tensor_copy(cols[:, 0:4, :] if dst is None else dst, T[0][:, 0:4 * N]).then_inc(cols_a, 1)

            def sums_root(name, src, squares, least):
                k, q = COMBINES.index(name), POWERS.index(name)
                link(v.tensor_tensor_reduce(out=squares, in0=src, in1=src, scale=1.0, scalar=0.0, op0=ALU.mult,
                                            op1=ALU.add, accum_out=mv[:, k, 0:1]))
                v.tensor_copy(mv[:, k, 1:2], mv[:, k, 0:1]).then_inc(stats_ready, 1)
                dve.wait_ge(combined, k + 1)
                v.tensor_scalar(pin[:, q:q + 1], SM[:, 0:1], 2.0, least, ALU.mult, ALU.max).then_inc(power_asked, 1)

            v.memset(ew1[:, :], 0.0).then_inc(ew1_clear, 1)
            dve.wait_ge(x_in, 16)
            dve.wait_ge(consts_made, at(CONSTS, "mix"))
            moments("x0", x0[:, :])
            dve.wait_ge(idx_in, 16)
            dve.wait_ge(consts_made, at(CONSTS, "iota"))
            v.tensor_copy(idxf[:, :], idx[:, :])
            link(v.tensor_copy(irow[:, :], irow_i[:, :]))
            normalise(row[:, :], "x0", x0[:, :]).then_inc(rows_ready, 1)

            def onehot(o, c0):
                return v.tensor_tensor(o, idxf[:, c0:c0 + TE].unsqueeze(2).to_broadcast([P, TE, N]),
                                       irow[:, :].unsqueeze(1).to_broadcast([P, TE, N]), ALU.is_equal)

            onehot(ends_b[:, :, 1, :], TE)
            link(onehot(ends_b[:, :, 0, :], 0))
            for a in range(2):
                last = v.tensor_tensor(both_b[:, :, a, :], ends_b[:, :, 0, :], ends_b[:, :, 1, :], ALU.add)
            last.then_inc(onehots, 1)
            onehot(to_dst[:, :, :], TE).then_inc(onehot_copy, 1)
            collect("x0")
            v.tensor_copy(ident_b[:, :], ident[:, :]).then_inc(onehots, 1)
            dve.wait_ge(consts_made, at(CONSTS, "blocks"))
            dve.wait_ge(sums_made, 1)
            v.tensor_copy(spread[0:N, 1, :], ACC[3][0:N, 0:N])
            v.tensor_copy(spread[N:P, 3, :], ACC[3][N:P, 0:N])
            v.tensor_copy(degsel[0:1, :], ACC[3][0:1, N:2 * N]).then_inc(spread_ready, 1)
            dve.wait_ge(slots_in, 16)
            dve.wait_ge(col_in, 16)
            sums_root("slots", slots[:, :], nodes[:, :], EPS * EPS)
            dve.wait_ge(consts_made, at(CONSTS, "fills"))
            e2 = edges2[:, :, :, :].rearrange("p j (h q) n -> p j h q n", q=2)[:, :, :, 1, :]
            dve.wait_ge(turned_a, at(TURNS, "edges"))
            v.tensor_copy(e2[:, 0:2], T[0][:, 0:4 * N].rearrange("p (j h n) -> p j h n", j=2, h=2)).then_inc(cols_a, 1)
            r = root("slots")
            v.tensor_scalar(slots[:, :], slots[:, :], r, colp[:, C_SCALE:C_SCALE + 1], ALU.mult, ALU.mult)\
                .then_inc(rows_ready, 1)
            collect("slots", slots_t[:, 0:4, :])
            for k in range(2):
                dve.wait_ge(pair_turned, k + 1)
                v.tensor_copy(pair[:, k * E // 2:(k + 1) * E // 2], ACC[1 + k][:, :].bitcast(bf16)).then_inc(pair_ready, 1)
            dve.wait_ge(ring_used, used("Wn"))
            v.tensor_copy(nodes[:, :], ACC[0][:, 0:HALF]).then_inc(nodes_ready, 1)
            dve.wait_ge(cols_b, at(TURNS, "edges"))

            u = 0
            for l in range(L):
                for j in range(NJ):
                    dve.wait_ge(comb_made, NJ * l + j + 1)
                    v.tensor_tensor(comb[:, j, :, :], T[j][:, 0:4 * N].rearrange("p (q n) -> p q n", q=4),
                                    edges2[:, j, :, :], ALU.add).then_inc(comb_ready, 1)
                if l == 0:
                    dve.wait_ge(type_in, 16)
                    v.tensor_copy(ramp[:, :], ramp_i[:, :])
                    v.tensor_copy(icol[:, :], icol_i[:, :])
                    link(v.tensor_copy(typesf[:, :], types[:, :]))
                    for t in range(TYPES):
                        v.tensor_scalar(typemask[:, t, :], typesf[:, :], float(t), None, ALU.is_equal)
                    v.tensor_scalar(typesel[:, :], typesf[:, :], icol[:, 0:1], None, ALU.is_equal).then_inc(typesel_ready, 1)
                while u < GATES[l]:
                    dve.wait_ge(gate_mult, u + 1)
                    v.tensor_reduce(gate_in[:, 2 * u:2 * u + 2], eprod[:, u % 2, :].rearrange("p (a c) -> p a c", a=2),
                                    AX.X, ALU.add).then_inc(gate_red, 1)
                    u += 1
                dve.wait_ge(ring_used, used(f"W1b{l}"))
                moments(f"l{l}", ACC[1][:, 0:HALF])
                normalise(row[:, :], f"l{l}", ACC[1][:, 0:HALF]).then_inc(rows_ready, 1)
                dve.wait_ge(turned_b, at(TURNS, f"l{l}"))
                for i in (4, 5):
                    op = v.tensor_scalar(cols[:, i, :], T[1][:, (i - 4) * N:(i - 3) * N], colp[:, C_G + l * NI + i:C_G + l * NI + i + 1],
                                         colp[:, C_B + l * NI + i:C_B + l * NI + i + 1], ALU.mult, ALU.add)
                link(op)
                v.tensor_scalar(cols[:, 4:6, :], cols[:, 4:6, :], 0.0, None, ALU.max).then_inc(cols_b, 1)
                dve.wait_ge(ring_used, used(f"W2{l}"))
                last = v.tensor_tensor(nodes[:, :], ACC[0][:, 0:HALF], nodes[:, :], ALU.add)
                if l < L - 1:
                    last.then_inc(nodes_ready, 1)
                else:
                    last.then_inc(rows_ready, 1)
            while u < TE // 2:
                dve.wait_ge(gate_mult, u + 1)
                op = v.tensor_reduce(gate_in[:, 2 * u:2 * u + 2], eprod[:, u % 2, :].rearrange("p (a c) -> p a c", a=2),
                                     AX.X, ALU.add)
                op.then_inc(gate_red, 1)
                u += 1
            collect("nodes")
            dve.wait_ge(gate_red, TE // 2)
            dve.wait_ge(tail_in, 16)
            v.tensor_scalar(gate_z[:, :], gate_in[:, :], tail[:, X:X + 1], None, ALU.add).then_inc(gate_asked, 1)
            link(v.tensor_tensor(x1[:, :], nodes[:, :], x0[:, :], ALU.add))
            dve.wait_ge(gate_exp, 1)
            link(v.tensor_scalar(gate_d[:, :], gate_e[:, :], 1.0, None, ALU.add))
            v.reciprocal(gate[:, :], gate_d[:, :]).then_inc(gate_ready, 1)
            dve.wait_ge(ring_used, used("Wk"))
            v.tensor_copy(krow, ACC[1][:, 0:HALF]).then_inc(k_row, 1)
            dve.wait_ge(heads_turned, 2)
            v.tensor_copy(kt, T[1][0:DH, 0:HJ * P].rearrange("p (j n) -> p j n", j=HJ)).then_inc(k_cols, 1)
            dve.wait_ge(scores_made, 1)
            s3 = ACC[0][:, 0:HJ * N].rearrange("p (j m) -> p j m", j=HJ)
            link(v.tensor_reduce(mx[:, :], s3, AX.X, ALU.max))
            v.tensor_tensor(shifted, s3, mx[:, :].unsqueeze(2).to_broadcast([P, HJ, N]), ALU.subtract)\
                .then_inc(scores_shift, 1)
            dve.wait_ge(probs_made, 2)
            link(v.tensor_reduce(ssum[:, :], probs, AX.X, ALU.add))
            link(v.reciprocal(rsum[:, :], ssum[:, :]))
            dve.wait_ge(probs_turned, 1)
            v.tensor_copy(probs_t[:, 0:2, :], T[0][:, 0:2 * P].rearrange("p (j n) -> p j n", j=2)).then_inc(probs_a, 1)
            dve.wait_ge(attn_made, 1)
            v.tensor_tensor(row[:, :].rearrange("p (j c) -> p j c", j=HJ), ACC[1][:, 0:HALF].rearrange("p (j c) -> p j c", j=HJ),
                            rsum[:, :].unsqueeze(2).to_broadcast([P, HJ, DH]), ALU.mult).then_inc(rows_ready, 1)
            collect("attn")
            dve.wait_ge(ring_used, used("Wo"))
            link(v.tensor_tensor(x1[:, :], ACC[2][:, 0:HALF], x1[:, :], ALU.add))

            statistics("f0", x1[:, :], None)
            kf, cf = POWERS.index("f0"), COMBINES.index("f0")
            link(v.scalar_tensor_tensor(out=small[:, 0:1], in0=sc[:, cf, 2:3], scalar=sc[:, cf, 2:3], in1=sc[:, cf, 1:2],
                                        op0=ALU.mult, op1=ALU.add))
            v.tensor_scalar(pin[:, kf:kf + 1], small[:, 0:1], 1.0 + EPS, EPS * EPS, ALU.mult, ALU.add).then_inc(power_asked, 1)
            v.tensor_scalar(small[:, 1:2], small[:, 0:1], (1.0 + EPS) * EPS ** 2, EPS ** 4, ALU.mult, ALU.add)
            dve.wait_ge(rows_kept, 2)
            link(v.scalar_tensor_tensor(out=tmp[:, :], in0=x1[:, :], scalar=sc[:, cf, 0:1], in1=rows4[:, 0, :],
                                        op0=ALU.subtract, op1=ALU.mult))
            sums_root("tok", tmp[:, :], hrow[:, :], small[:, 1:2])
            v.tensor_scalar(keep[:, :], tmp[:, :], root("f0"), None, ALU.mult)
            v.tensor_scalar(row[:, :], tmp[:, :], root("tok"), None, ALU.mult).then_inc(rows_ready, 1)
            collect("tok")
            dve.wait_ge(logits_made, 1)
            v.tensor_reduce(small[:, 1:2], ACC[0][:, 0:N], AX.X, ALU.max, negate=True).then_inc(logits_max, 1)
            dve.wait_ge(soft_made, 1)
            link(v.reciprocal(small[:, 3:4], small[:, 2:3]))
            v.tensor_scalar(soft2[:, 0, :].rearrange("p (a n) -> p a n", a=2),
                            soft[:, :].unsqueeze(1).to_broadcast([P, 2, N]), small[:, 3:4], None, ALU.mult)
            for k in range(SB):
                last = v.tensor_scalar(soft2[:, 1 + k, :].rearrange("p (a n) -> p a n", a=4),
                                       soft[:, 32 * k:32 * k + 32].unsqueeze(1).to_broadcast([P, 4, 32]),
                                       small[:, 3:4], None, ALU.mult)
            last.then_inc(soft_ready, 1)
            dve.wait_ge(soft_turned, 1)
            v.tensor_copy(dispatch_w[N:P, N:P], T[0][N:P, N:P]).then_inc(weights_dve, 1)
            dve.wait_ge(gsum_made, 1)
            v.tensor_copy(gatesel[ROW_MSG2:ROW_MSG2 + 1, :], SM[ROW_MSG2:ROW_MSG2 + 1, 0:N]).then_inc(gsum_ready, 1)
            dve.wait_ge(mixed_made, 1)
            v.tensor_copy(cols[:, 0:4, :], T[1][:, 0:4 * N].rearrange("p (i n) -> p i n", n=N)).then_inc(mixed_a, 1)
            dve.wait_ge(consts_made, at(CONSTS, "slotmask"))
            for k in range(SB):
                dve.wait_ge(hid_turned, k + 1)
                v.tensor_tensor(hid_t[:, k, :, :], T[1 + k][:, 0:HALF].rearrange("p (j n) -> p j n", j=NJ),
                                slotmask[:, :, :], ALU.mult).then_inc(hid_masked, 1)
            dve.wait_ge(mix_out, 1)
            v.tensor_tensor(x2[:, 0:Q], ACC[2][:, 0:Q], x1[:, 0:Q], ALU.add)
            link(v.tensor_tensor(x2[:, Q:HALF], ACC[3][:, 0:Q], x1[:, Q:HALF], ALU.add))

            moments("g1", x2[:, :])
            normalise(keep[:, :], "g1", x2[:, :]).then_inc(rows_ready, 1)
            collect("xn1")
            dve.wait_ge(cols_a, at(TURNS, "xn1"))
            dve.wait_ge(cols_b, at(TURNS, "xn1"))
            for t in range(TYPES):
                v.tensor_tensor(typed[:, t, :, :], cols[:, :, :], typemask[:, t, :].unsqueeze(1).to_broadcast([P, NI, N]),
                                ALU.mult).then_inc(typed_ready, 1)
            dve.wait_ge(ring_used, used(f"Wt{TYPES - 1}"))
            v.tensor_copy(hrow[:, :], ACC[0][:, 0:HALF]).then_inc(rows_ready, 1)
            collect("h")
            dve.wait_ge(rows_kept, 4)
            link(v.tensor_tensor(x2[:, :], x2[:, :], rows4[:, 2, :], ALU.add))
            dve.wait_ge(ring_used, used("Wmb"))
            link(v.tensor_copy(pq[:, 0, HALF:D], ACC[2][:, 0:HALF]))
            v.tensor_tensor(pq[:, 1, HALF:D], ACC[2][:, 0:HALF], pq[:, 0, HALF:D].bitcast(fp32), ALU.subtract)
            dve.wait_ge(pq_round, 1)
            v.tensor_tensor(pq[:, 1, 0:HALF], ACC[1][:, 0:HALF], pq[:, 0, 0:HALF].bitcast(fp32), ALU.subtract)\
                .then_inc(pq_dve, 1)
            second = [T[1], SM, ACC[1]]
            for t in range(TE):
                dve.wait_ge(gathered, t + 1)
                if t >= 3:
                    dve.wait_ge(scattered, t - 2)
                v.tensor_scalar(msg[:, t % 3, HALF:D], second[t % 3][:, 0:HALF], gate[:, t:t + 1], 0.0, ALU.mult, ALU.max)\
                    .then_inc(msg_dve, 1)
            dve.wait_ge(scattered, TE)
            v.tensor_copy(row[:, :], ACC[0][:, 0:HALF]).then_inc(rows_ready, 1)
            collect("msg")
            dve.wait_ge(ring_used, used("Wm2"))
            v.tensor_copy(row[:, :], ACC[1][:, 0:HALF]).then_inc(rows_ready, 1)
            collect("agg1")
            dve.wait_ge(ring_used, used("Wg1"))
            v.tensor_scalar(row[:, :], ACC[2][:, 0:HALF], 0.0, None, ALU.max).then_inc(rows_ready, 1)
            collect("agg2")
            dve.wait_ge(ring_used, used("Wg2"))
            v.tensor_tensor(row[:, :], ACC[1][:, 0:HALF], hrow[:, :], ALU.add).then_inc(rows_ready, 1)
            collect("h2")
            dve.wait_ge(ring_used, used("Wout"))
            link(v.tensor_tensor(tmp[:, :], ACC[2][:, 0:HALF], keep[:, :], ALU.add))
            moments("go", tmp[:, :])
            ko = COMBINES.index("go")
            link(v.scalar_tensor_tensor(out=hrow[:, :], in0=tmp[:, :], scalar=sc[:, ko, 0:1], in1=rows4[:, 1, :],
                                        op0=ALU.subtract, op1=ALU.mult))
            link(v.scalar_tensor_tensor(out=x3[:, :], in0=hrow[:, :], scalar=root("go"), in1=x2[:, :],
                                        op0=ALU.mult, op1=ALU.add))

            moments("f1", x3[:, :])
            normalise(row[:, :], "f1", x3[:, :]).then_inc(rows_ready, 1)
            collect("x3")
            dve.wait_ge(enc_made, 1)
            v.tensor_scalar(enc_t[:, :, :], ACC[3][0:R, 0:N].unsqueeze(1).to_broadcast([R, 2, N]),
                            colp[0:R, C_ENCB:C_ENCB + 1], None, ALU.add).then_inc(enc_ready, 1)
            dve.wait_ge(route_made, 1)
            link(v.tensor_tensor(lg[:, :], T[2][:, 0:X], tail[:, 0:X], ALU.add))
            v.tensor_reduce(small[:, 4:5], lg[:, :], AX.X, ALU.max, negate=True).then_inc(route_max, 1)
            dve.wait_ge(route_exp, 1)
            link(v.reciprocal(small[:, 6:7], small[:, 5:6]))
            link(v.tensor_scalar(pr[:, :], pe_[:, :], small[:, 6:7], None, ALU.mult))
            link(v.tensor_reduce(small[:, 7:8], pr[:, :], AX.X, ALU.max))
            link(v.scalar_tensor_tensor(out=cand[:, :], in0=pr[:, :], scalar=small[:, 7:8], in1=ramp[:, :],
                                        op0=ALU.is_equal, op1=ALU.mult))
            link(v.tensor_reduce(mx[:, 0:1], cand[:, :], AX.X, ALU.max))
            link(v.tensor_scalar(route[:, :], cand[:, :], mx[:, 0:1], small[:, 7:8], ALU.is_equal, ALU.mult))
            v.tensor_copy(route_pad[:, ROW_FFN2:ROW_FFN2 + X], route[0:N, :]).then_inc(route_ready, 1)
            dve.wait_ge(act_link, 1)
            for h in range(2):
                rows = slice(h * N, (h + 1) * N)
                last = v.tensor_tensor(tmp[rows, 0:4 * R].rearrange("p (e r) -> p e r", e=4),
                                       hrow[rows, 0:4 * R].rearrange("p (e r) -> p e r", e=4),
                                       route[rows, 4 * h:4 * h + 4].unsqueeze(2).to_broadcast([N, 4, R]), ALU.mult)
            last.then_inc(gelu_made, 1)
            dve.wait_ge(route_turned, 1)
            v.tensor_copy(routesel[:, :], ACC[3][:, 0:N]).then_inc(routesel_ready, 1)
            dve.wait_ge(exp_turned, 1)
            v.tensor_copy(cols[:, 0:4, :], T[0][:, 0:4 * N].rearrange("p (i n) -> p i n", n=N)).then_inc(exp_cols, 1)
            dve.wait_ge(ring_used, used("w2"))
            v.tensor_tensor(row[:, :], ACC[1][:, 0:HALF], x3[:, :], ALU.add).then_inc(final_ready, 1)

        @block.scalar
        def _(act):
            a = nc.scalar

            def copy(dst, src):
                return a.activation(dst, src, ACT.Copy)

            def collect(name, dst=None):
                act.wait_ge(turned_b, at(TURNS, name))
                copy(cols[:, 4:6, :] if dst is None else dst,
                     T[1][:, 0:2 * N].rearrange("p (i n) -> p i n", n=N)).then_inc(cols_b, 1)

            act.dma_start(idx[:, :], ins["idx"]).then_inc(idx_in, 16)
            act.dma_start(bias[:, :], ins["bias"]).then_inc(bias_in, 16)
            act.dma_start(slots[:, :], ins["slots"]).then_inc(slots_in, 16)
            act.dma_start(colp[:, :], ins["colp"]).then_inc(col_in, 16)
            act.dma_start(types[:, :], ins["types"].to_broadcast([P, N])).then_inc(type_in, 16)
            act.wait_ge(ew1_clear, 1)
            for t in range(4):
                act.dma_start(ew1[t * DA:(t + 1) * DA, t * H4:(t + 1) * H4], ins["ew1"]).then_inc(ew1_in, 16)
            act.dma_start(ea[:, :, :], ins["ea"].rearrange("p (g e) -> p g e", g=4)).then_inc(ea_in, 16)
            act.dma_start(encw[:, :, :], ins["encw"].rearrange("p (i r) -> p i r", i=NI)).then_inc(encw_in, 16)
            act.dma_start(sww[:, :], ins["sww"]).then_inc(sww_in, 16)
            act.dma_start(tail[:, :], ins["tail"].to_broadcast([P, X + 1])).then_inc(tail_in, 16)
            collect("x0")
            act.wait_ge(ring_used, used("ef"))
            copy(tmp[:, 0:DE], ACC[1][:, 0:DE]).then_inc(edges_kept, 1)
            act.wait_ge(edges_made, 1)
            copy(hrow[:, 0:2 * N], ACC[2][:, 0:2 * N]).then_inc(edges_kept, 1)
            act.wait_ge(ring_used, used("We", 0))
            copy(tmp[:, :], ACC[1][:, 0:HALF]).then_inc(rows_ready, 1)
            e2 = edges2[:, :, :, :].rearrange("p j (h q) n -> p j h q n", q=2)[:, :, :, 1, :]
            act.wait_ge(consts_made, at(CONSTS, "fills"))
            act.wait_ge(turned_b, at(TURNS, "edges"))
            copy(e2[:, 2], T[1][:, 0:2 * N].rearrange("p (h n) -> p h n", h=2)).then_inc(cols_b, 1)
            act.wait_ge(rows_made, 1)
            copy(rows4[:, 3, :], ACC[3][:, 0:2 * H4]).then_inc(rows_kept, 1)
            collect("slots", slots_t[:, 4:6, :])
            act.wait_ge(col_in, 16)

            def gate_hidden(first, last):
                for u in range(first, last):
                    act.wait_ge(gate_made, u + 1)
                    if u >= 2:
                        act.wait_ge(gate_mult, u - 1)
                    a.activation(ehid[:, u % 2, :], ACC[2 + u % 2][:, 0:2 * H4], ACT.Relu).then_inc(gate_relu, 1)

            gate_hidden(0, GATES[0])
            for l in range(L):
                gate_hidden(GATES[l], GATES[l] + 1)
                act.wait_ge(turned_a, at(TURNS, f"l{l}"))
                for i in range(4):
                    op = a.activation(cols[:, i, :], T[0][:, i * N:(i + 1) * N], ACT.Relu,
                                      scale=colp[:, C_G + l * NI + i:C_G + l * NI + i + 1],
                                      bias=colp[:, C_B + l * NI + i:C_B + l * NI + i + 1])
                op.then_inc(cols_a, 1)
                gate_hidden(GATES[l] + 1, GATES[l + 1])
            collect("nodes")
            act.wait_ge(gate_asked, 1)
            a.activation(gate_e[:, :], gate_z[:, :], ACT.Exp, scale=-1.0).then_inc(gate_exp, 1)
            act.wait_ge(ring_used, used("Wq"))
            copy(qrow, ACC[0][:, 0:HALF]).then_inc(q_row, 1)
            act.wait_ge(heads_turned, 1)
            copy(qt, T[0][0:DH, 0:HJ * P].rearrange("p (j n) -> p j n", j=HJ)).then_inc(q_cols, 1)
            act.wait_ge(ring_used, used("Wv"))
            act.wait_ge(consts_made, at(CONSTS, "probs"))
            copy(vrow, ACC[2][:, 0:HALF]).then_inc(v_row, 1)
            act.wait_ge(scores_shift, 1)
            for h in range(2):
                rows = slice(h * N, (h + 1) * N)
                a.activation(probs[rows, :, h * N:(h + 1) * N], shifted[rows, :, :], ACT.Exp, scale=DH ** -0.5)\
                    .then_inc(probs_made, 1)
            act.wait_ge(probs_turned, 2)
            copy(probs_t[:, 2:4, :], T[1][:, 0:2 * P].rearrange("p (j n) -> p j n", j=2)).then_inc(probs_b, 1)
            collect("attn")
            for k in range(3):
                act.wait_ge(rows_made, k + 2)
                copy(rows4[:, k, :], ACC[(3, 0, 3)[k]][:, 0:HALF]).then_inc(rows_kept, 1)
            collect("tok")
            act.wait_ge(logits_max, 1)
            a.activation(soft[:, :], ACC[0][:, 0:N], ACT.Exp, bias=small[:, 1:2], accum_out=small[:, 2:3]).then_inc(soft_made, 1)
            act.wait_ge(soft_turned, 1)
            copy(dispatch_w[0:N, 0:N], T[0][0:N, N:P]).then_inc(weights_act, 1)
            act.wait_ge(mixed_made, 1)
            copy(cols[:, 4:6, :], T[2][:, 0:2 * N].rearrange("p (i n) -> p i n", n=N)).then_inc(mixed_b, 1)
            for c in range(4):
                rows = slice(32 * c, 32 * c + 32)
                copy(combine_w[rows, c % 2, :, c // 2 * N:(c // 2 + 1) * N],
                     T[0][rows, P:(1 + SB) * P].rearrange("p (k n) -> p k n", k=SB)[:, :, 0:N]).then_inc(weights_act, 1)
            for b in range(NB):
                act.wait_ge(ring_used, used(f"fc1{b}"))
                a.activation(hid[:, b // 2, b % 2 * Q:(b % 2 + 1) * Q], ACC[b][:, 0:Q], ACT.Gelu).then_inc(hid_made, 1)
            for k in range(SB):
                act.wait_ge(ring_used, used(f"fc2{2 * k + 1}"))
                copy(mixed[:, k, :], ACC[k][:, 0:Q]).then_inc(y_ready, 1)
            collect("xn1")
            collect("h")
            act.wait_ge(ring_used, used("Wmb"))
            copy(pq[:, 0, 0:HALF], ACC[1][:, 0:HALF]).then_inc(pq_round, 1)
            first = [T[0], T[2], ACC[3]]
            act.wait_ge(gate_ready, 1)
            for t in range(TE):
                act.wait_ge(gathered, t + 1)
                if t >= 3:
                    act.wait_ge(scattered, t - 2)
                a.activation(msg[:, t % 3, 0:HALF], first[t % 3][:, 0:HALF], ACT.Relu, scale=gate[:, t:t + 1]).then_inc(msg_act, 1)
            for name in ("msg", "agg1", "agg2", "h2", "x3"):
                collect(name)
            act.wait_ge(route_max, 1)
            a.activation(pe_[:, :], lg[:, :], ACT.Exp, bias=small[:, 4:5], accum_out=small[:, 5:6]).then_inc(route_exp, 1)
            act.wait_ge(ring_used, used("w1"))
            a.activation(hrow[:, 0:4 * R], ACC[0][:, 0:4 * R], ACT.Gelu).then_inc(act_link, 1)


def _weight(w, groups=1):
    import numpy as np
    rows, cols = w.shape
    n = rows // P
    half = n // 2
    order = [half * (i % 2) + i // 2 for i in range(n)]
    return np.ascontiguousarray(w.reshape(n, P, cols)[order].transpose(1, 0, 2)).reshape(P, n * cols)


def _halves(x):
    import numpy as np
    return np.ascontiguousarray(x.reshape(N, 2, HALF).transpose(1, 0, 2)).reshape(P, HALF)


def kernel(**inputs):
    import numpy as np
    import concourse.bacc as bacc
    from concourse.bass_utils import run_bass_kernel_spmd

    g = {k: np.asarray(v) for k, v in inputs.items()}
    a = {"x": _halves(g["x"]), "slots": _halves(g["L0_ffn_slots"])}
    a["idx"] = np.concatenate([g["src"].reshape(P, TE), g["dst"].reshape(P, TE)], axis=1)
    a["types"] = g["node_type_6"].reshape(1, N)
    a["ef"] = g["edge_attr_256"].reshape(P, TE * DE)
    a["ea"] = np.ascontiguousarray(g["edge_attr_32"].reshape(P, 4, 4, DA).transpose(2, 3, 1, 0)).reshape(P, 4 * P)
    a["ew1"] = g["L1_gnn_edge_W1"]
    a["We"] = np.ascontiguousarray(g["L0_gnn_We"].T.reshape(2, P, D).transpose(1, 0, 2)).reshape(P, 2 * D)
    a["Wn"] = _weight(g["L0_gnn_Wn"].T)
    for l in range(L):
        w = g["L0_gnn_W1"][l].T
        a[f"W1a{l}"], a[f"W1b{l}"], a[f"W2{l}"] = _weight(w[:D]), _weight(w[D:]), _weight(g["L0_gnn_W2"][l].T)
    for k, c in enumerate("qkv"):
        a[f"W{c}"] = _weight(g["L0_gnn_Wqkv"][k * D:(k + 1) * D].T)
    a["Wo"] = _weight(g["L0_gnn_Wo"].T)
    fc1 = g["L0_ffn_fc1_weight"].reshape(SB, 4, 2, 4, D, F).transpose(0, 2, 4, 1, 3, 5).reshape(NB, D, D)
    fc2 = g["L0_ffn_fc2_weight"].reshape(NB, NI, P, D).transpose(0, 2, 1, 3).reshape(NB, P, NI * D)
    for b in range(NB):
        a[f"fc1{b}"] = _weight(fc1[b])
        a[f"fc2{b}"] = fc2[b]
    for t in range(TYPES):
        a[f"Wt{t}"] = _weight(g["L1_gnn_W_type"][t])
    a["Wma"], a["Wmb"] = _weight(g["L1_gnn_msg_W1"][:D]), _weight(g["L1_gnn_msg_W1"][D:])
    for k, n in (("Wm2", "msg_W2"), ("Wg1", "agg_W1"), ("Wg2", "agg_W2"), ("Wout", "out_W")):
        a[k] = _weight(g["L1_gnn_" + n])
    a["w1"] = _weight(g["L1_ffn_w1"].transpose(1, 0, 2).reshape(D, X * R))
    a["w2"] = _weight(g["L1_ffn_w2"].reshape(X * R, D))
    a["encw"] = _weight(g["L1_ffn_enc_w"])
    a["sww"] = g["L1_ffn_sw_w"]

    bias = np.zeros((P, D), np.float32)
    bias[ROW_BE], bias[ROW_BN], bias[ROW_BO] = g["L0_gnn_be"], g["L0_gnn_bn"], g["L0_gnn_bo"]
    bias[ROW_B1:ROW_B1 + L], bias[ROW_B2:ROW_B2 + L] = g["L0_gnn_b1"], g["L0_gnn_b2"]
    bias[ROW_BQKV:ROW_BQKV + 3] = g["L0_gnn_bqkv"].reshape(3, D)
    bias[ROW_FC1:ROW_FC1 + NB] = g["L0_ffn_fc1_bias"].reshape(SB, 4, 2, 4, F).transpose(0, 2, 1, 3, 4).reshape(NB, D)
    bias[ROW_TYPE:ROW_TYPE + TYPES] = g["L1_gnn_b_type"]
    bias[ROW_MSG1], bias[ROW_MSG2] = g["L1_gnn_msg_b1"], g["L1_gnn_msg_b2"]
    bias[ROW_AGG1], bias[ROW_AGG2], bias[ROW_OUT] = g["L1_gnn_agg_b1"], g["L1_gnn_agg_b2"], g["L1_gnn_out_b"]
    bias[ROW_FFN1, 0:X * R] = g["L1_ffn_b1"].reshape(X * R)
    bias[ROW_EDGE1, 0:H4] = g["L1_gnn_edge_b1"]
    bias[ROW_EDGE1, H4:2 * H4] = g["L1_gnn_edge_b1"]
    bias[ROW_NORM], bias[ROW_LNG], bias[ROW_LNB] = g["L0_ffn_norm_weight"], g["L1_gnn_ln_g"], g["L1_gnn_ln_b"]
    bias[ROW_EDGE2, 0:2 * H4] = np.concatenate([g["L1_gnn_edge_W2"].reshape(H4)] * 2)
    bias[ROW_FFN2:ROW_FFN2 + X] = g["L1_ffn_b2"]
    bias[ROW_FC2:ROW_FC2 + N] = g["L0_ffn_fc2_bias"]
    a["bias"] = bias

    a["tail"] = np.concatenate([g["L1_ffn_sw_b"], g["L1_gnn_edge_b2"]]).reshape(1, X + 1)

    colp = np.zeros((P, COL_PACK), np.float32)
    for l in range(L):
        for i in range(NI):
            c = chunk(i)
            colp[:, C_G + l * NI + i] = g["L0_gnn_ln_g"][l, c * P:(c + 1) * P]
            colp[:, C_B + l * NI + i] = g["L0_gnn_ln_b"][l, c * P:(c + 1) * P]
    colp[0:R, C_ENCB] = g["L1_ffn_enc_b"]
    colp[0:N, C_SCALE] = g["L0_ffn_scale"]
    colp[N:P, C_SCALE] = g["L0_ffn_scale"]
    a["colp"] = colp

    nc = bacc.Bacc("TRN2", target_bir_lowering=False, num_devices=1)
    arrays, ins = {}, {}
    for name, v in a.items():
        v = np.ascontiguousarray(v)
        arrays[f"in_{name}"] = v
        ins[name] = nc.dram_tensor(f"in_{name}", v.shape, mybir.dt.from_np(v.dtype), kind="ExternalInput").ap()
    out = nc.dram_tensor("out", (P, HALF), mybir.dt.float32, kind="ExternalOutput").ap()
    build(nc, ins, out)
    r = run_bass_kernel_spmd(nc, [arrays], core_ids=[0])
    got = np.asarray(r.results[0]["out"])
    return np.ascontiguousarray(got.reshape(2, N, HALF).transpose(1, 0, 2)).reshape(N, D)
```

```python
import concourse.bass as bass
from concourse import mybir
from contextlib import ExitStack

N = 64
E = 2048
D = 768
HALF = D // 2
P = 128
NI = D // P
NJ = NI // 2
L = 3
DE = 256
DA = 32
H4 = D // 4
HEADS = 8
DH = D // HEADS
HJ = HEADS // 2
F = 48
TYPES = 6
R = 64
X = 8
TE = E // P
NB = N * F // D
SB = N // 32
Q = D // 4
SLOT = 3 * D
RING = 14
EPS = 1e-5

ROW_BE, ROW_BN, ROW_B1, ROW_B2, ROW_BQKV, ROW_BO, ROW_FC1 = 0, 1, 2, 5, 8, 11, 12
ROW_TYPE, ROW_MSG1, ROW_AGG1, ROW_AGG2, ROW_OUT, ROW_FFN1, ROW_EDGE1 = 16, 22, 23, 24, 25, 26, 27
ROW_NORM, ROW_LNG, ROW_LNB, ROW_EDGE2 = 28, 29, 30, 31
ROW_MSG2, ROW_FFN2, ROW_FC2 = 32, 33, 64

C_G, C_B, C_ENCB, C_SCALE = 0, L * NI, 2 * L * NI, 2 * L * NI + 1
COL_PACK = 2 * L * NI + 2


def chunk(i):
    return 3 * (i % 2) + i // 2


def load_order():
    order = [("ef", 0), ("ef", 1), ("We", 0), ("Wn", 0), ("Wn", 1)]
    for l in range(L):
        order += [(f"W1a{l}", 0), (f"W1a{l}", 1), (f"W1b{l}", 0), (f"W1b{l}", 1), (f"W2{l}", 0), (f"W2{l}", 1)]
    order += [(f"W{c}", k) for c in "qkvo" for k in range(2)]
    order += [(f"fc1{b}", k) for b in range(NB) for k in range(2)]
    order += [(f"fc2{b}", k) for b in range(NB) for k in range(2)]
    order += [(f"Wt{t}", k) for t in range(TYPES) for k in range(2)]
    order += [("Wm", k) for k in range(4)]
    order += [(w, k) for w in ("Wm2", "Wg1", "Wg2", "Wout", "w1", "w2") for k in range(2)]
    return order


def part_width(name):
    return {"ef": TE // 2 * DE, "We": 2 * D, "w1": 3 * X * R, "w2": 2 * D}.get(name, SLOT)


BY_CHUNK = [("Wt5", 1), ("Wm", 2), ("Wm", 3)]
LOADS = load_order()
LOAD = {part: k for k, part in enumerate(LOADS)}

COMBINES = ["x0", "slots", "l0", "l1", "l2", "f0", "tok", "g1", "go", "f1"]
POWERS = ["x0", "slots", "l0", "l1", "l2", "f0", "tok", "g1", "go", "f1"]
TURNS = ["x0", "edges", "slots", "l0", "l1", "l2", "nodes", "attn", "tok", "xn1", "h", "x3"]
CHAIN = ["Wm2", "Wg1", "Wg2", "Wout"]
LEFT = 2 * P
GATES = [2, 4, 6, 8]
CONSTS = ["ident", "iota", "mix", "blocks", "small", "pair", "fills", "slotmask", "probs"]


def build(nc, ins, out):
    fp32, bf16, i32, f32r = mybir.dt.float32, mybir.dt.bfloat16, mybir.dt.int32, mybir.dt.float32r
    ALU, ACT, AX = mybir.AluOpType, mybir.ActivationFunctionType, mybir.AxisListType
    ctx = ExitStack()
    with ctx:
        def sb(name, shape, dt=fp32):
            return ctx.enter_context(nc.sbuf_tensor(name, shape, dt))

        def bank(name):
            return ctx.enter_context(nc.psum_tensor(name, [P, 512], fp32))

        def sem(name):
            return ctx.enter_context(nc.semaphore(name))

        ring = sb("ring", [P, RING, SLOT])
        bias = sb("bias", [P, D])
        rows4 = sb("rows4", [P, 4, HALF])
        tail = sb("tail", [P, X + 1])
        colp = sb("colp", [P, COL_PACK])
        x0 = sb("x0", [P, HALF])
        x1 = sb("x1", [P, HALF])
        nodes = sb("nodes", [P, HALF])
        x2 = nodes
        row = sb("row", [P, HALF])
        keep = sb("keep", [P, HALF])
        hrow = sb("hrow", [P, HALF])
        tmp = sb("tmp", [P, HALF])
        cols = sb("cols", [P, NI, N])
        hbias = x0
        slots = sb("slots", [P, HALF])
        x3 = slots
        slots_t = sb("slots_t", [P, NI, N])
        edges2 = sb("edges2", [P, NJ, 4, N])
        comb = sb("comb", [P, NJ, 4, N])
        cols2 = comb[:, :, :, :].rearrange("p j q n -> p (j q) n")[:, 0:NI]
        spread = sb("spread", [P, 4, N])
        idx = sb("idx", [P, 2 * TE], i32)
        idxf = sb("idxf", [P, 2 * TE])
        types = sb("types", [P, N], i32)
        typesf = sb("typesf", [P, N])
        typemask = sb("typemask", [P, TYPES, N])
        typesel = sb("typesel", [P, N])
        irow_i = sb("irow_i", [P, N], i32)
        irow = sb("irow", [P, N])
        icol_i = sb("icol_i", [P, 1], i32)
        icol = sb("icol", [P, 1])
        ramp_i = sb("ramp_i", [P, X], i32)
        ramp = sb("ramp", [P, X])
        pair = sb("pair", [P, E], f32r)
        pq = sb("pq", [P, 2, D], f32r)
        ident_b = sb("ident_b", [P, P], bf16)
        to_dst = sb("to_dst", [P, TE, N])
        ones_b = sb("ones_b", [P, 1], bf16)
        degsel = sb("degsel", [P, N])
        gatesel = sb("gatesel", [P, N])
        routesel = sb("routesel", [P, N])
        ident = sb("ident", [P, P])
        swap2 = sb("swap2", [P, P])
        sum2 = sb("sum2", [P, P])
        pairup = sb("pairup", [P, N])
        nhalf = sb("nhalf", [P, 1])
        slotmask = sb("slotmask", [P, NJ, P], bf16)
        stat6 = sb("stat6", [P, 12])
        mv = sb("mv", [P, len(COMBINES), 2])
        pin = sb("pin", [P, len(POWERS)])
        pout = sb("pout", [P, len(POWERS)])
        small = sb("small", [P, 8])
        ea = sb("ea", [P, 4, P])
        ew1 = sb("ew1", [P, 4 * H4])
        gate_in = sb("gate_in", [P, TE])
        gate_z = sb("gate_z", [P, TE])
        gate_e = sb("gate_e", [P, TE])
        gate_d = sb("gate_d", [P, TE])
        gate = sb("gate", [P, TE])
        encw = sb("encw", [P, NI, R])
        sww = sb("sww", [R, X])
        big = sb("big", [P, 2048 + 4 * HALF])
        ends_b = big[:, 0:1024].bitcast(bf16).rearrange("p (t a n) -> p t a n", t=TE, a=2)
        both_b = big[:, 1024:2048].bitcast(bf16).rearrange("p (t a n) -> p t a n", t=TE, a=2)
        ehid = big[:, 2048:2048 + 4 * H4].rearrange("p (k c) -> p k c", k=2)
        eprod = big[:, 2048 + 4 * H4:2048 + 8 * H4].rearrange("p (k c) -> p k c", k=2)
        qt = big[0:DH, 0:HJ * P].rearrange("p (j n) -> p j n", j=HJ)
        kt = big[0:DH, HJ * P:2 * HJ * P].rearrange("p (j n) -> p j n", j=HJ)
        qrow = big[:, 1024:1024 + HALF]
        krow = big[:, 1408:1408 + HALF]
        vrow = big[:, 1792:1792 + HALF]
        shifted = big[:, 2176:2432].rearrange("p (j m) -> p j m", j=HJ)
        probs = big[:, 2432:2944].rearrange("p (j m) -> p j m", j=HJ)
        probs_t = big[:, 2944:3456].rearrange("p (j m) -> p j m", j=HJ)
        hid = big[:, 0:SB * HALF].rearrange("p (b c) -> p b c", b=SB)
        hid_t = big[:, SB * HALF:2 * SB * HALF].rearrange("p (b j n) -> p b j n", b=SB, j=NJ)
        mixed = big[:, 2 * SB * HALF:2 * SB * HALF + SB * Q].rearrange("p (b c) -> p b c", b=SB)
        typed = big[:, 0:TYPES * HALF].rearrange("p (t i n) -> p t i n", t=TYPES, i=NI)
        msg = big[:, 0:3 * D].rearrange("p (k c) -> p k c", k=3)
        combine_w = edges2[:, :, :, :].rearrange("p j q n -> p (j q n)")[:, 0:2 * SB * P].rearrange("p (q k n) -> p q k n", q=2, k=SB)
        dispatch_w = sb("dispatch_w", [P, P])
        soft = sb("soft", [P, N])
        soft2 = sb("soft2", [P, 1 + SB, P])
        mx = sb("mx", [P, HJ])
        ssum = sb("ssum", [P, HJ])
        rsum = sb("rsum", [P, HJ])
        enc_t = sb("enc_t", [R, 2, N])
        lg = sb("lg", [P, X])
        route_e = sb("route_e", [P, X])
        cand = sb("cand", [P, X])
        route4 = sb("route4", [P, X // 2])
        route_pad = sb("route_pad", [N, P])

        T = [bank(f"T{k}") for k in range(3)]
        ACC = [bank(f"ACC{k}") for k in range(4)]
        SM = bank("SM")
        chain_acc = [(ACC[1], ACC[3]), (ACC[2], T[2])]

        arrived = [sem(f"arrived{k}") for k in range(RING)]
        ring_used = sem("ring_used")
        x_in, idx_in, type_in, bias_in, col_in, tail_in = (sem(n) for n in ("x_in", "idx_in", "type_in", "bias_in", "col_in", "tail_in"))
        ew1_clear = sem("ew1_clear")
        rows_made, rows_kept = sem("rows_made"), sem("rows_kept")
        slots_in, ea_in, ew1_in, encw_in, sww_in = (sem(n) for n in ("slots_in", "ea_in", "ew1_in", "encw_in", "sww_in"))
        chunk_in = {part: [sem(f"chunk_in_{part[0]}_{part[1]}_{i}") for i in range(3)] for part in BY_CHUNK}
        out_done = sem("out_done")
        consts_made, pool_link = sem("consts_made"), sem("pool_link")
        dve_link = sem("dve_link")
        stats_ready, combined, power_asked, power_done = sem("stats_ready"), sem("combined"), sem("power_asked"), sem("power_done")
        rows_ready, turned_a, turned_b, cols_a, cols_b = sem("rows_ready"), sem("turned_a"), sem("turned_b"), sem("cols_a"), sem("cols_b")
        onehots, onehot_copy, sums_made, spread_ready = sem("onehots"), sem("onehot_copy"), sem("sums_made"), sem("spread_ready")
        edges_made, edges_kept = sem("edges_made"), sem("edges_kept")
        nodes_ready, comb_made, comb_ready = sem("nodes_ready"), sem("comb_made"), sem("comb_ready")
        gate_made, gate_relu, gate_mult, gate_red = sem("gate_made"), sem("gate_relu"), sem("gate_mult"), sem("gate_red")
        gate_asked, gate_exp, gate_ready, gsum_made, gsum_ready = sem("gate_asked"), sem("gate_exp"), sem("gate_ready"), sem("gsum_made"), sem("gsum_ready")
        q_row, k_row, v_row, heads_turned, q_cols, k_cols = (sem(n) for n in ("q_row", "k_row", "v_row", "heads_turned", "q_cols", "k_cols"))
        scores_made, scores_shift, probs_made, probs_turned = sem("scores_made"), sem("scores_shift"), sem("probs_made"), sem("probs_turned")
        probs_a, probs_b, attn_made = sem("probs_a"), sem("probs_b"), sem("attn_made")
        logits_made, logits_max, soft_made, soft_ready, soft_turned = sem("logits_made"), sem("logits_max"), sem("soft_made"), sem("soft_ready"), sem("soft_turned")
        weights_act, weights_dve, mixed_made, mixed_a, mixed_b = sem("weights_act"), sem("weights_dve"), sem("mixed_made"), sem("mixed_a"), sem("mixed_b")
        hid_made, hid_turned, hid_masked, y_ready, mix_out = sem("hid_made"), sem("hid_turned"), sem("hid_masked"), sem("y_ready"), sem("mix_out")
        typed_ready, typesel_ready = sem("typed_ready"), sem("typesel_ready")
        pair_turned, pq_left, pq_round, pq_rest = (sem(n) for n in ("pair_turned", "pq_left", "pq_round", "pq_rest"))
        tail_bias = sem("tail_bias")
        left_made, left_ready, left_turned, left_cols = (sem(n) for n in ("left_made", "left_ready", "left_turned", "left_cols"))
        right_ready, right_turned, right_cols = (sem(n) for n in ("right_ready", "right_turned", "right_cols"))
        pair_ready, gathered_left, gathered_right, msg_act, msg_dve, scattered = sem("pair_ready"), sem("gathered_left"), sem("gathered_right"), sem("msg_act"), sem("msg_dve"), sem("scattered")
        enc_made, enc_ready, route_made, route_max, route_exp = sem("enc_made"), sem("enc_ready"), sem("route_made"), sem("route_max"), sem("route_exp")
        route_ready, route_turned, routesel_ready = sem("route_ready"), sem("route_turned"), sem("routesel_ready")
        w1_made, exp_ready, left_used = sem("w1_made"), sem("exp_ready"), sem("left_used")
        gelu_made, exp_turned, exp_cols, final_ready = sem("gelu_made"), sem("exp_turned"), sem("exp_cols"), sem("final_ready")

        def used(name, part=1):
            return LOAD[name, part] + 1

        def slot(name, part):
            k = LOAD[name, part]
            return ring[:, k % RING, 0:part_width(name)]

        def at(names, name):
            return names.index(name) + 1

        def halves(ap, n=HALF):
            return [(h, ap[h * N:(h + 1) * N, 0:n]) for h in range(2)]

        block = ctx.enter_context(nc.Block())

        @block.sync
        def _(sp):
            sp.dma_start(x0[:, :], ins["x"]).then_inc(x_in, 16)
            for k, (name, part) in enumerate(LOADS):
                if k >= RING:
                    sp.wait_ge(ring_used, k - RING + 1)
                src = ins[name]
                w = part_width(name)
                if (name, part) in BY_CHUNK:
                    for i in range(3):
                        cs = slice(i * D, (i + 1) * D)
                        sp.dma_start(slot(name, part)[:, cs], src[:, part * w:(part + 1) * w][:, cs])\
                            .then_inc(chunk_in[name, part][i], 16)
                    if (name, part) == ("Wm", 3):
                        sp.dma_start(encw[:, :, :], ins["encw"].rearrange("p (i r) -> p i r", i=NI)).then_inc(encw_in, 16)
                        sp.dma_start(sww[:, :], ins["sww"]).then_inc(sww_in, 16)
                    continue
                sp.dma_start(slot(name, part), src[:, part * w:(part + 1) * w]).then_inc(arrived[k % RING], 16)
                if (name, part) == ("Wn", 0):
                    sp.wait_ge(ew1_clear, 1)
                    for t in range(4):
                        sp.dma_start(ew1[t * DA:(t + 1) * DA, t * H4:(t + 1) * H4], ins["ew1"]).then_inc(ew1_in, 16)
                    sp.dma_start(ea[:, :, :], ins["ea"].rearrange("p (g e) -> p g e", g=4)).then_inc(ea_in, 16)
            sp.wait_ge(final_ready, 1)
            sp.dma_start(out, row[:, :]).then_inc(out_done, 16)
            sp.wait_ge(out_done, 16)

        @block.gpsimd
        def _(pool):
            links = [0]

            def link(op):
                links[0] += 1
                op.then_inc(pool_link, 1)
                pool.wait_ge(pool_link, links[0])

            made = [0]

            def done(op):
                made[0] += 1
                op.then_inc(consts_made, 1)
                pool.wait_ge(consts_made, made[0])

            def diagonal(ap, base, pattern, fill):
                return nc.gpsimd.affine_select(out=ap, in_=ap, pattern=pattern, compare_op=ALU.not_equal, fill=fill,
                                               base=base, channel_multiplier=1)

            link(nc.gpsimd.memset(ident[:, :], 0.0))
            done(diagonal(ident[:, :], 0, [[-1, P]], 1.0))
            done(nc.gpsimd.iota(irow_i[:, :], pattern=[[1, N]], base=0, channel_multiplier=0))
            link(nc.gpsimd.memset(swap2[:, :], 0.0))
            link(nc.gpsimd.memset(sum2[:, :], 0.0))
            link(nc.gpsimd.memset(nhalf[:, :], -0.5))
            link(diagonal(swap2[0:N, N:P], 0, [[-1, N]], 1.0))
            done(diagonal(swap2[N:P, 0:N], 0, [[-1, N]], 1.0))

            def power(name):
                k = POWERS.index(name)
                pool.wait_ge(power_asked, k + 1)
                nc.gpsimd.tensor_tensor(pout[:, k:k + 1], pin[:, k:k + 1], nhalf[:, :], ALU.pow).then_inc(power_done, 1)

            power("x0")
            link(nc.gpsimd.memset(spread[:, :, :], 0.0))
            link(diagonal(spread[0:N, 0, :], 0, [[-1, N]], 1.0))
            done(diagonal(spread[N:P, 2, :], 0, [[-1, N]], 1.0))
            for h in range(2):
                link(diagonal(sum2[h * N:(h + 1) * N, :].rearrange("p (a n) -> p a n", a=2), 0, [[0, 2], [-1, N]], 1.0))
            link(nc.gpsimd.iota(icol_i[:, :], pattern=[[0, 1]], base=-ROW_TYPE, channel_multiplier=1))
            link(nc.gpsimd.iota(ramp_i[:, :], pattern=[[-1, X]], base=X, channel_multiplier=0))
            link(nc.gpsimd.memset(ones_b[:, :], 1.0))
            link(nc.gpsimd.memset(degsel[:, :], 0.0))
            done(nc.gpsimd.memset(gatesel[:, :], 0.0))
            link(nc.gpsimd.memset(pairup[:, :], 0.0))
            link(diagonal(pairup[0:N, :], 0, [[-1, N]], 1.0))
            done(diagonal(pairup[N:P, :], 0, [[-1, N]], 1.0))
            done(nc.gpsimd.memset(edges2[:, :, :, :], 0.0))
            power("slots")
            link(nc.gpsimd.memset(dispatch_w[:, :], 0.0))
            link(nc.gpsimd.memset(route_pad[:, :], 0.0))
            link(nc.gpsimd.memset(slotmask[:, :, :], 1.0))
            mask4 = slotmask[:, :, :].rearrange("p j (g s) -> p j g s", g=4)
            link(nc.gpsimd.affine_select(out=mask4, in_=mask4, pattern=[[P, NJ], [HALF, 4], [-F, 32]],
                                         compare_op=ALU.is_ge, fill=0.0, base=0, channel_multiplier=1))
            done(nc.gpsimd.affine_select(out=mask4, in_=mask4, pattern=[[-P, NJ], [-HALF, 4], [F, 32]],
                                         compare_op=ALU.is_ge, fill=0.0, base=F - 1, channel_multiplier=-1))

            def gate_products(first, last):
                for u in range(first, last):
                    pool.wait_ge(gate_relu, u + 1)
                    if u >= 2:
                        pool.wait_ge(gate_red, u - 1)
                    nc.gpsimd.tensor_tensor(eprod[:, u % 2, :], ehid[:, u % 2, :], rows4[:, 3, :], ALU.mult).then_inc(gate_mult, 1)

            pool.wait_ge(rows_kept, 1)
            gate_products(0, GATES[0])
            for l in range(L):
                power(f"l{l}")
                gate_products(GATES[l], GATES[l + 1])
            pool.wait_ge(gate_red, TE // 2)
            link(nc.gpsimd.memset(combine_w, 0.0))
            done(nc.gpsimd.memset(probs, 0.0))
            for name in POWERS[POWERS.index("f0"):]:
                power(name)

        @block.tensor
        def _(pe):
            def mm(o, lhsT, rhs, start=True, stop=True):
                return nc.tensor.matmul(o, lhsT, rhs, start=start, stop=stop)

            def ready(name, part):
                k = LOAD[name, part]
                whole = [LOADS[m] not in BY_CHUNK for m in range(k % RING, k + 1, RING)]
                pe.wait_ge(arrived[k % RING], 16 * sum(whole))

            def combine(name, pieces=1):
                pe.wait_ge(stats_ready, COMBINES.index(name) + 1)
                mm(SM[:, 0:6 * pieces], ident[:, :], stat6[:, 0:6 * pieces])
                mm(SM[:, 6 * pieces:12 * pieces], swap2[:, :], stat6[:, 0:6 * pieces]).then_inc(combined, 1)

            def combine_sums(name):
                k = COMBINES.index(name)
                pe.wait_ge(stats_ready, k + 1)
                mm(SM[:, 0:1], sum2[:, :], mv[:, k, 0:1]).then_inc(combined, 1)

            def turn(name, src):
                pe.wait_ge(rows_ready, at(TURNS, name))
                for j in range(NJ):
                    o = T[j // 2][:, (j % 2) * P:(j % 2 + 1) * P]
                    last = nc.tensor.transpose(o, src[:, j * P:(j + 1) * P], ident[:, :])
                    if j == 1:
                        last.then_inc(turned_a, 1)
                last.then_inc(turned_b, 1)

            def pick(k, n=N):
                return ident[:, k:k + 1].to_broadcast([P, n])

            def add_bias(acc, k, stat=None, width=HALF, end=False):
                for h in range(2):
                    last = mm(acc[h * N:(h + 1) * N, 0:width], pick(k) if stat is None else stat,
                              bias[:, h * width:(h + 1) * width], True, end)
                return last

            def product(acc, stationary, name, turn_name=None, first=False, end=True, width=HALF, per=3, n=NI):
                for i in range(n):
                    if turn_name and i == 0:
                        pe.wait_ge(cols_a, at(TURNS, turn_name))
                    if turn_name and i == 4:
                        pe.wait_ge(cols_b, at(TURNS, turn_name))
                    if (name, i // per) in BY_CHUNK:
                        pe.wait_ge(chunk_in[name, i // per][i % per], 16)
                    elif i % per == 0:
                        ready(name, i // per)
                    w = slot(name, i // per).rearrange("p (i c) -> p i c", i=per)
                    for h in range(2):
                        last = mm(acc[h * N:(h + 1) * N, 0:width], stationary(i),
                                  w[:, i % per, h * width:(h + 1) * width], first and i == 0, end and i == n - 1)
                    if i % per == per - 1:
                        last.then_inc(ring_used, 1)

            def chunks(t):
                return lambda i: t[:, i, :]

            def edge_sums(part):
                ready("ef", part)
                ef = slot("ef", part).rearrange("p (t c) -> p t c", c=DE)
                for t in range(TE // 2):
                    tt = part * TE // 2 + t
                    h = t % 2
                    last = mm(ACC[1][h * N:(h + 1) * N, 0:DE], to_dst[:, tt, :], ef[:, t, :], tt < 2, tt >= TE - 2)
                last.then_inc(ring_used, 1)

            pe.wait_ge(consts_made, at(CONSTS, "mix"))
            combine("x0")
            pe.wait_ge(onehot_copy, 1)
            edge_sums(0)
            turn("x0", row)
            pe.wait_ge(onehots, 1)
            for t in range(TE):
                mm(ACC[3][:, 0:N], both_b[:, t, :, :], ends_b[:, t, 1, :], t == 0, t == TE - 1)
            pe.wait_ge(consts_made, at(CONSTS, "small"))
            for t in range(TE):
                last = mm(ACC[3][0:1, N:2 * N], ones_b[:, :], ends_b[:, t, 1, :], t == 0, t == TE - 1)
            last.then_inc(sums_made, 1)
            edge_sums(1)
            pe.wait_ge(edges_kept, 1)
            pe.wait_ge(consts_made, at(CONSTS, "pair"))
            for c in range(2):
                last = mm(ACC[2][:, c * N:(c + 1) * N], tmp[:, c * P:(c + 1) * P], pairup[:, :])
            last.then_inc(edges_made, 1)
            pe.wait_ge(spread_ready, 1)
            pe.wait_ge(bias_in, 16)
            add_bias(ACC[1], None, degsel[:, :])
            pe.wait_ge(edges_kept, 2)
            ready("We", 0)
            we = slot("We", 0).rearrange("p (c n) -> p c n", c=2)
            for c in range(2):
                for h in range(2):
                    last = mm(ACC[1][h * N:(h + 1) * N, 0:HALF], hrow[:, c * N:(c + 1) * N],
                              we[:, c, h * HALF:(h + 1) * HALF], False, c == 1)
            last.then_inc(ring_used, 1)
            pe.wait_ge(cols_a, at(TURNS, "x0"))
            pe.wait_ge(cols_b, at(TURNS, "x0"))
            turn("edges", tmp)
            add_bias(ACC[0], ROW_BN)
            combine_sums("slots")
            mm(ACC[3][:, 0:2 * H4], pick(ROW_EDGE2, P), bias[:, 0:2 * H4]).then_inc(rows_made, 1)
            pe.wait_ge(cols_a, at(TURNS, "edges"))
            pe.wait_ge(cols_b, at(TURNS, "edges"))
            turn("slots", slots)
            pe.wait_ge(onehots, 2)
            for k in range(2):
                for t in range(TE // 2):
                    last = nc.tensor.transpose(ACC[1 + k][:, :].bitcast(bf16)[:, t * P:(t + 1) * P],
                                               ends_b[:, k * TE // 2 + t, :, :], ident_b[:, :])
                last.then_inc(pair_turned, 1)
            product(ACC[0], chunks(cols), "Wn")
            pe.wait_ge(cols_a, at(TURNS, "slots"))
            pe.wait_ge(cols_b, at(TURNS, "slots"))

            def gate_hidden(first, last):
                for u in range(first, last):
                    acc = ACC[2 + u % 2]
                    if u >= 2:
                        pe.wait_ge(gate_relu, u - 1)
                    mm(acc[:, 0:2 * H4], pick(ROW_EDGE1, P), bias[:, 0:2 * H4], True, False)
                    mm(acc[:, 0:2 * H4], ea[:, u // 2, :], ew1[:, (u % 2) * 2 * H4:(u % 2 + 1) * 2 * H4], False, True)\
                        .then_inc(gate_made, 1)

            pe.wait_ge(pair_ready, 2)
            pe.wait_ge(rows_kept, 1)
            pe.wait_ge(ea_in, 16)
            pe.wait_ge(ew1_in, 64)
            for l in range(L):
                add_bias(ACC[1], ROW_B1 + l)
                if l == 0:
                    gate_hidden(0, GATES[0])
                pe.wait_ge(nodes_ready, l + 1)
                for j in range(NJ):
                    mm(T[j][:, 0:4 * N], nodes[:, j * P:(j + 1) * P], spread[:, :, :]).then_inc(comb_made, 1)
                pe.wait_ge(comb_ready, NJ * (l + 1))
                product(ACC[1], lambda i: comb[:, i // 2, 2 * (i % 2), :], f"W1a{l}", end=False)
                product(ACC[1], lambda i: comb[:, i // 2, 2 * (i % 2) + 1, :], f"W1b{l}")
                gate_hidden(GATES[l], GATES[l] + 1)
                combine(f"l{l}")
                gate_hidden(GATES[l] + 1, GATES[l + 1])
                add_bias(ACC[0], ROW_B2 + l)
                turn(f"l{l}", row)
                product(ACC[0], chunks(cols), f"W2{l}", f"l{l}")

            add_bias(ACC[1], ROW_BQKV + 1)
            turn("nodes", nodes)
            add_bias(ACC[0], ROW_BQKV)
            for k, c in enumerate("qkv"):
                if k == 2:
                    pe.wait_ge(gate_relu, TE // 2)
                    add_bias(ACC[2], ROW_BQKV + 2)
                product(ACC[k], chunks(cols), f"W{c}", "nodes")
            for k, (src, there) in enumerate(((qrow, q_row), (krow, k_row))):
                pe.wait_ge(there, 1)
                for j in range(HJ):
                    last = nc.tensor.transpose(T[k][0:DH, j * P:(j + 1) * P], src[:, j * DH:(j + 1) * DH], ident[:, :])
                last.then_inc(heads_turned, 1)
            pe.wait_ge(q_cols, 1)
            pe.wait_ge(k_cols, 1)
            for j in range(HJ):
                for h in range(2):
                    last = mm(ACC[0][h * N:(h + 1) * N, j * N:(j + 1) * N], qt[:, j, h * N:(h + 1) * N],
                              kt[:, j, h * N:(h + 1) * N])
            last.then_inc(scores_made, 1)
            pe.wait_ge(probs_made, 2)
            for k in range(2):
                for j in range(2):
                    last = nc.tensor.transpose(T[k][:, j * P:(j + 1) * P], probs[:, 2 * k + j, :], ident[:, :])
                last.then_inc(probs_turned, 1)
            pe.wait_ge(v_row, 1)
            pe.wait_ge(probs_a, 1)
            pe.wait_ge(probs_b, 1)
            for j in range(HJ):
                last = mm(ACC[1][:, j * DH:(j + 1) * DH], probs_t[:, j, :], vrow[:, j * DH:(j + 1) * DH])
            last.then_inc(attn_made, 1)
            add_bias(ACC[2], ROW_BO)
            turn("attn", row)
            product(ACC[2], chunks(cols), "Wo", "attn")
            for k in range(2):
                add_bias(ACC[3 * (1 - k)], ROW_NORM + k, end=True).then_inc(rows_made, 1)
            combine("f0")
            pe.wait_ge(rows_kept, 2)
            add_bias(ACC[3], ROW_NORM + 2, end=True).then_inc(rows_made, 1)
            combine_sums("tok")
            turn("tok", row)
            pe.wait_ge(cols_a, at(TURNS, "tok"))
            pe.wait_ge(cols_b, at(TURNS, "tok"))
            pe.wait_ge(rows_kept, 3)
            for i in range(NI):
                mm(ACC[0][0:N, 0:N], cols[:, i, :], slots_t[:, i, :], i == 0, i == NI - 1)
                last = mm(ACC[0][N:P, 0:N], slots_t[:, i, :], cols[:, i, :], i == 0, i == NI - 1)
            last.then_inc(logits_made, 1)
            pe.wait_ge(gate_ready, 1)
            for t in range(TE):
                last = mm(SM[ROW_MSG2:ROW_MSG2 + 1, 0:N], gate[:, t:t + 1], to_dst[:, t, :], t == 0, t == TE - 1)
            last.then_inc(gsum_made, 1)
            pe.wait_ge(soft_ready, 1)
            for k in range(1 + SB):
                last = nc.tensor.transpose(T[0][:, k * P:(k + 1) * P], soft2[:, k, :], ident[:, :])
            last.then_inc(soft_turned, 1)
            pe.wait_ge(weights_act, 1)
            pe.wait_ge(weights_dve, 1)
            for j in range(NJ):
                last = mm(T[1 + j // 2][:, (j % 2) * P:(j % 2 + 1) * P], keep[:, j * P:(j + 1) * P], dispatch_w[:, :])
            last.then_inc(mixed_made, 1)

            def fc1(b):
                for g in range(4):
                    mm(ACC[b][32 * g:32 * g + 32, 0:Q], pick(ROW_FC1 + b, 32), bias[:, g * Q:(g + 1) * Q], True, False)
                if b == 0:
                    pe.wait_ge(mixed_a, 1)
                    pe.wait_ge(mixed_b, 1)
                for i in range(NI):
                    if i % 3 == 0:
                        ready(f"fc1{b}", i // 3)
                    w = slot(f"fc1{b}", i // 3).rearrange("p (i c) -> p i c", i=3)
                    for g in range(4):
                        last = mm(ACC[b][32 * g:32 * g + 32, 0:Q], cols[:, i, b // 2 * 32:b // 2 * 32 + 32],
                                  w[:, i % 3, g * Q:(g + 1) * Q], False, i == NI - 1)
                    if i % 3 == 2:
                        last.then_inc(ring_used, 1)

            def turn_hidden(k):
                pe.wait_ge(hid_made, 2 * k + 2)
                for j in range(NJ):
                    last = nc.tensor.transpose(T[1 + k][:, j * P:(j + 1) * P], hid[:, k, j * P:(j + 1) * P], ident[:, :])
                last.then_inc(hid_turned, 1)

            fc1(0)
            fc1(1)
            fc1(2)
            turn_hidden(0)
            pe.wait_ge(rows_kept, 4)
            fc1(3)
            for k in range(SB):
                pe.wait_ge(hid_made, 2 * k + 2)
                for c in range(4):
                    mm(ACC[k][32 * c:32 * c + 32, 0:Q], ident[:, ROW_FC2 + 32 * k:ROW_FC2 + 32 * k + 32],
                       bias[:, c * Q:(c + 1) * Q], True, False)
                pe.wait_ge(hid_masked, k + 1)
                for g in range(4):
                    name, part = f"fc2{2 * k + g // 2}", g % 2
                    ready(name, part)
                    w = slot(name, part).rearrange("p (j c) -> p j c", j=NJ)
                    for j in range(NJ):
                        for c in range(4):
                            last = mm(ACC[k][32 * c:32 * c + 32, 0:Q], hid_t[:, k, j, 32 * g:32 * g + 32],
                                      w[:, j, c * Q:(c + 1) * Q], False, g == 3 and j == NJ - 1)
                    last.then_inc(ring_used, 1)
                    if k == 0 and g == 0:
                        turn_hidden(1)
            pe.wait_ge(weights_act, 5)
            for k in range(SB):
                pe.wait_ge(y_ready, k + 1)
                for q in range(2):
                    last = mm(ACC[2 + q][:, 0:Q], combine_w[:, q, k, :], mixed[:, k, :], k == 0, k == SB - 1)
            last.then_inc(mix_out, 1)

            pe.wait_ge(typesel_ready, 1)
            add_bias(ACC[0], None, typesel[:, :])
            combine("g1")
            add_bias(T[2], ROW_AGG2, end=True)
            add_bias(ACC[3], ROW_OUT, end=True).then_inc(tail_bias, 1)
            for f in range(2):
                mm(ACC[1 + f][N:P, 0:HALF], pick(ROW_MSG1), bias[:, f * HALF:(f + 1) * HALF], True, False)
            turn("xn1", keep)
            for t in range(TYPES):
                pe.wait_ge(typed_ready, t + 1)
                product(ACC[0], lambda i: typed[:, t, i, :], f"Wt{t}", end=t == TYPES - 1)
            turn("h", hrow)
            pe.wait_ge(cols_a, at(TURNS, "h"))
            pe.wait_ge(cols_b, at(TURNS, "h"))

            def pq_product(k):
                if ("Wm", k) not in BY_CHUNK:
                    ready("Wm", k)
                w = slot("Wm", k).rearrange("p (i a c) -> p i a c", i=3, a=2)
                f = k // 2
                for i in range(3 * (k % 2), 3 * (k % 2) + 3):
                    if k == 3:
                        pe.wait_ge(pq_left, 1)
                        gather(i % 3, 0)
                    if ("Wm", k) in BY_CHUNK:
                        pe.wait_ge(chunk_in["Wm", k][i % 3], 16)
                    mm(ACC[1 + f][0:N, 0:HALF], cols[:, i, :], w[:, i % 3, 0, :], i == 0, i == NI - 1)
                    last = mm(ACC[1 + f][N:P, 0:HALF], cols[:, i, :], w[:, i % 3, 1, :], False, i == NI - 1)
                last.then_inc(ring_used, 1)

            banks = [(T[0], T[1]), (T[2], SM), (ACC[3], ACC[1])]

            def gather(t, f):
                if t >= 3:
                    pe.wait_ge((msg_act, msg_dve)[f], t - 2)
                for k in range(2):
                    if t == 0 and f == 1:
                        pe.wait_ge((pq_round, pq_rest)[k], 1)
                    last = mm(banks[t % 3][f][:, 0:HALF], pair[:, t * P:(t + 1) * P],
                              pq[:, k, f * HALF:(f + 1) * HALF], k == 0, k == 1)
                last.then_inc((gathered_left, gathered_right)[f], 1)

            def scatter(t):
                pe.wait_ge(msg_act, t + 1)
                pe.wait_ge(msg_dve, t + 1)
                for h in range(2):
                    last = mm(ACC[0][h * N:(h + 1) * N, 0:HALF], to_dst[:, t, :], msg[:, t % 3, h * HALF:(h + 1) * HALF],
                              t == 0, t == TE - 1)
                last.then_inc(scattered, 1)

            for k in range(4):
                pq_product(k)
            gather(0, 1)
            gather(1, 1)
            for t in range(TE):
                if t + 2 < TE:
                    if t > 0:
                        gather(t + 2, 0)
                    gather(t + 2, 1)
                scatter(t)

            def turn_left(src):
                n = turns[0]
                pe.wait_ge(left_ready, n + 1)
                for j in range(2):
                    last = nc.tensor.transpose(T[0][:, j * P:(j + 1) * P], src[:, j * P:(j + 1) * P], ident[:, :])
                last.then_inc(left_turned, 1)

            def turn_right(src):
                n = turns[0]
                pe.wait_ge(right_ready, n + 1)
                nc.tensor.transpose(T[1][:, 0:P], src[:, LEFT:HALF], ident[:, :]).then_inc(right_turned, 1)
                turns[0] += 1

            turns = [0]
            pe.wait_ge(gsum_ready, 1)
            def chain_bias(n, stat):
                for side, (lo, hi) in enumerate(((0, LEFT), (LEFT, HALF))):
                    for h in range(2):
                        mm(chain_acc[n % 2][side][h * N:(h + 1) * N, 0:hi - lo], stat,
                           bias[:, h * HALF + lo:h * HALF + hi], True, False)

            chain_bias(0, gatesel[:, :])
            turn_left(row)
            turn_right(row)
            chain_bias(1, pick(ROW_AGG1))
            for n, name in enumerate(CHAIN):
                turned = (cols, cols2)[n % 2]
                for side, (lo, hi) in enumerate(((0, LEFT), (LEFT, HALF))):
                    for i in range(NI):
                        if side == 0 and i == 0:
                            pe.wait_ge(left_cols, n + 1)
                        if side == 0 and i == 4:
                            pe.wait_ge(right_cols, n + 1)
                        if side == 0 and i % 3 == 0:
                            ready(name, i // 3)
                        if side == 0 and i == 2 and n > 0:
                            turn_right(row)
                        if side == 1 and i == 3 and n < len(CHAIN) - 1:
                            turn_left(row)
                        w = slot(name, i // 3).rearrange("p (i c) -> p i c", i=3)
                        for h in range(2):
                            last = mm(chain_acc[n % 2][side][h * N:(h + 1) * N, 0:hi - lo], turned[:, i, :],
                                      w[:, i % 3, h * HALF + lo:h * HALF + hi], n >= 2 and i == 0, i == NI - 1)
                        if side == 1 and i % 3 == 2:
                            last.then_inc(ring_used, 1)
                    if side == 0:
                        last.then_inc(left_made, 1)
            for side in range(2):
                if side == 1:
                    pe.wait_ge(left_used, 1)
                for h in range(2):
                    c0 = h * 4 * R + side * 2 * R
                    mm(ACC[2 * side][h * N:(h + 1) * N, 0:2 * R], pick(ROW_FFN1), bias[:, c0:c0 + 2 * R], True, False)

            def keep_warm(n):
                for _ in range(n):
                    mm(T[0][:, 0:P], ident[:, :], ident[:, :])

            combine("go", 2)
            keep_warm(11)

            combine("f1")
            keep_warm(7)
            turn("x3", row)
            pe.wait_ge(encw_in, 16)
            pe.wait_ge(cols_a, at(TURNS, "x3"))
            pe.wait_ge(cols_b, at(TURNS, "x3"))
            for i in range(NI):
                last = mm(ACC[3][0:R, 0:N], encw[:, i, :], cols[:, i, :], i == 0, i == NI - 1)
            last.then_inc(enc_made, 1)
            def exp_turn(j):
                pe.wait_ge(exp_ready, j + 1)
                nc.tensor.transpose(T[j][:, 0:P], tmp[:, j * P:(j + 1) * P], ident[:, :]).then_inc(exp_turned, 1)

            for side in range(2):
                for i in range(NI):
                    if side == 0 and i % 3 == 0:
                        ready("w1", i // 3)
                    if side == 0 and i == 3:
                        pe.wait_ge(enc_ready, 1)
                        pe.wait_ge(sww_in, 16)
                        mm(T[2][:, 0:X], enc_t[:, :, :], sww[:, :]).then_inc(route_made, 1)
                    if side == 1 and i == 4:
                        pe.wait_ge(route_ready, 1)
                        nc.tensor.transpose(ACC[3][:, 0:N], route_pad[:, :], ident[0:N, 0:N]).then_inc(route_turned, 1)
                        exp_turn(0)
                    w = slot("w1", i // 3).rearrange("p (i c) -> p i c", i=3)
                    for h in range(2):
                        c0 = h * 4 * R + side * 2 * R
                        last = mm(ACC[2 * side][h * N:(h + 1) * N, 0:2 * R], cols[:, i, :], w[:, i % 3, c0:c0 + 2 * R],
                                  False, i == NI - 1)
                    if side == 1 and i % 3 == 2:
                        last.then_inc(ring_used, 1)
                if side == 0:
                    last.then_inc(w1_made, 1)
            def exp_product(side, j):
                acc, lo, hi = ((ACC[1], 0, LEFT), (T[2], LEFT, HALF))[side]
                w = slot("w2", j).rearrange("p (i c) -> p i c", i=2)
                for i in range(2):
                    for h in range(2):
                        last = mm(acc[h * N:(h + 1) * N, 0:hi - lo], cols2[:, 2 * j + i, :],
                                  w[:, i, h * HALF + lo:h * HALF + hi], j == 0 and i == 0, False)
                return last

            def exp_bias(side):
                acc, lo, hi = ((ACC[1], 0, LEFT), (T[2], LEFT, HALF))[side]
                for h in range(2):
                    last = mm(acc[h * N:(h + 1) * N, 0:hi - lo], routesel[:, :], bias[:, h * HALF + lo:h * HALF + hi], False, True)
                return last

            pe.wait_ge(exp_cols, 1)
            ready("w2", 0)
            exp_product(0, 0)
            exp_turn(1)
            exp_product(1, 0).then_inc(ring_used, 1)
            pe.wait_ge(exp_cols, 2)
            ready("w2", 1)
            exp_product(0, 1)
            pe.wait_ge(routesel_ready, 1)
            exp_bias(0).then_inc(left_made, 1)
            exp_product(1, 1)
            exp_bias(1).then_inc(ring_used, 1)

        @block.vector
        def _(dve):
            v = nc.vector
            links = [0]

            def link(op):
                links[0] += 1
                op.then_inc(dve_link, 1)
                dve.wait_ge(dve_link, links[0])

            def statistics(name, src, piece=0):
                k = COMBINES.index(name)
                v.bn_stats(stat6[:, 6 * piece:6 * piece + 6], src).then_inc(stats_ready, 1)
                dve.wait_ge(combined, k + 1)
                return v.bn_aggr(mv[:, k, :], SM[:, 0:12 * (piece + 1)])

            def moments(name, src, piece=0):
                link(statistics(name, src, piece))
                k, q = COMBINES.index(name), POWERS.index(name)
                v.tensor_scalar(pin[:, q:q + 1], mv[:, k, 1:2], EPS, None, ALU.add).then_inc(power_asked, 1)

            def root(name):
                q = POWERS.index(name)
                dve.wait_ge(power_done, q + 1)
                return pout[:, q:q + 1]

            def normalise(dst, name, src):
                r = root(name)
                k = COMBINES.index(name)
                return v.tensor_scalar(dst, src, mv[:, k, 0:1], r, ALU.subtract, ALU.mult)

            def collect(name, dst=None):
                dve.wait_ge(turned_a, at(TURNS, name))
                v.tensor_copy(cols[:, 0:4, :] if dst is None else dst, T[0][:, 0:4 * N]).then_inc(cols_a, 1)

            def sums_root(name, src, squares, least):
                k, q = COMBINES.index(name), POWERS.index(name)
                v.tensor_tensor_reduce(out=squares, in0=src, in1=src, scale=1.0, scalar=0.0, op0=ALU.mult,
                                            op1=ALU.add, accum_out=mv[:, k, 0:1]).then_inc(stats_ready, 1)
                dve.wait_ge(combined, k + 1)
                v.tensor_scalar(pin[:, q:q + 1], SM[:, 0:1], least, None, ALU.max).then_inc(power_asked, 1)

            v.memset(ew1[:, :], 0.0).then_inc(ew1_clear, 1)
            dve.wait_ge(idx_in, 16)
            dve.wait_ge(consts_made, at(CONSTS, "iota"))
            v.tensor_copy(idxf[:, :], idx[:, :])
            link(v.tensor_copy(irow[:, :], irow_i[:, :]))

            def onehot(o, c0):
                return v.tensor_tensor(o, idxf[:, c0:c0 + TE].unsqueeze(2).to_broadcast([P, TE, N]),
                                       irow[:, :].unsqueeze(1).to_broadcast([P, TE, N]), ALU.is_equal)

            onehot(to_dst[:, :, :], TE).then_inc(onehot_copy, 1)
            dve.wait_ge(x_in, 16)
            moments("x0", x0[:, :])
            onehot(ends_b[:, :, 1, :], TE)
            link(onehot(ends_b[:, :, 0, :], 0))
            normalise(row[:, :], "x0", x0[:, :]).then_inc(rows_ready, 1)
            for a in range(2):
                last = v.tensor_tensor(both_b[:, :, a, :], ends_b[:, :, 0, :], ends_b[:, :, 1, :], ALU.add)
            last.then_inc(onehots, 1)
            collect("x0")
            v.tensor_copy(ident_b[:, :], ident[:, :]).then_inc(onehots, 1)
            dve.wait_ge(consts_made, at(CONSTS, "blocks"))
            dve.wait_ge(sums_made, 1)
            v.tensor_copy(spread[0:N, 1, :], ACC[3][0:N, 0:N])
            v.tensor_copy(spread[N:P, 3, :], ACC[3][N:P, 0:N])
            v.tensor_copy(degsel[0:1, :], ACC[3][0:1, N:2 * N]).then_inc(spread_ready, 1)
            dve.wait_ge(slots_in, 16)
            dve.wait_ge(col_in, 16)
            sums_root("slots", slots[:, :], nodes[:, :], EPS * EPS)
            dve.wait_ge(consts_made, at(CONSTS, "fills"))
            e2 = edges2[:, :, :, :].rearrange("p j (h q) n -> p j h q n", q=2)[:, :, :, 1, :]
            dve.wait_ge(turned_a, at(TURNS, "edges"))
            v.tensor_copy(e2[:, 0:2], T[0][:, 0:4 * N].rearrange("p (j h n) -> p j h n", j=2, h=2)).then_inc(cols_a, 1)
            r = root("slots")
            v.tensor_scalar(slots[:, :], slots[:, :], r, colp[:, C_SCALE:C_SCALE + 1], ALU.mult, ALU.mult)\
                .then_inc(rows_ready, 1)
            collect("slots", slots_t[:, 0:4, :])
            for k in range(2):
                dve.wait_ge(pair_turned, k + 1)
                v.tensor_copy(pair[:, k * E // 2:(k + 1) * E // 2], ACC[1 + k][:, :].bitcast(bf16)).then_inc(pair_ready, 1)
            dve.wait_ge(ring_used, used("Wn"))
            v.tensor_copy(nodes[:, :], ACC[0][:, 0:HALF]).then_inc(nodes_ready, 1)
            dve.wait_ge(cols_b, at(TURNS, "edges"))

            u = 0
            for l in range(L):
                for j in range(NJ):
                    dve.wait_ge(comb_made, NJ * l + j + 1)
                    v.tensor_tensor(comb[:, j, :, :], T[j][:, 0:4 * N].rearrange("p (q n) -> p q n", q=4),
                                    edges2[:, j, :, :], ALU.add).then_inc(comb_ready, 1)
                if l == 0:
                    dve.wait_ge(type_in, 16)
                    v.tensor_copy(ramp[:, :], ramp_i[:, :])
                    v.tensor_copy(icol[:, :], icol_i[:, :])
                    link(v.tensor_copy(typesf[:, :], types[:, :]))
                    for t in range(TYPES):
                        v.tensor_scalar(typemask[:, t, :], typesf[:, :], float(t), None, ALU.is_equal)
                    v.tensor_scalar(typesel[:, :], typesf[:, :], icol[:, 0:1], None, ALU.is_equal).then_inc(typesel_ready, 1)
                while u < GATES[l]:
                    dve.wait_ge(gate_mult, u + 1)
                    v.tensor_reduce(gate_in[:, 2 * u:2 * u + 2], eprod[:, u % 2, :].rearrange("p (a c) -> p a c", a=2),
                                    AX.X, ALU.add).then_inc(gate_red, 1)
                    u += 1
                dve.wait_ge(ring_used, used(f"W1b{l}"))
                moments(f"l{l}", ACC[1][:, 0:HALF])
                normalise(row[:, :], f"l{l}", ACC[1][:, 0:HALF]).then_inc(rows_ready, 1)
                dve.wait_ge(turned_b, at(TURNS, f"l{l}"))
                for i in (4, 5):
                    op = v.tensor_scalar(cols[:, i, :], T[1][:, (i - 4) * N:(i - 3) * N], colp[:, C_G + l * NI + i:C_G + l * NI + i + 1],
                                         colp[:, C_B + l * NI + i:C_B + l * NI + i + 1], ALU.mult, ALU.add)
                link(op)
                v.tensor_scalar(cols[:, 4:6, :], cols[:, 4:6, :], 0.0, None, ALU.max).then_inc(cols_b, 1)
                dve.wait_ge(ring_used, used(f"W2{l}"))
                last = v.tensor_tensor(nodes[:, :], ACC[0][:, 0:HALF], nodes[:, :], ALU.add)
                if l < L - 1:
                    last.then_inc(nodes_ready, 1)
                else:
                    last.then_inc(rows_ready, 1)
            while u < TE // 2:
                dve.wait_ge(gate_mult, u + 1)
                op = v.tensor_reduce(gate_in[:, 2 * u:2 * u + 2], eprod[:, u % 2, :].rearrange("p (a c) -> p a c", a=2),
                                     AX.X, ALU.add)
                op.then_inc(gate_red, 1)
                u += 1
            collect("nodes")
            dve.wait_ge(gate_red, TE // 2)
            dve.wait_ge(tail_in, 16)
            v.tensor_scalar(gate_z[:, :], gate_in[:, :], tail[:, X:X + 1], None, ALU.add).then_inc(gate_asked, 1)
            link(v.tensor_tensor(x1[:, :], nodes[:, :], x0[:, :], ALU.add))
            dve.wait_ge(gate_exp, 1)
            link(v.tensor_scalar(gate_d[:, :], gate_e[:, :], 1.0, None, ALU.add))
            v.reciprocal(gate[:, :], gate_d[:, :]).then_inc(gate_ready, 1)
            dve.wait_ge(ring_used, used("Wk"))
            v.tensor_copy(krow, ACC[1][:, 0:HALF]).then_inc(k_row, 1)
            dve.wait_ge(heads_turned, 2)
            v.tensor_copy(kt, T[1][0:DH, 0:HJ * P].rearrange("p (j n) -> p j n", j=HJ)).then_inc(k_cols, 1)
            dve.wait_ge(scores_made, 1)
            s3 = ACC[0][:, 0:HJ * N].rearrange("p (j m) -> p j m", j=HJ)
            link(v.tensor_reduce(mx[:, :], s3, AX.X, ALU.max))
            v.tensor_tensor(shifted, s3, mx[:, :].unsqueeze(2).to_broadcast([P, HJ, N]), ALU.subtract)\
                .then_inc(scores_shift, 1)
            dve.wait_ge(probs_made, 2)
            link(v.tensor_reduce(ssum[:, :], probs, AX.X, ALU.add))
            link(v.reciprocal(rsum[:, :], ssum[:, :]))
            dve.wait_ge(probs_turned, 1)
            v.tensor_copy(probs_t[:, 0:2, :], T[0][:, 0:2 * P].rearrange("p (j n) -> p j n", j=2)).then_inc(probs_a, 1)
            dve.wait_ge(attn_made, 1)
            v.tensor_tensor(row[:, :].rearrange("p (j c) -> p j c", j=HJ), ACC[1][:, 0:HALF].rearrange("p (j c) -> p j c", j=HJ),
                            rsum[:, :].unsqueeze(2).to_broadcast([P, HJ, DH]), ALU.mult).then_inc(rows_ready, 1)
            collect("attn")
            dve.wait_ge(ring_used, used("Wo"))
            link(v.tensor_tensor(x1[:, :], ACC[2][:, 0:HALF], x1[:, :], ALU.add))

            link(statistics("f0", x1[:, :]))
            kf, cf = POWERS.index("f0"), COMBINES.index("f0")
            v.tensor_scalar(pin[:, kf:kf + 1], mv[:, cf, 1:2], 1.0 + EPS, EPS * EPS, ALU.mult, ALU.add).then_inc(power_asked, 1)
            v.tensor_scalar(small[:, 1:2], mv[:, cf, 1:2], (1.0 + EPS) * EPS ** 2, EPS ** 4, ALU.mult, ALU.add)
            dve.wait_ge(rows_kept, 2)
            link(v.scalar_tensor_tensor(out=tmp[:, :], in0=x1[:, :], scalar=mv[:, cf, 0:1], in1=rows4[:, 0, :],
                                        op0=ALU.subtract, op1=ALU.mult))
            sums_root("tok", tmp[:, :], hrow[:, :], small[:, 1:2])
            v.tensor_scalar(keep[:, :], tmp[:, :], root("f0"), None, ALU.mult)
            v.tensor_scalar(row[:, :], tmp[:, :], root("tok"), None, ALU.mult).then_inc(rows_ready, 1)
            collect("tok")
            dve.wait_ge(logits_made, 1)
            v.tensor_reduce(small[:, 1:2], ACC[0][:, 0:N], AX.X, ALU.max, negate=True).then_inc(logits_max, 1)
            dve.wait_ge(soft_made, 1)
            link(v.reciprocal(small[:, 3:4], small[:, 2:3]))
            v.tensor_scalar(soft2[:, 0, :].rearrange("p (a n) -> p a n", a=2),
                            soft[:, :].unsqueeze(1).to_broadcast([P, 2, N]), small[:, 3:4], None, ALU.mult)
            for k in range(SB):
                last = v.tensor_scalar(soft2[:, 1 + k, :].rearrange("p (a n) -> p a n", a=4),
                                       soft[:, 32 * k:32 * k + 32].unsqueeze(1).to_broadcast([P, 4, 32]),
                                       small[:, 3:4], None, ALU.mult)
            last.then_inc(soft_ready, 1)
            dve.wait_ge(soft_turned, 1)
            v.tensor_copy(dispatch_w[N:P, N:P], T[0][N:P, N:P]).then_inc(weights_dve, 1)
            dve.wait_ge(gsum_made, 1)
            v.tensor_copy(gatesel[ROW_MSG2:ROW_MSG2 + 1, :], SM[ROW_MSG2:ROW_MSG2 + 1, 0:N]).then_inc(gsum_ready, 1)
            dve.wait_ge(mixed_made, 1)
            v.tensor_copy(cols[:, 0:4, :], T[1][:, 0:4 * N].rearrange("p (i n) -> p i n", n=N)).then_inc(mixed_a, 1)
            dve.wait_ge(consts_made, at(CONSTS, "slotmask"))
            for k in range(SB):
                dve.wait_ge(hid_turned, k + 1)
                v.tensor_tensor(hid_t[:, k, :, :], T[1 + k][:, 0:HALF].rearrange("p (j n) -> p j n", j=NJ),
                                slotmask[:, :, :], ALU.mult).then_inc(hid_masked, 1)
            dve.wait_ge(mix_out, 1)
            v.tensor_tensor(x2[:, 0:Q], ACC[2][:, 0:Q], x1[:, 0:Q], ALU.add)
            link(v.tensor_tensor(x2[:, Q:HALF], ACC[3][:, 0:Q], x1[:, Q:HALF], ALU.add))

            moments("g1", x2[:, :])
            normalise(keep[:, :], "g1", x2[:, :]).then_inc(rows_ready, 1)
            collect("xn1")
            dve.wait_ge(cols_a, at(TURNS, "xn1"))
            dve.wait_ge(cols_b, at(TURNS, "xn1"))
            for t in range(TYPES):
                v.tensor_tensor(typed[:, t, :, :], cols[:, :, :], typemask[:, t, :].unsqueeze(1).to_broadcast([P, NI, N]),
                                ALU.mult).then_inc(typed_ready, 1)
            dve.wait_ge(ring_used, used(f"Wt{TYPES - 1}"))
            v.tensor_copy(hrow[:, :], ACC[0][:, 0:HALF]).then_inc(rows_ready, 1)
            collect("h")
            dve.wait_ge(tail_bias, 1)
            dve.wait_ge(rows_kept, 4)
            v.tensor_tensor(hbias[:, :], T[2][:, 0:HALF], hrow[:, :], ALU.add)
            v.tensor_tensor(keep[:, :], ACC[3][:, 0:HALF], keep[:, :], ALU.add)
            link(v.tensor_tensor(x2[:, :], x2[:, :], rows4[:, 2, :], ALU.add))
            dve.wait_ge(ring_used, used("Wm", 1))
            link(v.tensor_copy(pq[:, 0, 0:HALF], ACC[1][:, 0:HALF]))
            v.tensor_tensor(pq[:, 1, 0:HALF], ACC[1][:, 0:HALF], pq[:, 0, 0:HALF].bitcast(fp32), ALU.subtract)\
                .then_inc(pq_left, 1)
            dve.wait_ge(pq_round, 1)
            v.tensor_tensor(pq[:, 1, HALF:D], ACC[2][:, 0:HALF], pq[:, 0, HALF:D].bitcast(fp32), ALU.subtract)\
                .then_inc(pq_rest, 1)
            second = [T[1], SM, ACC[1]]
            for t in range(TE):
                dve.wait_ge(gathered_right, t + 1)
                if t >= 3:
                    dve.wait_ge(scattered, t - 2)
                v.tensor_scalar(msg[:, t % 3, HALF:D], second[t % 3][:, 0:HALF], gate[:, t:t + 1], 0.0, ALU.mult, ALU.max)\
                    .then_inc(msg_dve, 1)

            def left_out(n):
                dve.wait_ge(left_turned, n + 1)
                v.tensor_copy((cols, cols2)[n % 2][:, 0:4, :], T[0][:, 0:LEFT]).then_inc(left_cols, 1)

            dve.wait_ge(scattered, TE)
            v.tensor_copy(row[:, 0:LEFT], ACC[0][:, 0:LEFT]).then_inc(left_ready, 1)
            left_out(0)
            for n, name in enumerate(CHAIN[:-1]):
                for side, cs in enumerate((slice(0, LEFT), slice(LEFT, HALF))):
                    if side == 0:
                        dve.wait_ge(left_made, n + 1)
                        dve.wait_ge(right_turned, n + 1)
                    else:
                        dve.wait_ge(ring_used, used(name))
                    acc = chain_acc[n % 2][side][:, 0:cs.stop - cs.start]
                    if name == "Wm2":
                        op = v.tensor_copy(row[:, cs], acc)
                    elif name == "Wg1":
                        op = v.tensor_scalar(row[:, cs], acc, 0.0, None, ALU.max)
                    else:
                        op = v.tensor_tensor(row[:, cs], acc, hbias[:, cs], ALU.add)
                    op.then_inc(left_ready if side == 0 else right_ready, 1)
                    if side == 0:
                        left_out(n + 1)
            acc = chain_acc[(len(CHAIN) - 1) % 2]
            dve.wait_ge(left_made, len(CHAIN))
            v.tensor_tensor(tmp[:, 0:LEFT], acc[0][:, 0:LEFT], keep[:, 0:LEFT], ALU.add).then_inc(left_used, 1)
            dve.wait_ge(left_used, 1)
            v.bn_stats(stat6[:, 0:6], tmp[:, 0:LEFT])
            dve.wait_ge(ring_used, used("Wout"))
            link(v.tensor_tensor(tmp[:, LEFT:HALF], acc[1][:, 0:HALF - LEFT], keep[:, LEFT:HALF], ALU.add))
            moments("go", tmp[:, LEFT:HALF], 1)
            ko = COMBINES.index("go")
            link(v.scalar_tensor_tensor(out=hrow[:, :], in0=tmp[:, :], scalar=mv[:, ko, 0:1], in1=rows4[:, 1, :],
                                        op0=ALU.subtract, op1=ALU.mult))
            link(v.scalar_tensor_tensor(out=x3[:, :], in0=hrow[:, :], scalar=root("go"), in1=x2[:, :],
                                        op0=ALU.mult, op1=ALU.add))

            moments("f1", x3[:, :])
            normalise(row[:, :], "f1", x3[:, :]).then_inc(rows_ready, 1)
            collect("x3")
            dve.wait_ge(enc_made, 1)
            v.tensor_scalar(enc_t[:, :, :], ACC[3][0:R, 0:N].unsqueeze(1).to_broadcast([R, 2, N]),
                            colp[0:R, C_ENCB:C_ENCB + 1], None, ALU.add).then_inc(enc_ready, 1)
            dve.wait_ge(route_made, 1)
            link(v.tensor_tensor(lg[:, :], T[2][:, 0:X], tail[:, 0:X], ALU.add))
            link(v.tensor_reduce(small[:, 7:8], lg[:, :], AX.X, ALU.max))
            link(v.scalar_tensor_tensor(out=cand[:, :], in0=lg[:, :], scalar=small[:, 7:8], in1=ramp[:, :],
                                        op0=ALU.is_equal, op1=ALU.mult))
            link(v.tensor_reduce(mx[:, 0:1], cand[:, :], AX.X, ALU.max))
            for h in range(2):
                rows = slice(h * N, (h + 1) * N)
                v.tensor_scalar(route4[rows, :], cand[rows, 4 * h:4 * h + 4], mx[rows, 0:1], None, ALU.is_equal)
            v.tensor_scalar(route_pad[:, ROW_FFN2:ROW_FFN2 + X], cand[0:N, :], mx[0:N, 0:1], None, ALU.is_equal)\
                .then_inc(route_ready, 1)
            dve.wait_ge(route_ready, 1)
            for j in range(2):
                dve.wait_ge(gelu_made, j + 1)
                cs = slice(2 * j * R, 2 * (j + 1) * R)
                v.tensor_tensor(tmp[:, cs].rearrange("p (e r) -> p e r", e=2), hrow[:, cs].rearrange("p (e r) -> p e r", e=2),
                                route4[:, 2 * j:2 * j + 2].unsqueeze(2).to_broadcast([P, 2, R]), ALU.mult).then_inc(exp_ready, 1)
                dve.wait_ge(exp_turned, j + 1)
                v.tensor_copy(cols2[:, 2 * j:2 * j + 2, :], T[j][:, 0:P].rearrange("p (i n) -> p i n", n=N)).then_inc(exp_cols, 1)
            dve.wait_ge(route_turned, 1)
            v.tensor_copy(routesel[:, :], ACC[3][:, 0:N]).then_inc(routesel_ready, 1)
            v.tensor_scalar(small[:, 4:5], small[:, 7:8], -1.0, None, ALU.mult).then_inc(route_max, 1)
            dve.wait_ge(route_exp, 1)
            link(v.reciprocal(small[:, 6:7], small[:, 5:6]))
            dve.wait_ge(left_made, len(CHAIN) + 1)
            v.scalar_tensor_tensor(out=row[:, 0:LEFT], in0=ACC[1][:, 0:LEFT], scalar=small[:, 6:7], in1=x3[:, 0:LEFT],
                                   op0=ALU.mult, op1=ALU.add)
            dve.wait_ge(ring_used, used("w2"))
            v.scalar_tensor_tensor(out=row[:, LEFT:HALF], in0=T[2][:, 0:HALF - LEFT], scalar=small[:, 6:7], in1=x3[:, LEFT:HALF],
                                   op0=ALU.mult, op1=ALU.add).then_inc(final_ready, 1)

        @block.scalar
        def _(act):
            a = nc.scalar

            def copy(dst, src):
                return a.activation(dst, src, ACT.Copy)

            def collect(name, dst=None):
                act.wait_ge(turned_b, at(TURNS, name))
                copy(cols[:, 4:6, :] if dst is None else dst,
                     T[1][:, 0:2 * N].rearrange("p (i n) -> p i n", n=N)).then_inc(cols_b, 1)

            act.dma_start(idx[:, :], ins["idx"]).then_inc(idx_in, 16)
            act.dma_start(bias[:, :], ins["bias"]).then_inc(bias_in, 16)
            act.dma_start(slots[:, :], ins["slots"]).then_inc(slots_in, 16)
            act.dma_start(colp[:, :], ins["colp"]).then_inc(col_in, 16)
            act.dma_start(types[:, :], ins["types"].to_broadcast([P, N])).then_inc(type_in, 16)
            act.dma_start(tail[:, :], ins["tail"].to_broadcast([P, X + 1])).then_inc(tail_in, 16)
            collect("x0")
            act.wait_ge(ring_used, used("ef"))
            copy(tmp[:, 0:DE], ACC[1][:, 0:DE]).then_inc(edges_kept, 1)
            act.wait_ge(edges_made, 1)
            copy(hrow[:, 0:2 * N], ACC[2][:, 0:2 * N]).then_inc(edges_kept, 1)
            act.wait_ge(ring_used, used("We", 0))
            copy(tmp[:, :], ACC[1][:, 0:HALF]).then_inc(rows_ready, 1)
            e2 = edges2[:, :, :, :].rearrange("p j (h q) n -> p j h q n", q=2)[:, :, :, 1, :]
            act.wait_ge(consts_made, at(CONSTS, "fills"))
            act.wait_ge(turned_b, at(TURNS, "edges"))
            copy(e2[:, 2], T[1][:, 0:2 * N].rearrange("p (h n) -> p h n", h=2)).then_inc(cols_b, 1)
            act.wait_ge(rows_made, 1)
            copy(rows4[:, 3, :], ACC[3][:, 0:2 * H4]).then_inc(rows_kept, 1)
            collect("slots", slots_t[:, 4:6, :])
            act.wait_ge(col_in, 16)

            def gate_hidden(first, last):
                for u in range(first, last):
                    act.wait_ge(gate_made, u + 1)
                    if u >= 2:
                        act.wait_ge(gate_mult, u - 1)
                    a.activation(ehid[:, u % 2, :], ACC[2 + u % 2][:, 0:2 * H4], ACT.Relu).then_inc(gate_relu, 1)

            gate_hidden(0, GATES[0])
            for l in range(L):
                gate_hidden(GATES[l], GATES[l] + 1)
                act.wait_ge(turned_a, at(TURNS, f"l{l}"))
                for i in range(4):
                    op = a.activation(cols[:, i, :], T[0][:, i * N:(i + 1) * N], ACT.Relu,
                                      scale=colp[:, C_G + l * NI + i:C_G + l * NI + i + 1],
                                      bias=colp[:, C_B + l * NI + i:C_B + l * NI + i + 1])
                op.then_inc(cols_a, 1)
                gate_hidden(GATES[l] + 1, GATES[l + 1])
            collect("nodes")
            act.wait_ge(gate_asked, 1)
            a.activation(gate_e[:, :], gate_z[:, :], ACT.Exp, scale=-1.0).then_inc(gate_exp, 1)
            act.wait_ge(ring_used, used("Wq"))
            copy(qrow, ACC[0][:, 0:HALF]).then_inc(q_row, 1)
            act.wait_ge(heads_turned, 1)
            copy(qt, T[0][0:DH, 0:HJ * P].rearrange("p (j n) -> p j n", j=HJ)).then_inc(q_cols, 1)
            act.wait_ge(ring_used, used("Wv"))
            act.wait_ge(consts_made, at(CONSTS, "probs"))
            copy(vrow, ACC[2][:, 0:HALF]).then_inc(v_row, 1)
            act.wait_ge(scores_shift, 1)
            for h in range(2):
                rows = slice(h * N, (h + 1) * N)
                a.activation(probs[rows, :, h * N:(h + 1) * N], shifted[rows, :, :], ACT.Exp, scale=DH ** -0.5)\
                    .then_inc(probs_made, 1)
            act.wait_ge(probs_turned, 2)
            copy(probs_t[:, 2:4, :], T[1][:, 0:2 * P].rearrange("p (j n) -> p j n", j=2)).then_inc(probs_b, 1)
            collect("attn")
            for k in range(3):
                act.wait_ge(rows_made, k + 2)
                copy(rows4[:, k, :], ACC[(3, 0, 3)[k]][:, 0:HALF]).then_inc(rows_kept, 1)
            collect("tok")
            act.wait_ge(logits_max, 1)
            a.activation(soft[:, :], ACC[0][:, 0:N], ACT.Exp, bias=small[:, 1:2], accum_out=small[:, 2:3]).then_inc(soft_made, 1)
            act.wait_ge(soft_turned, 1)
            copy(dispatch_w[0:N, 0:N], T[0][0:N, N:P]).then_inc(weights_act, 1)
            act.wait_ge(mixed_made, 1)
            copy(cols[:, 4:6, :], T[2][:, 0:2 * N].rearrange("p (i n) -> p i n", n=N)).then_inc(mixed_b, 1)
            for c in range(4):
                rows = slice(32 * c, 32 * c + 32)
                copy(combine_w[rows, c % 2, :, c // 2 * N:(c // 2 + 1) * N],
                     T[0][rows, P:(1 + SB) * P].rearrange("p (k n) -> p k n", k=SB)[:, :, 0:N]).then_inc(weights_act, 1)
            for b in range(NB):
                act.wait_ge(ring_used, used(f"fc1{b}"))
                a.activation(hid[:, b // 2, b % 2 * Q:(b % 2 + 1) * Q], ACC[b][:, 0:Q], ACT.Gelu).then_inc(hid_made, 1)
            for k in range(SB):
                act.wait_ge(ring_used, used(f"fc2{2 * k + 1}"))
                copy(mixed[:, k, :], ACC[k][:, 0:Q]).then_inc(y_ready, 1)
            collect("xn1")
            collect("h")
            act.wait_ge(ring_used, used("Wm", 3))
            copy(pq[:, 0, HALF:D], ACC[2][:, 0:HALF]).then_inc(pq_round, 1)
            first = [T[0], T[2], ACC[3]]
            act.wait_ge(gate_ready, 1)
            for t in range(TE):
                act.wait_ge(gathered_left, t + 1)
                if t >= 3:
                    act.wait_ge(scattered, t - 2)
                a.activation(msg[:, t % 3, 0:HALF], first[t % 3][:, 0:HALF], ACT.Relu, scale=gate[:, t:t + 1]).then_inc(msg_act, 1)
            act.wait_ge(scattered, TE)
            act.wait_ge(left_ready, 1)
            copy(row[:, LEFT:HALF], ACC[0][:, LEFT:HALF]).then_inc(right_ready, 1)
            for n in range(len(CHAIN)):
                act.wait_ge(right_turned, n + 1)
                copy((cols, cols2)[n % 2][:, 4:6, :], T[1][:, 0:2 * N].rearrange("p (i n) -> p i n", n=N)).then_inc(right_cols, 1)
            collect("x3")
            for j in range(2):
                if j == 0:
                    act.wait_ge(w1_made, 1)
                else:
                    act.wait_ge(ring_used, used("w1"))
                a.activation(hrow[:, 2 * j * R:2 * (j + 1) * R], ACC[2 * j][:, 0:2 * R], ACT.Gelu).then_inc(gelu_made, 1)
            act.wait_ge(route_max, 1)
            a.activation(route_e[:, :], lg[:, :], ACT.Exp, bias=small[:, 4:5], accum_out=small[:, 5:6]).then_inc(route_exp, 1)


def _weight(w, groups=1):
    import numpy as np
    rows, cols = w.shape
    n = rows // P
    half = n // 2
    order = [half * (i % 2) + i // 2 for i in range(n)]
    return np.ascontiguousarray(w.reshape(n, P, cols)[order].transpose(1, 0, 2)).reshape(P, n * cols)


def _halves(x):
    import numpy as np
    return np.ascontiguousarray(x.reshape(N, 2, HALF).transpose(1, 0, 2)).reshape(P, HALF)


def kernel(**inputs):
    import numpy as np
    import concourse.bacc as bacc
    from concourse.bass_utils import run_bass_kernel_spmd

    g = {k: np.asarray(v) for k, v in inputs.items()}
    a = {"x": _halves(g["x"]), "slots": _halves(g["L0_ffn_slots"])}
    a["idx"] = np.concatenate([g["src"].reshape(P, TE), g["dst"].reshape(P, TE)], axis=1)
    a["types"] = g["node_type_6"].reshape(1, N)
    a["ef"] = g["edge_attr_256"].reshape(P, TE * DE)
    a["ea"] = np.ascontiguousarray(g["edge_attr_32"].reshape(P, 4, 4, DA).transpose(2, 3, 1, 0)).reshape(P, 4 * P)
    a["ew1"] = g["L1_gnn_edge_W1"]
    a["We"] = np.ascontiguousarray(g["L0_gnn_We"].T.reshape(2, P, D).transpose(1, 0, 2)).reshape(P, 2 * D)
    a["Wn"] = _weight(g["L0_gnn_Wn"].T)
    for l in range(L):
        w = g["L0_gnn_W1"][l].T
        a[f"W1a{l}"], a[f"W1b{l}"], a[f"W2{l}"] = _weight(w[:D]), _weight(w[D:]), _weight(g["L0_gnn_W2"][l].T)
    for k, c in enumerate("qkv"):
        a[f"W{c}"] = _weight(g["L0_gnn_Wqkv"][k * D:(k + 1) * D].T)
    a["Wo"] = _weight(g["L0_gnn_Wo"].T)
    fc1 = g["L0_ffn_fc1_weight"].reshape(SB, 4, 2, 4, D, F).transpose(0, 2, 4, 1, 3, 5).reshape(NB, D, D)
    fc2 = g["L0_ffn_fc2_weight"].reshape(NB, NI, P, D).transpose(0, 2, 1, 3).reshape(NB, P, NI * D)
    for b in range(NB):
        a[f"fc1{b}"] = _weight(fc1[b])
        a[f"fc2{b}"] = fc2[b]
    for t in range(TYPES):
        a[f"Wt{t}"] = _weight(g["L1_gnn_W_type"][t])
    both = [_weight(w).reshape(P, NI, 2, HALF) for w in (g["L1_gnn_msg_W1"][:D], g["L1_gnn_msg_W1"][D:])]
    a["Wm"] = np.stack(both, axis=2).transpose(0, 3, 1, 2, 4).reshape(P, 4 * SLOT)
    for k, n in (("Wm2", "msg_W2"), ("Wg1", "agg_W1"), ("Wg2", "agg_W2"), ("Wout", "out_W")):
        a[k] = _weight(g["L1_gnn_" + n])
    a["w1"] = _weight(g["L1_ffn_w1"].transpose(1, 0, 2).reshape(D, X * R))
    a["w2"] = _weight(g["L1_ffn_w2"].reshape(X * R, D))
    a["encw"] = _weight(g["L1_ffn_enc_w"])
    a["sww"] = g["L1_ffn_sw_w"]

    bias = np.zeros((P, D), np.float32)
    bias[ROW_BE], bias[ROW_BN], bias[ROW_BO] = g["L0_gnn_be"], g["L0_gnn_bn"], g["L0_gnn_bo"]
    bias[ROW_B1:ROW_B1 + L], bias[ROW_B2:ROW_B2 + L] = g["L0_gnn_b1"], g["L0_gnn_b2"]
    bias[ROW_BQKV:ROW_BQKV + 3] = g["L0_gnn_bqkv"].reshape(3, D)
    bias[ROW_FC1:ROW_FC1 + NB] = g["L0_ffn_fc1_bias"].reshape(SB, 4, 2, 4, F).transpose(0, 2, 1, 3, 4).reshape(NB, D)
    bias[ROW_TYPE:ROW_TYPE + TYPES] = g["L1_gnn_b_type"]
    bias[ROW_MSG1], bias[ROW_MSG2] = g["L1_gnn_msg_b1"], g["L1_gnn_msg_b2"]
    bias[ROW_AGG1], bias[ROW_AGG2], bias[ROW_OUT] = g["L1_gnn_agg_b1"], g["L1_gnn_agg_b2"], g["L1_gnn_out_b"]
    bias[ROW_FFN1, 0:X * R] = g["L1_ffn_b1"].reshape(X * R)
    bias[ROW_EDGE1, 0:H4] = g["L1_gnn_edge_b1"]
    bias[ROW_EDGE1, H4:2 * H4] = g["L1_gnn_edge_b1"]
    bias[ROW_NORM], bias[ROW_LNG], bias[ROW_LNB] = g["L0_ffn_norm_weight"], g["L1_gnn_ln_g"], g["L1_gnn_ln_b"]
    bias[ROW_EDGE2, 0:2 * H4] = np.concatenate([g["L1_gnn_edge_W2"].reshape(H4)] * 2)
    bias[ROW_FFN2:ROW_FFN2 + X] = g["L1_ffn_b2"]
    bias[ROW_FC2:ROW_FC2 + N] = g["L0_ffn_fc2_bias"]
    a["bias"] = bias

    a["tail"] = np.concatenate([g["L1_ffn_sw_b"], g["L1_gnn_edge_b2"]]).reshape(1, X + 1)

    colp = np.zeros((P, COL_PACK), np.float32)
    for l in range(L):
        for i in range(NI):
            c = chunk(i)
            colp[:, C_G + l * NI + i] = g["L0_gnn_ln_g"][l, c * P:(c + 1) * P]
            colp[:, C_B + l * NI + i] = g["L0_gnn_ln_b"][l, c * P:(c + 1) * P]
    colp[0:R, C_ENCB] = g["L1_ffn_enc_b"]
    colp[0:N, C_SCALE] = g["L0_ffn_scale"]
    colp[N:P, C_SCALE] = g["L0_ffn_scale"]
    a["colp"] = colp

    nc = bacc.Bacc("TRN2", target_bir_lowering=False, num_devices=1)
    arrays, ins = {}, {}
    for name, v in a.items():
        v = np.ascontiguousarray(v)
        arrays[f"in_{name}"] = v
        ins[name] = nc.dram_tensor(f"in_{name}", v.shape, mybir.dt.from_np(v.dtype), kind="ExternalInput").ap()
    out = nc.dram_tensor("out", (P, HALF), mybir.dt.float32, kind="ExternalOutput").ap()
    build(nc, ins, out)
    r = run_bass_kernel_spmd(nc, [arrays], core_ids=[0])
    got = np.asarray(r.results[0]["out"])
    return np.ascontiguousarray(got.reshape(2, N, HALF).transpose(1, 0, 2)).reshape(N, D)
```
